# Optimizing a Trainium2 kernel written in Bass

```python
import numpy as np
import jax
import jax.numpy as jnp

def _softmax(x, axis=-1):
    return jax.nn.softmax(x, axis=axis)

def _gelu(x):
    return jax.nn.gelu(x, approximate=True)

def _silu(x):
    return jax.nn.silu(x)

def _sigmoid(x):
    return jax.nn.sigmoid(x)

def _layernorm(x, axis=-1, eps=1e-05):
    m = jnp.mean(x, axis=axis, keepdims=True)
    v = jnp.var(x, axis=axis, keepdims=True)
    return (x - m) / jnp.sqrt(v + eps)

def _scatter_add(tgt, idx, src, axis=0):
    return tgt.at[idx].add(src)

def _segment_sum(src, seg, n):
    return jax.ops.segment_sum(src, seg, n)
kernel_name = 'mk_macaron_d2_jaxref_r8_3e36d1'

def setup_inputs(seed: int=0):
    np.random.seed(seed)
    _w = jnp.asarray

    def _L0_attn_setup():
        import jax, jax.numpy as jnp
        import numpy as np
        DIM = 128
        NUM_HEADS = 16
        HEAD_DIM = DIM // NUM_HEADS
        PATCH_SIZE = 20
        SHIFT = 2
        B, N = (8, 512)

        def _patch_index(n, patch_size, shift):
            base = np.arange(0, patch_size * shift, shift, dtype=np.int64)[None, :]
            group = np.concatenate([base + i for i in range(shift)], axis=0)
            blocks = [group]
            idx = group
            while idx[-1, -1] < n:
                idx = idx + patch_size * shift
                blocks.append(idx)
            return np.concatenate(blocks, axis=0)
        PATCH_INDEX = _patch_index(N, PATCH_SIZE, SHIFT)
        PAD_SIZE = PATCH_SIZE * SHIFT - N % (PATCH_SIZE * SHIFT)
        key = jax.random.key(seed)
        k1, k2, k3 = jax.random.split(key, 3)
        x = jax.random.normal(k1, (B, N, DIM), dtype=jnp.float32)
        Wqkv = jax.random.normal(k2, (3 * DIM, DIM), dtype=jnp.float32) * 0.02
        Wout = jax.random.normal(k3, (DIM, DIM), dtype=jnp.float32) * 0.02
        bout = jnp.zeros((DIM,), dtype=jnp.float32)
        return {'x': x, 'Wqkv': Wqkv, 'Wout': Wout, 'bout': bout}
    _L0_attn_in = _L0_attn_setup()

    def _L0_ffn_setup():
        import jax, jax.numpy as jnp
        import numpy as np
        N, T, D = (4, 512, 128)
        NUM_EXPERTS = 8
        EXPERT_CAP = 2.0
        MLP_RATIO = 4
        HIDDEN = MLP_RATIO * D
        key = jax.random.key(seed)
        k1, k2, k3, k4 = jax.random.split(key, 4)
        x = jax.random.normal(k1, (N, T, D), dtype=jnp.float32)
        gate_w = jax.random.truncated_normal(k2, -2.0, 2.0, (D, NUM_EXPERTS), dtype=jnp.float32) * 0.02
        w1 = jax.random.normal(k3, (NUM_EXPERTS, D, HIDDEN), dtype=jnp.float32) * 0.02
        w2 = jax.random.normal(k4, (NUM_EXPERTS, HIDDEN, D), dtype=jnp.float32) * 0.02
        return {'x': x, 'gate_w': gate_w, 'w1': w1, 'w2': w2}
    _L0_ffn_in = _L0_ffn_setup()

    def _L1_attn_setup():
        import jax, jax.numpy as jnp
        import numpy as np
        EMBED_DIM = 128
        NUM_HEADS = 16
        HEAD_DIM = EMBED_DIM // NUM_HEADS
        SEQ_LEN = 128
        BATCH = 4
        MAX_REL_POS = 2

        def _rel_index(length_q, length_k):
            q = jnp.arange(length_q)[:, None]
            k = jnp.arange(length_k)[None, :]
            return jnp.clip(k - q, -MAX_REL_POS, MAX_REL_POS) + MAX_REL_POS
        key = jax.random.key(seed)
        ks = jax.random.split(key, 12)
        s = 1.0 / np.sqrt(EMBED_DIM)
        x = jax.random.normal(ks[0], (BATCH, SEQ_LEN, EMBED_DIM), dtype=jnp.float32)
        W_q = jax.random.normal(ks[1], (EMBED_DIM, EMBED_DIM), dtype=jnp.float32) * s
        b_q = jnp.zeros((EMBED_DIM,), dtype=jnp.float32)
        W_k = jax.random.normal(ks[2], (EMBED_DIM, EMBED_DIM), dtype=jnp.float32) * s
        b_k = jnp.zeros((EMBED_DIM,), dtype=jnp.float32)
        W_v = jax.random.normal(ks[3], (EMBED_DIM, EMBED_DIM), dtype=jnp.float32) * s
        b_v = jnp.zeros((EMBED_DIM,), dtype=jnp.float32)
        W_o = jax.random.normal(ks[4], (EMBED_DIM, EMBED_DIM), dtype=jnp.float32) * s
        b_o = jnp.zeros((EMBED_DIM,), dtype=jnp.float32)
        lim = float(np.sqrt(6.0 / (2 * MAX_REL_POS + 1 + HEAD_DIM)))
        rel_k_table = jax.random.uniform(ks[5], (2 * MAX_REL_POS + 1, HEAD_DIM), jnp.float32, -lim, lim)
        rel_v_table = jax.random.uniform(ks[6], (2 * MAX_REL_POS + 1, HEAD_DIM), jnp.float32, -lim, lim)
        return {'x': x, 'W_q': W_q, 'b_q': b_q, 'W_k': W_k, 'b_k': b_k, 'W_v': W_v, 'b_v': b_v, 'W_o': W_o, 'b_o': b_o, 'rel_k_table': rel_k_table, 'rel_v_table': rel_v_table}
    _L1_attn_in = _L1_attn_setup()

    def _L1_ffn_setup():
        import jax, jax.numpy as jnp
        import numpy as np
        B, S, D, F, E, NS, K = (2, 128, 128, 512, 8, 8, 2)
        FS = F // NS
        key = jax.random.key(seed)
        ks = jax.random.split(key, 8)
        scale = 0.02
        return {'hidden_states': jax.random.normal(ks[0], (B, S, D), jnp.float32), 'gate_W': jax.random.normal(ks[1], (E, D), jnp.float32) * scale, 'w1_e': jax.random.normal(ks[2], (E, D, F), jnp.float32) * scale, 'w3_e': jax.random.normal(ks[3], (E, D, F), jnp.float32) * scale, 'w2_e': jax.random.normal(ks[4], (E, F, D), jnp.float32) * scale, 'w1_s': jax.random.normal(ks[5], (NS, D, FS), jnp.float32) * scale, 'w3_s': jax.random.normal(ks[6], (NS, D, FS), jnp.float32) * scale, 'w2_s': jax.random.normal(ks[7], (NS, FS, D), jnp.float32) * scale}
    _L1_ffn_in = _L1_ffn_setup()
    _d = {'L0_attn_x': _L0_attn_in['x'], 'L0_attn_Wqkv': _L0_attn_in['Wqkv'], 'L0_attn_Wout': _L0_attn_in['Wout'], 'L0_attn_bout': _L0_attn_in['bout'], 'L0_ffn_gate_w': _L0_ffn_in['gate_w'], 'L0_ffn_w1': _L0_ffn_in['w1'], 'L0_ffn_w2': _L0_ffn_in['w2'], 'L1_attn_W_q': _L1_attn_in['W_q'], 'L1_attn_b_q': _L1_attn_in['b_q'], 'L1_attn_W_k': _L1_attn_in['W_k'], 'L1_attn_b_k': _L1_attn_in['b_k'], 'L1_attn_W_v': _L1_attn_in['W_v'], 'L1_attn_b_v': _L1_attn_in['b_v'], 'L1_attn_W_o': _L1_attn_in['W_o'], 'L1_attn_b_o': _L1_attn_in['b_o'], 'L1_attn_rel_k_table': _L1_attn_in['rel_k_table'], 'L1_attn_rel_v_table': _L1_attn_in['rel_v_table'], 'L1_ffn_gate_W': _L1_ffn_in['gate_W'], 'L1_ffn_w1_e': _L1_ffn_in['w1_e'], 'L1_ffn_w3_e': _L1_ffn_in['w3_e'], 'L1_ffn_w2_e': _L1_ffn_in['w2_e'], 'L1_ffn_w1_s': _L1_ffn_in['w1_s'], 'L1_ffn_w3_s': _L1_ffn_in['w3_s'], 'L1_ffn_w2_s': _L1_ffn_in['w2_s']}
    _x0 = _d['L0_attn_x']
    _d['L0_attn_x'] = jax.random.normal(jax.random.fold_in(jax.random.key(seed), 1), (8, 256, 128), dtype=_x0.dtype)
    del _x0
    return _d

def reference(L0_attn_x, L0_attn_Wqkv, L0_attn_Wout, L0_attn_bout, L0_ffn_gate_w, L0_ffn_w1, L0_ffn_w2, L1_attn_W_q, L1_attn_b_q, L1_attn_W_k, L1_attn_b_k, L1_attn_W_v, L1_attn_b_v, L1_attn_W_o, L1_attn_b_o, L1_attn_rel_k_table, L1_attn_rel_v_table, L1_ffn_gate_W, L1_ffn_w1_e, L1_ffn_w3_e, L1_ffn_w2_e, L1_ffn_w1_s, L1_ffn_w3_s, L1_ffn_w2_s):

    def _L0_attn_ref(x, Wqkv, Wout, bout):
        import jax, jax.numpy as jnp
        import numpy as np
        DIM = 128
        NUM_HEADS = 16
        HEAD_DIM = DIM // NUM_HEADS
        PATCH_SIZE = 20
        SHIFT = 2
        B, N = (8, 512)

        def _patch_index(n, patch_size, shift):
            base = np.arange(0, patch_size * shift, shift, dtype=np.int64)[None, :]
            group = np.concatenate([base + i for i in range(shift)], axis=0)
            blocks = [group]
            idx = group
            while idx[-1, -1] < n:
                idx = idx + patch_size * shift
                blocks.append(idx)
            return np.concatenate(blocks, axis=0)
        PATCH_INDEX = _patch_index(N, PATCH_SIZE, SHIFT)
        PAD_SIZE = PATCH_SIZE * SHIFT - N % (PATCH_SIZE * SHIFT)
        Bq, Nq, C = x.shape
        scale = HEAD_DIM ** (-0.5)
        pidx = jnp.asarray(PATCH_INDEX)
        x_pad = jnp.concatenate([x, jnp.zeros((Bq, PAD_SIZE, C), dtype=x.dtype)], axis=1)
        xp = x_pad[:, pidx, :]
        qkv = jnp.einsum('brsc,dc->brsd', xp, Wqkv)
        Rr, Sp = pidx.shape
        qkv = qkv.reshape(Bq, Rr, Sp, 3, NUM_HEADS, HEAD_DIM)
        q = qkv[..., 0, :, :].transpose(0, 1, 3, 2, 4)
        k = qkv[..., 1, :, :].transpose(0, 1, 3, 2, 4)
        v = qkv[..., 2, :, :].transpose(0, 1, 3, 2, 4)
        dots = jnp.einsum('brhsd,brhtd->brhst', q, k) * scale
        attn = jax.nn.softmax(dots, axis=-1)
        out = jnp.einsum('brhst,brhtd->brhsd', attn, v)
        out = out.transpose(0, 1, 3, 2, 4).reshape(Bq, Rr, Sp, C)
        x_pad = x_pad.at[:, pidx.reshape(-1), :].set(out.reshape(Bq, -1, C))
        return x_pad[:, :Nq, :] @ Wout.T + bout

    def _L0_ffn_ref(x, gate_w, w1, w2):
        import jax, jax.numpy as jnp
        import numpy as np
        N, T, D = (4, 512, 128)
        NUM_EXPERTS = 8
        EXPERT_CAP = 2.0
        MLP_RATIO = 4
        HIDDEN = MLP_RATIO * D
        x = x.astype(jnp.float32)
        n, t, d = x.shape
        k = int(EXPERT_CAP * t / NUM_EXPERTS)
        scores = jnp.einsum('ntd,de->nte', x, gate_w)
        probs = jax.nn.softmax(scores, axis=-1)
        probs = jnp.transpose(probs, (0, 2, 1))
        g, m = jax.lax.top_k(probs, k)
        xin = jax.vmap(lambda xb, mb: xb[mb])(x, m)
        h = jax.nn.gelu(jnp.einsum('nekd,edf->nekf', xin, w1))
        h = jnp.einsum('nekf,efd->nekd', h, w2)
        weighted = g[..., None] * h
        flat_idx = (m + jnp.arange(n, dtype=m.dtype)[:, None, None] * t).reshape(-1)
        out = jnp.zeros((n * t, d), dtype=jnp.float32).at[flat_idx].add(weighted.reshape(-1, d))
        out = out.reshape(n, t, d)
        return out.astype(jnp.bfloat16)

    def _L1_attn_ref(x, W_q, b_q, W_k, b_k, W_v, b_v, W_o, b_o, rel_k_table, rel_v_table):
        import jax, jax.numpy as jnp
        import numpy as np
        EMBED_DIM = 128
        NUM_HEADS = 16
        HEAD_DIM = EMBED_DIM // NUM_HEADS
        SEQ_LEN = 128
        BATCH = 4
        MAX_REL_POS = 2

        def _rel_index(length_q, length_k):
            q = jnp.arange(length_q)[:, None]
            k = jnp.arange(length_k)[None, :]
            return jnp.clip(k - q, -MAX_REL_POS, MAX_REL_POS) + MAX_REL_POS
        B, S, E = x.shape
        H, D = (NUM_HEADS, HEAD_DIM)
        scale = jnp.sqrt(jnp.asarray(D, x.dtype))
        Q = x @ W_q + b_q
        K = x @ W_k + b_k
        V = x @ W_v + b_v
        Qh = Q.reshape(B, S, H, D).transpose(0, 2, 1, 3)
        Kh = K.reshape(B, S, H, D).transpose(0, 2, 1, 3)
        Vh = V.reshape(B, S, H, D).transpose(0, 2, 1, 3)
        scores = jnp.einsum('bhqd,bhkd->bhqk', Qh, Kh)
        idx = _rel_index(S, S)
        rel_k = rel_k_table[idx]
        scores = (scores + jnp.einsum('bhqd,qkd->bhqk', Qh, rel_k)) / scale
        causal = jnp.tril(jnp.ones((S, S), dtype=bool))
        scores = jnp.where(causal[None, None], scores, jnp.asarray(-1000000000.0, scores.dtype))
        attn = jax.nn.softmax(scores, axis=-1)
        out = jnp.einsum('bhqk,bhkd->bhqd', attn, Vh)
        rel_v = rel_v_table[idx]
        out = out + jnp.einsum('bhqk,qkd->bhqd', attn, rel_v)
        out = out.transpose(0, 2, 1, 3).reshape(B, S, E)
        return out @ W_o + b_o

    def _L1_ffn_ref(hidden_states, gate_W, w1_e, w3_e, w2_e, w1_s, w3_s, w2_s):
        import jax, jax.numpy as jnp
        import numpy as np
        B, S, D, F, E, NS, K = (2, 128, 128, 512, 8, 8, 2)
        FS = F // NS
        b, s, d = hidden_states.shape
        e = gate_W.shape[0]
        flat = hidden_states.reshape(-1, d)
        T = flat.shape[0]
        logits = (flat @ gate_W.T).astype(jnp.float32)
        probs = jax.nn.softmax(logits, axis=-1)
        top_v, top_i = jax.lax.top_k(probs, K)
        gates = jnp.zeros((T, e), probs.dtype).at[jnp.arange(T)[:, None], top_i].set(top_v)
        g = jax.nn.silu(jnp.einsum('td,edf->etf', flat, w1_e))
        u = jnp.einsum('td,edf->etf', flat, w3_e)
        out_e = jnp.einsum('etf,efd->etd', g * u, w2_e)
        routed = jnp.einsum('te,etd->td', gates, out_e).reshape(b, s, d)
        gs = jax.nn.silu(jnp.einsum('bsd,ndf->nbsf', hidden_states, w1_s))
        us = jnp.einsum('bsd,ndf->nbsf', hidden_states, w3_s)
        shared = jnp.einsum('nbsf,nfd->bsd', gs * us, w2_s) / w1_s.shape[0]
        alpha = 0.5
        return alpha * shared + (1.0 - alpha) * routed
    x = L0_attn_x
    x = x + 0.5 * _L0_ffn_ref(_layernorm(x, axis=-1), L0_ffn_gate_w, L0_ffn_w1, L0_ffn_w2)
    x = x + _L0_attn_ref(_layernorm(x, axis=-1), L0_attn_Wqkv, L0_attn_Wout, L0_attn_bout)
    x = x + 0.5 * _L0_ffn_ref(_layernorm(x, axis=-1), L0_ffn_gate_w, L0_ffn_w1, L0_ffn_w2)
    x = x + 0.5 * _L1_ffn_ref(_layernorm(x, axis=-1), L1_ffn_gate_W, L1_ffn_w1_e, L1_ffn_w3_e, L1_ffn_w2_e, L1_ffn_w1_s, L1_ffn_w3_s, L1_ffn_w2_s)
    x = x + _L1_attn_ref(_layernorm(x, axis=-1), L1_attn_W_q, L1_attn_b_q, L1_attn_W_k, L1_attn_b_k, L1_attn_W_v, L1_attn_b_v, L1_attn_W_o, L1_attn_b_o, L1_attn_rel_k_table, L1_attn_rel_v_table)
    x = x + 0.5 * _L1_ffn_ref(_layernorm(x, axis=-1), L1_ffn_gate_W, L1_ffn_w1_e, L1_ffn_w3_e, L1_ffn_w2_e, L1_ffn_w1_s, L1_ffn_w3_s, L1_ffn_w2_s)
    return x

_drawn_inputs = setup_inputs


def setup_inputs(seed=0):
    import zlib

    import numpy as np

    out = dict(_drawn_inputs(seed))
    spreads = {'L0_attn_bout': (0.0, 0.1),
     'L1_attn_b_q': (0.0, 0.375),
     'L1_attn_b_k': (0.0, 0.8),
     'L1_attn_b_v': (0.0, 0.1),
     'L1_attn_b_o': (0.0, 0.1)}
    factors = {'L0_attn_Wqkv': 4.764,
     'L0_attn_Wout': 4.578,
     'L0_ffn_gate_w': 5.6,
     'L0_ffn_w1': 4.957,
     'L0_ffn_w2': 4.876,
     'L1_ffn_gate_W': 8.0,
     'L1_ffn_w1_e': 8.0,
     'L1_ffn_w3_e': 8.0,
     'L1_ffn_w2_e': 8.0,
     'L1_ffn_w1_s': 8.0,
     'L1_ffn_w3_s': 8.0,
     'L1_ffn_w2_s': 8.0}
    for name, (base, spread) in spreads.items():
        noise = np.random.default_rng([zlib.crc32(name.encode()), seed]).standard_normal(out[name].shape)
        drawn = base * np.exp(spread * noise) if base else spread * noise
        out[name] = jnp.asarray(drawn.astype(out[name].dtype))
    for name, factor in factors.items():
        out[name] = (out[name] * factor).astype(out[name].dtype)
    return out
```

```python
from contextlib import ExitStack

import numpy as np

import concourse.bass as bass
from concourse import mybir

FP32 = mybir.dt.float32
BF16 = mybir.dt.bfloat16
ALU = mybir.AluOpType
ACT = mybir.ActivationFunctionType
AX = mybir.AxisListType

P = 128
B, S, D = 8, 256, 128
TPB = S // P
T = B * TPB
E = 8
F = 512
FT = F // P
CAP = 2 * S // E
H, HD = 16, 8
EPS = 1e-5
NEG = -1e30
TAKEN = -1.0


class Net:

    def __init__(self, nc, ctx, dram):
        self.nc, self.ctx, self.dram = nc, ctx, dram
        self.x = self.sb("x_tokens", [P, T, D])
        self.xnT = self.sb("normed_T", [P, T * P])
        self.xn = self.sb("normed_pair", [P, TPB, D])
        self.stats = self.sb("ln_stats", [P, T, 6])
        self.mv = self.sb("ln_mean_var", [P, T, 2])
        self.vareps = self.sb("ln_var_eps", [P, T])
        self.rstd = self.sb("ln_rstd", [P, T])
        self.minus_half = self.sb("minus_half", [P, T])
        self.ident = self.sb("ident", [P, P])
        self.identb = self.sb("ident_bf16", [P, P], BF16)
        self.scores = ctx.enter_context(nc.psum_tensor("banks0to3", [P, 2, 2, 512], FP32))
        later = [ctx.enter_context(nc.psum_tensor(f"bank{n}", [P, 512], FP32)) for n in range(4, 8)]
        self.bank = [self.scores[:, n // 2, n % 2, :] for n in range(4)] + [b[:, :] for b in later]
        self.bankb = [b.bitcast(BF16) for b in self.bank]
        self.logit = self.sb("router_logit", [P, T, E])
        self.prob = self.sb("router_prob", [P, T, E])
        self.rmax = self.sb("router_max", [P, T])
        self.rsum = self.sb("router_sum", [P, T])
        self.gate = self.sb("gate", [P, T, E])
        self.top8 = self.sb("top8", [P, T, 8])
        self.left = self.sb("probs_left", [P, T, E])
        self.probT = self.sb("prob_T", [B * E, S])
        self.leftT = self.sb("left_T", [B * E, S])
        self.gateT = self.sb("gate_T", [B * E, S])
        self.best = self.sb("best8", [B * E, 8])
        self.hid = self.sb("hidden", [P, 2, 2 * FT, P])
        self.sil = self.sb("silu_gate", [P, 2, 4 * P])
        self.acc = self.sb("expert_sum", [P, TPB, D])
        self.accb = self.sb("expert_sum_bf16", [P, TPB, D], BF16)
        self.xload = self.sem("x_loaded")
        self.const = self.sem("constants_made")
        self.ready = None

    def sb(self, name, shape, dt=FP32):
        return self.ctx.enter_context(self.nc.sbuf_tensor(name, shape, dt))

    def sem(self, name):
        return self.ctx.enter_context(self.nc.semaphore(name))


class Chain:

    def __init__(self, eng, sem, base=0):
        self.eng, self.sem, self.base, self.n = eng, sem, base, 0

    def __call__(self, ins):
        ins.then_inc(self.sem, 1)
        self.n += 1
        return self.base + self.n

    def then_wait(self, ins):
        self.eng.wait_ge(self.sem, self(ins))


def layernorm_stats(net, name):
    nc = net.nc
    own = net.sem(f"{name}_stats_chain")
    var_ready = net.sem(f"{name}_var_ready")
    rstd_ready = net.sem(f"{name}_rstd_ready")

    def vector(dve):
        chain = Chain(dve, own)
        for t in range(T):
            ins = nc.vector.bn_stats(net.stats[:, t, :], net.x[:, t, :])
        chain.then_wait(ins)
        for t in range(T):
            ins = nc.vector.bn_aggr(net.mv[:, t, :], net.stats[:, t, :])
        chain.then_wait(ins)
        nc.vector.tensor_scalar_add(net.vareps[:, :], net.mv[:, :, 1], EPS).then_inc(var_ready, 1)

    def gpsimd(pool):
        pool.wait_ge(var_ready, 1)
        nc.gpsimd.tensor_tensor(net.rstd[:, :], net.vareps[:, :], net.minus_half[:, :],
                                ALU.pow).then_inc(rstd_ready, 1)

    return vector, gpsimd, rstd_ready


class Moe:

    def __init__(self, net, name, choice, gate_w, w1, w3, w2, weights_sem, weights_count):
        self.net, self.name, self.choice = net, name, choice
        self.gate_w, self.w1, self.w3, self.w2 = gate_w, w1, w3, w2
        self.weights = (weights_sem, weights_count)
        self.before = net.ready
        self.experts = E if choice else E + 1
        self.stats_dve, self.stats_pool, self.rstd_ready = layernorm_stats(net, name)
        self.xn = net.sem(f"{name}_xn")
        self.xnT_psum = net.sem(f"{name}_xnT_psum")
        self.xnT = net.sem(f"{name}_xnT")
        self.logits = net.sem(f"{name}_logits")
        self.exps = net.sem(f"{name}_exps")
        self.logit = net.sem(f"{name}_logit")
        self.probT_psum = net.sem(f"{name}_probT_psum")
        self.picked = net.sem(f"{name}_picked")
        self.gateT_psum = net.sem(f"{name}_gateT_psum")
        self.gates = net.sem(f"{name}_gates")
        self.up = net.sem(f"{name}_up")
        self.act = net.sem(f"{name}_act")
        self.hidden = net.sem(f"{name}_hidden")
        self.down = net.sem(f"{name}_down")
        self.added = net.sem(f"{name}_added")
        self.turn = net.sem(f"{name}_turn")
        self.chain = net.sem(f"{name}_chain")
        self.loop_chain = net.sem(f"{name}_loop_chain")
        self.last = (self.turn, B)
        net.ready = self.last

    def vector(self, dve):
        net, nc = self.net, self.net.nc
        if self.before:
            dve.wait_ge(*self.before)
        else:
            dve.wait_ge(net.xload, 16)
            dve.wait_ge(net.const, 4)
        dve.sem_inc(self.loop_chain, 1)
        if not self.choice:
            dve.sem_inc(self.hidden, 1)
        self.stats_dve(dve)
        dve.wait_ge(self.rstd_ready, 1)
        with dve.Fori(0, B) as n:
            dve.wait_ge(self.xnT_psum, n + 1)
            for tt in range(TPB):
                t = n * TPB + tt
                ins = nc.vector.tensor_scalar(net.xn[:, tt, :], net.x[:, bass.ds(t, 1), :].rearrange("p a d -> p (a d)"),
                                              net.mv[:, bass.ds(t, 1), 0], net.rstd[:, bass.ds(t, 1)],
                                              ALU.subtract, ALU.mult)
            ins.then_inc(self.xn, 1)
        chain = Chain(dve, self.chain)
        dve.wait_ge(self.logits, 1)
        lg = net.bank[7][:, 0:T * E].rearrange("p (t e) -> p t e", e=E)
        chain.then_wait(nc.vector.reduce_max(net.rmax[:, :], lg, AX.X))
        nc.vector.tensor_tensor(net.logit[:, :, :], lg, net.rmax[:, :].unsqueeze(2).to_broadcast([P, T, E]),
                                ALU.subtract).then_inc(self.logit, 1)
        dve.wait_ge(self.exps, 1)
        chain.then_wait(nc.vector.reduce_sum(net.rsum[:, :], net.prob[:, :, :], AX.X))
        chain.then_wait(nc.vector.reciprocal(net.rsum[:, :], net.rsum[:, :]))
        chain.then_wait(nc.vector.tensor_tensor(net.prob[:, :, :], net.prob[:, :, :],
                                                net.rsum[:, :].unsqueeze(2).to_broadcast([P, T, E]), ALU.mult))
        if self.choice:
            self.expert_choice(dve, chain)
        else:
            self.token_choice(dve, chain)
        self.main_vector(dve)

    def expert_choice(self, dve, chain):
        net, nc = self.net, self.net.nc
        by_half = net.gate[:, :, :].rearrange("p t e -> p (t e)").rearrange("p (a n e) -> p n a e", a=TPB, n=B)
        chain.then_wait(nc.vector.tensor_copy(by_half, net.prob[:, :, :].rearrange("p (n a) e -> p n a e", a=TPB)))
        dve.wait_ge(self.probT_psum, 1)
        pt = net.bank[7][0:B * E, 256:512]
        chain.then_wait(nc.vector.tensor_copy(net.probT[:, :], pt))
        src = net.probT
        for r in range(CAP // 8):
            chain.then_wait(nc.vector.max(net.best[:, :], src[:, :]))
            chain.then_wait(nc.vector.match_replace(net.leftT[:, :], net.best[:, :], src[:, :], TAKEN))
            src = net.leftT
        nc.vector.scalar_tensor_tensor(net.gateT[:, :], net.leftT[:, :], 0.0, net.probT[:, :],
                                       ALU.is_lt, ALU.mult).then_inc(self.picked, 1)
        dve.wait_ge(self.gateT_psum, 1)
        gp = net.bank[7][:, 0:TPB * B * E].rearrange("p (a n e) -> p n a e", a=TPB, n=B)
        nc.vector.tensor_copy(net.gate[:, :, :].rearrange("p (n a) e -> p n a e", a=TPB), gp).then_inc(self.gates, 1)

    def token_choice(self, dve, chain):
        net, nc = self.net, self.net.nc
        for t in range(T):
            ins = nc.vector.max(net.top8[:, t, :], net.prob[:, t, :])
        chain.then_wait(ins)
        chain.then_wait(nc.vector.memset(net.top8[:, :, 2:8], -3.0))
        for t in range(T):
            ins = nc.vector.match_replace(net.left[:, t, :], net.top8[:, t, :], net.prob[:, t, :], TAKEN)
        chain.then_wait(ins)
        chain.then_wait(nc.vector.tensor_scalar(net.left[:, :, :], net.left[:, :, :], 0.0, 0.25, ALU.is_lt, ALU.mult))
        nc.vector.tensor_tensor(net.gate[:, :, :], net.left[:, :, :], net.prob[:, :, :],
                                ALU.mult).then_inc(self.gates, 1)

    def main_vector(self, dve):
        net, nc = self.net, self.net.nc
        ne = self.experts
        dve.wait_ge(self.gates, 1)
        with dve.Fori(0, B) as n:
            per = ne + (2 if self.choice else 0)
            chain = Chain(dve, self.loop_chain, n * per + 1)
            last_add = None

            def add(e):
                nonlocal last_add
                dve.wait_ge(self.down, n * ne + e + 2)
                y = net.bank[4 + e % 2]
                if last_add is not None:
                    dve.wait_ge(self.loop_chain, last_add)
                for tt in range(TPB):
                    t = n * TPB + tt
                    acc = net.acc[:, tt, :] if self.choice else net.x[:, bass.ds(t, 1), :].rearrange("p a d -> p (a d)")
                    yt = y[:, tt * D:(tt + 1) * D]
                    if e == E:
                        ins = nc.vector.scalar_tensor_tensor(acc, yt, 1 / 32, acc, ALU.mult, ALU.add)
                    elif self.choice and e == 0:
                        ins = nc.vector.tensor_scalar(acc, yt, net.gate[:, bass.ds(t, 1), e], None, ALU.mult)
                    else:
                        ins = nc.vector.scalar_tensor_tensor(acc, yt, net.gate[:, bass.ds(t, 1), e], acc,
                                                             ALU.mult, ALU.add)
                last_add = chain(ins)

            def gated(e, half):
                k = 2 * e + half
                dve.wait_ge(self.act, n * 2 * ne + k + 1)
                if e >= 2:
                    dve.wait_ge(self.down, n * ne + e)
                else:
                    dve.wait_ge(self.down, n * ne + 1)
                nc.vector.tensor_tensor(
                    net.hid[:, e % 2, 4 * half:4 * half + 4, :].rearrange("p a b -> p (a b)"),
                    net.sil[:, k % 2, :], net.bank[2 + k % 2][:, :], ALU.mult).then_inc(self.hidden, 1)

            for e in range(ne):
                if not self.choice:
                    gated(e, 0)
                    gated(e, 1)
                if e >= 1:
                    add(e - 1)
            add(ne - 1)
            dve.wait_ge(self.loop_chain, last_add)
            if self.choice:
                chain.then_wait(nc.vector.tensor_copy(net.accb[:, :, :], net.acc[:, :, :]))
                xt = net.x[:, bass.ds(n * TPB, TPB), :]
                chain.then_wait(nc.vector.scalar_tensor_tensor(xt, net.accb[:, :, :], 0.5, xt, ALU.mult, ALU.add))
            nc.vector.memset(net.best[0:1, 0:1], 0.0).then_inc(self.turn, 1)
            assert chain.n == per

    def gpsimd(self, pool):
        self.stats_pool(pool)

    def scalar(self, act):
        net, nc = self.net, self.net.nc
        act.sem_inc(self.xnT, 1)
        if self.choice:
            act.sem_inc(self.hidden, 1)
        with act.Fori(0, B) as n:
            act.wait_ge(self.xnT_psum, n + 2)
            nc.scalar.copy(net.xnT[:, bass.ds(n * S, S)], net.bank[6][:, 0:S]).then_inc(self.xnT, 1)
        act.wait_ge(self.logit, 1)
        nc.scalar.activation(net.prob[:, :, :], net.logit[:, :, :], ACT.Exp).then_inc(self.exps, 1)
        ne = self.experts
        with act.Fori(0, B) as n:
            if self.choice:
                for e in range(ne):
                    act.wait_ge(self.up, n * ne + e + 1)
                    act.wait_ge(self.down, n * ne + (e if e >= 2 else 1))
                    for half in range(2):
                        ins = nc.scalar.activation(
                            net.hid[:, e % 2, 4 * half:4 * half + 4, :].rearrange("p a b -> p (a b)"),
                            net.bank[2 * (e % 2) + half][:, :], ACT.Gelu_apprx_tanh)
                    ins.then_inc(self.hidden, 1)
            else:
                for k in range(2 * ne):
                    act.wait_ge(self.up, n * 2 * ne + k + 1)
                    act.wait_ge(self.hidden, n * 2 * ne + (k if k >= 2 else 1))
                    nc.scalar.activation(net.sil[:, k % 2, :], net.bank[k % 2][:, :], ACT.Silu).then_inc(self.act, 1)

    def tensor(self, pe):
        net, nc = self.net, self.net.nc
        ne = self.experts
        if not self.before:
            pe.wait_ge(net.const, 4)
        pe.sem_inc(self.xnT_psum, 1)
        pe.sem_inc(self.down, 1)
        with pe.Fori(0, B) as n:
            pe.wait_ge(self.xn, n + 1)
            pe.wait_ge(self.xnT, n + 1)
            for tt in range(TPB):
                ins = nc.tensor.transpose(net.bank[6][:, tt * P:(tt + 1) * P], net.xn[:, tt, :], net.ident[:, :])
            ins.then_inc(self.xnT_psum, 1)
        pe.wait_ge(self.xnT, B + 1)
        pe.wait_ge(*self.weights)
        for t in range(T):
            ins = nc.tensor.matmul(net.bank[7][:, t * E:(t + 1) * E], net.xnT[:, t * P:(t + 1) * P],
                                   self.gate_w, start=True, stop=True)
        ins.then_inc(self.logits, 1)
        if self.choice:
            pe.wait_ge(self.chain, 5)
            pr = net.gate[:, :, :].rearrange("p t e -> p (t e)")
            for tt in range(TPB):
                ins = nc.tensor.transpose(net.bank[7][0:B * E, 256 + tt * P:256 + (tt + 1) * P],
                                          pr[:, tt * B * E:(tt + 1) * B * E], net.ident[:, :])
            ins.then_inc(self.probT_psum, 1)
            pe.wait_ge(self.picked, 1)
            for tt in range(TPB):
                ins = nc.tensor.transpose(net.bank[7][:, tt * B * E:(tt + 1) * B * E],
                                          net.gateT[:, tt * P:(tt + 1) * P], net.ident[0:B * E, 0:B * E])
            ins.then_inc(self.gateT_psum, 1)
        with pe.Fori(0, B) as n:
            xt = net.xnT[:, bass.ds(n * S, S)]

            def up(e):
                if self.choice:
                    pe.wait_ge(self.hidden, n * ne + (e if e >= 2 else 1))
                    for f in range(FT):
                        ins = nc.tensor.matmul(net.bank[2 * (e % 2) + f // 2][:, (f % 2) * S:(f % 2 + 1) * S],
                                               self.w1[:, e, f * P:(f + 1) * P], xt, start=True, stop=True)
                    ins.then_inc(self.up, 1)
                    return
                for half in range(2):
                    k = 2 * e + half
                    pe.wait_ge(self.hidden, n * 2 * ne + (k if k >= 2 else 1))
                    for w, at in ((self.w1, 0), (self.w3, 2)):
                        for f in range(2):
                            c = (2 * half + f) * P
                            ins = nc.tensor.matmul(net.bank[at + k % 2][:, f * S:(f + 1) * S],
                                                   w[:, e, c:c + P], xt, start=True, stop=True)
                    ins.then_inc(self.up, 1)

            def down(e):
                per = ne if self.choice else 2 * ne
                pe.wait_ge(self.hidden, n * per + (e + 1) * (per // ne) + 1)
                steps = ne + (2 if self.choice else 0)
                pe.wait_ge(self.loop_chain, n * steps + (e if e >= 2 else 1))
                hid = net.hid[:, e % 2, :, :].rearrange("p (f a) t -> p f a t", a=TPB)
                for tt in range(TPB):
                    for f in range(FT):
                        ins = nc.tensor.matmul(net.bank[4 + e % 2][:, tt * D:(tt + 1) * D], hid[:, f, tt, :],
                                               self.w2[:, e, f, :], start=(f == 0), stop=(f == FT - 1))
                ins.then_inc(self.down, 1)

            for e in range(ne):
                up(e)
                if e >= 1:
                    down(e - 1)
            down(ne - 1)

    def sync(self, sp):
        pass


ST = 64
SPLIT_Q = ((0, 3), (3, 2), (5, 1))
SPLIT_K = (((0, 2, 3),), ((1, 2, 3),), ((2, 1, 1),))
SCALE = float(HD) ** -0.5


class Tally:

    def __init__(self, net, name, per):
        self.sem, self.per, self.n = net.sem(name), per, 0

    def at(self, n, k):
        return n * self.per + k + 1


class Attention:

    def __init__(self, net, name, rel, w):
        self.net, self.name, self.rel, self.w = net, name, rel, w
        self.before = net.ready
        self.pairs = ((0, 0), (1, 0), (1, 1)) if rel else ((0, 0), (1, 1))
        self.units = [(qt, kt, u) for qt, kt in self.pairs for u in range(2)]
        nu = len(self.units)
        self.stats_dve, self.stats_pool, self.rstd_ready = layernorm_stats(net, name)
        self.xn = Tally(net, f"{name}_xn", 1)
        self.xnT_psum = Tally(net, f"{name}_xnT_psum", 1)
        self.xnT = Tally(net, f"{name}_xnT", 1)
        self.proj = Tally(net, f"{name}_proj", 2)
        self.proj_read = Tally(net, f"{name}_proj_read", 2)
        self.parts = Tally(net, f"{name}_parts", 1)
        self.stacks = Tally(net, f"{name}_stacks", 1)
        self.stackT = Tally(net, f"{name}_stackT", 6)
        self.qkT = Tally(net, f"{name}_qkT", 4)
        self.a_scored = Tally(net, f"{name}_a_scored", nu)
        self.amax = Tally(net, f"{name}_amax", nu)
        self.mparts = Tally(net, f"{name}_mparts", 1)
        self.qTb = Tally(net, f"{name}_qTb", 2)
        self.b_scored = Tally(net, f"{name}_b_scored", nu)
        self.exps = Tally(net, f"{name}_exps", nu)
        self.pv = Tally(net, f"{name}_pv", nu)
        self.special = Tally(net, f"{name}_special", 1)
        self.pspecial = Tally(net, f"{name}_pspecial", 1)
        self.attended = Tally(net, f"{name}_attended", 2)
        self.oT_psum = Tally(net, f"{name}_oT_psum", 1)
        self.oT = Tally(net, f"{name}_oT", 1)
        self.y = Tally(net, f"{name}_y", 1)
        self.added = Tally(net, f"{name}_added", 1)
        self.steps = Tally(net, f"{name}_steps", 30 if rel else 17)
        self.stacking = net.sem(f"{name}_stacking")
        net.ready = (self.added.sem, B + 1)

    def permute(self, copy, dst, src, back=False):
        if self.rel:
            return copy(dst[:, 0:S], src[:, 0:S])
        for tt in range(TPB):
            runs = ((slice(tt * P, tt * P + 120), slice(tt * 120, tt * 120 + 120)),
                    (slice(tt * P + 120, tt * P + 128), slice(240 + tt, 255 + tt, 2)))
            for patched, natural in runs:
                to, fro = (natural, patched) if back else (patched, natural)
                ins = copy(dst[:, to], src[:, fro])
        return ins

    def scores_at(self, slot):
        return self.net.scores[:, slot, :, :]

    def vector(self, dve):
        net, nc, v = self.net, self.net.nc, self.net.nc.vector
        dve.wait_ge(*self.before) if self.before else dve.wait_ge(net.xload, 16)
        for t in (self.xn, self.proj_read, self.parts, self.amax, self.mparts, self.special, self.attended,
                  self.added, self.steps):
            dve.sem_inc(t.sem, 1)
        self.stats_dve(dve)
        dve.wait_ge(self.rstd_ready, 1)
        dve.wait_ge(net.att_const, 1)
        with dve.Fori(0, B) as n:
            chain = Chain(dve, self.steps.sem, n * self.steps.per + 1)
            dve.wait_ge(self.xnT_psum.sem, self.xnT_psum.at(n, 0))
            for tt in range(TPB):
                t = n * TPB + tt
                ins = v.tensor_scalar(net.xn[:, tt, :], net.x[:, bass.ds(t, 1), :].rearrange("p a d -> p (a d)"),
                                      net.mv[:, bass.ds(t, 1), 0], net.rstd[:, bass.ds(t, 1)],
                                      ALU.subtract, ALU.mult)
            ins.then_inc(self.xn.sem, 1)
            for tt in range(TPB):
                dve.wait_ge(self.proj.sem, self.proj.at(n, tt + 1))
                main, shifted = self.proj_banks(tt)
                vaug = net.vaug[:, tt, :, 0:HD]
                vps = main[:, 2 * D:3 * D].rearrange("p (h d) -> p h d", d=HD)
                if self.rel:
                    chain(v.tensor_tensor(net.qk[:, tt, :], main[:, 0:2 * D], net.add_far[:, 0:2 * D], ALU.add))
                    chain(v.tensor_tensor(vaug, vps, net.add_far[:, 2 * D:3 * D].rearrange("p (h d) -> p h d", d=HD),
                                          ALU.add))
                    chain(v.tensor_tensor(net.kv2[:, tt, 0, :], main[:, D:3 * D], net.add_self[:, :], ALU.add))
                    v.tensor_tensor(net.kv2[:, tt, 1, :], shifted[:, 0:2 * D], net.add_prev[:, :],
                                    ALU.add).then_inc(self.proj_read.sem, 1)
                else:
                    chain(v.tensor_copy(net.qk[:, tt, :], main[:, 0:2 * D]))
                    v.tensor_copy(vaug, vps).then_inc(self.proj_read.sem, 1)
            dve.wait_ge(self.proj_read.sem, self.proj_read.at(n, 2))
            chain.then_wait(v.tensor_copy(net.part[:, 0], net.qk[:, :, :]))
            chain.then_wait(v.tensor_tensor(net.rest[:, :, :], net.qk[:, :, :], net.part[:, 0], ALU.subtract))
            chain.then_wait(v.tensor_copy(net.part[:, 1], net.rest[:, :, :]))
            chain.then_wait(v.tensor_tensor(net.rest[:, :, :], net.rest[:, :, :], net.part[:, 1], ALU.subtract))
            v.tensor_copy(net.part[:, 2], net.rest[:, :, :]).then_inc(self.parts.sem, 1)
            if self.rel:
                for tt in range(TPB):
                    ins = v.tensor_tensor(net.prod[:, tt, :, :], net.kv2[:, tt, :, 0:D],
                                          net.qk[:, tt, 0:D].unsqueeze(1).to_broadcast([P, 2, D]), ALU.mult)
                chain.then_wait(ins)
                chain.then_wait(v.reduce_sum(
                    net.sp[:, :, :, :].rearrange("p a b h -> p (a b h)"),
                    net.prod[:, :, :, :].rearrange("p a b (h d) -> p (a b h) d", d=HD), AX.X))
                chain.then_wait(v.tensor_scalar(net.sp[:, 0, 1, :], net.sp[:, 0, 1, :], net.first_row[:, :], None,
                                                ALU.add))
            for a, (qt, kt, u) in enumerate(self.units):
                dve.wait_ge(self.a_scored.sem, self.a_scored.at(n, a + 1))
                out = net.mx[:, int(kt != qt), qt, :].rearrange("p (j r) -> p r j", r=2)[:, :, 4 * u:4 * u + 4]
                v.reduce_max(out, self.scores_at(a % 2).rearrange("p r (j k) -> p r j k", j=4),
                             AX.X).then_inc(self.amax.sem, 1)
            dve.wait_ge(self.amax.sem, self.amax.at(n, len(self.units)))
            m = net.mx[:, 0, :, :]
            if self.rel:
                chain.then_wait(v.tensor_tensor(m, m, net.sp[:, :, 0, :], ALU.max))
                chain.then_wait(v.tensor_tensor(m, m, net.sp[:, :, 1, :], ALU.max))
                chain.then_wait(v.tensor_tensor(net.mx[:, 0, 1, :], net.mx[:, 0, 1, :], net.mx[:, 1, 1, :], ALU.max))
            else:
                chain.then_wait(v.tensor_scalar(m, m, net.short_row[:, :], None, ALU.max))
            chain.then_wait(v.tensor_scalar(net.mneg[:, :, :], m, -1.0, None, ALU.mult))
            mrow = [net.qs[:, :, :, 48 + i] for i in range(3)]
            chain.then_wait(v.tensor_copy(mrow[0], net.mneg[:, :, :]))
            chain.then_wait(v.tensor_tensor(net.mrest[:, :, :], net.mneg[:, :, :], mrow[0], ALU.subtract))
            chain.then_wait(v.tensor_copy(mrow[1], net.mrest[:, :, :]))
            chain.then_wait(v.tensor_tensor(net.mrest[:, :, :], net.mrest[:, :, :], mrow[1], ALU.subtract))
            v.tensor_copy(mrow[2], net.mrest[:, :, :]).then_inc(self.mparts.sem, 1)
            if self.rel:
                v.tensor_tensor(net.sp[:, :, :, :], net.sp[:, :, :, :],
                                net.mneg[:, :, :].unsqueeze(2).to_broadcast([P, TPB, 2, H]),
                                ALU.add).then_inc(self.special.sem, 1)
                dve.wait_ge(self.pspecial.sem, self.pspecial.at(n, 1))
                for tt in range(TPB):
                    v2 = net.kv2[:, tt, :, D:2 * D].rearrange("p b (h d) -> p b h d", d=HD)
                    ins = v.tensor_tensor(net.prod[:, tt, :, :].rearrange("p b (h d) -> p b h d", d=HD), v2,
                                          net.sp[:, tt, :, :].unsqueeze(3).to_broadcast([P, 2, H, HD]), ALU.mult)
                chain.then_wait(ins)
                chain.then_wait(v.tensor_tensor(net.prod[:, :, 0, :], net.prod[:, :, 0, :], net.prod[:, :, 1, :],
                                                ALU.add))
                chain.then_wait(v.tensor_tensor(net.sp[:, :, 0, :], net.sp[:, :, 0, :], net.sp[:, :, 1, :],
                                                ALU.add))
            else:
                v.tensor_scalar(net.sp[:, :, 0, :], net.mneg[:, :, :], net.short_row[:, :], None,
                                ALU.add).then_inc(self.special.sem, 1)
                dve.wait_ge(self.pspecial.sem, self.pspecial.at(n, 1))
                chain.then_wait(v.tensor_scalar(net.sp[:, :, 0, :], net.sp[:, :, 0, :], 12.0, None, ALU.mult))
            for qt in range(TPB):
                done = sum(1 for q, _, _ in self.units if q <= qt)
                dve.wait_ge(self.pv.sem, self.pv.at(n, done))
                pv = net.bank[6 - qt][:, 0:H * (HD + 1)].rearrange("p (h d) -> p h d", d=HD + 1)
                den = net.den[:, qt, :]
                chain.then_wait(v.tensor_tensor(den, pv[:, :, HD], net.sp[:, qt, 0, :], ALU.add))
                chain.then_wait(v.reciprocal(den, den))
                o = net.att[:, qt, :].rearrange("p (h d) -> p h d", d=HD)
                src = pv[:, :, 0:HD]
                if self.rel:
                    chain.then_wait(v.tensor_tensor(o, src, net.prod[:, qt, 0, :].rearrange("p (h d) -> p h d", d=HD),
                                                    ALU.add))
                    src = o
                v.tensor_tensor(o, src, den.unsqueeze(2).to_broadcast([P, H, HD]),
                                ALU.mult).then_inc(self.attended.sem, 1)
            dve.wait_ge(self.y.sem, self.y.at(n, 1))
            xt = net.x[:, bass.ds(n * TPB, TPB), :]
            v.tensor_tensor(xt, net.bank[7][:, S:2 * S].rearrange("p (a d) -> p a d", a=TPB), xt,
                            ALU.add).then_inc(self.added.sem, 1)
            assert chain.n == self.steps.per, chain.n

    def proj_banks(self, tt):
        return self.net.bank[6 - 2 * tt], self.net.bank[7 - 2 * tt]

    def gpsimd(self, pool):
        net, g = self.net, self.net.nc.gpsimd
        self.stats_pool(pool)
        pool.sem_inc(self.stacks.sem, 1)
        with pool.Fori(0, B) as n:
            pool.wait_ge(self.parts.sem, self.parts.at(n, 1))
            pool.sem_inc(self.stacking, 1)
            g.memset(net.qs[:, :, :, 48:51], 0.0)
            for tt in range(TPB):
                for i in range(3):
                    q = net.part[:, i, tt, 0:D].rearrange("p (h d) -> p h d", d=HD).unsqueeze(2)
                    k = net.part[:, i, tt, D:2 * D].rearrange("p (h d) -> p h d", d=HD).unsqueeze(2)
                    first, many = SPLIT_Q[i]
                    slots = net.qs[:, tt, :, 0:48].rearrange("p h (s d) -> p h s d", d=HD)
                    g.tensor_copy(slots[:, :, first:first + many, :], q.to_broadcast([P, H, many, HD]))
                    slots = net.ks[:, tt, :, 0:48].rearrange("p h (s d) -> p h s d", d=HD)
                    for first, many, step in SPLIT_K[i]:
                        ins = g.tensor_copy(slots[:, :, first:first + (many - 1) * step + 1:step, :],
                                            k.to_broadcast([P, H, many, HD]))
                ins = g.tensor_copy(slots[:, :, 5, :], net.part[:, 0, tt, D:2 * D].rearrange("p (h d) -> p h d", d=HD))
            ins.then_inc(self.stacks.sem, 1)

    def scalar(self, act):
        net, nc = self.net, self.net.nc
        for t in (self.xnT, self.qkT, self.qTb, self.exps, self.pspecial, self.oT):
            act.sem_inc(t.sem, 1)
        with act.Fori(0, B) as n:
            act.wait_ge(self.xnT_psum.sem, self.xnT_psum.at(n, 1))
            self.permute(nc.scalar.copy, net.xnTb[:, 1:1 + S], net.bank[5][:, 0:S]).then_inc(self.xnT.sem, 1)
            for g, (dst, bank) in enumerate(((net.qT[:, 0], 4), (net.kT[:, 0], 5), (net.qT[:, 1], 6), (net.kT[:, 1], 7))):
                act.wait_ge(self.stackT.sem, self.stackT.at(n, g + 1))
                nc.scalar.copy(dst.rearrange("p j t -> p (j t)"), net.bankb[bank]).then_inc(self.qkT.sem, 1)
            for tt in range(TPB):
                act.wait_ge(self.stackT.sem, self.stackT.at(n, 5 + tt))
                nc.scalar.copy(net.qTm[:, tt].rearrange("p j t -> p (j t)"), net.bankb[4 + tt]).then_inc(self.qTb.sem, 1)
            act.wait_ge(self.special.sem, self.special.at(n, 1))
            sp = net.sp[:, :, :, :] if self.rel else net.sp[:, :, 0, :]
            nc.scalar.activation(sp, sp, ACT.Exp).then_inc(self.pspecial.sem, 1)
            for b in range(len(self.units)):
                act.wait_ge(self.b_scored.sem, self.b_scored.at(n, b + 1))
                act.wait_ge(self.pv.sem, self.pv.at(n, max(b - 1, 0)))
                nc.scalar.activation(net.pT[:, b % 2, :, :], self.scores_at(b % 2), ACT.Exp).then_inc(self.exps.sem, 1)
            act.wait_ge(self.oT_psum.sem, self.oT_psum.at(n, 1))
            self.permute(nc.scalar.copy, net.oT[:, :], net.bank[7][:, 0:S], back=True).then_inc(self.oT.sem, 1)

    def tensor(self, pe):
        net, nc, mm = self.net, self.net.nc, self.net.nc.tensor.matmul
        w = self.w
        nu = len(self.units)
        pe.wait_ge(net.att_const, 1)
        pe.wait_ge(*w["loaded"])
        for t in (self.xnT_psum, self.proj, self.stackT, self.a_scored, self.b_scored, self.pv, self.oT_psum, self.y):
            pe.sem_inc(t.sem, 1)

        def score(slot, left, right, lt, rt, u, mask):
            for r in range(2):
                bank = self.scores_at(slot)[:, r, :]
                mm(bank, net.identb[:, :], mask.unsqueeze(1).to_broadcast([P, 4, P]), start=True, stop=False,
                   skip_group_check=True)
            for jj in range(4):
                for r in range(2):
                    rows = slice(64 * r, 64 * r + 64)
                    ins = mm(self.scores_at(slot)[:, r, jj * P:(jj + 1) * P], left[rows, lt, 4 * u + jj, :],
                             right[rows, rt, 4 * u + jj, :], start=False, stop=(jj == 3), skip_group_check=True)
            return ins

        with pe.Fori(0, B) as n:
            pe.wait_ge(self.xn.sem, self.xn.at(n, 1))
            pe.wait_ge(self.attended.sem, self.attended.at(n, 0))
            for tt in range(TPB):
                ins = nc.tensor.transpose(net.bank[5][:, tt * P:(tt + 1) * P], net.xn[:, tt, :], net.ident[:, :])
            ins.then_inc(self.xnT_psum.sem, 1)
            pe.wait_ge(self.xnT.sem, self.xnT.at(n, 1))
            pe.wait_ge(self.added.sem, self.added.at(n, 0))
            for tt in range(TPB):
                main, shifted = self.proj_banks(tt)
                ins = mm(main[:, 0:3 * D], net.xnTb[:, 1 + tt * P:1 + (tt + 1) * P], w["qkv"], start=True, stop=True)
                if self.rel:
                    ins = mm(shifted[:, 0:2 * D], net.xnTb[:, tt * P:(tt + 1) * P], w["qkv"][:, D:3 * D],
                             start=True, stop=True)
                ins.then_inc(self.proj.sem, 1)
            pe.wait_ge(self.stacks.sem, self.stacks.at(n, 1))
            pe.wait_ge(self.proj_read.sem, self.proj_read.at(n, 2))
            for src, tt, bank in ((net.qs, 0, 4), (net.ks, 0, 5), (net.qs, 1, 6), (net.ks, 1, 7)):
                for j in range(H // 2):
                    ins = nc.tensor.transpose(net.bankb[bank][:, j * P:(j + 1) * P],
                                              src[:, tt, 2 * j:2 * j + 2, :].rearrange("p h s -> p (h s)"),
                                              net.identb[:, :])
                ins.then_inc(self.stackT.sem, 1)
            pe.wait_ge(self.qkT.sem, self.qkT.at(n, 4))
            for a, (qt, kt, u) in enumerate(self.units):
                if a < 2:
                    pe.wait_ge(self.exps.sem, self.exps.at(n, 0))
                else:
                    pe.wait_ge(self.amax.sem, self.amax.at(n, a - 1))
                score(a % 2, net.qT, net.kT, qt, kt, u, w["mask"][kt == qt]).then_inc(self.a_scored.sem, 1)
            pe.wait_ge(self.mparts.sem, self.mparts.at(n, 1))
            for tt in range(TPB):
                for j in range(H // 2):
                    ins = nc.tensor.transpose(net.bankb[4 + tt][:, j * P:(j + 1) * P],
                                              net.qs[:, tt, 2 * j:2 * j + 2, :].rearrange("p h s -> p (h s)"),
                                              net.identb[:, :])
                ins.then_inc(self.stackT.sem, 1)

            def values(b):
                qt, kt, u = self.units[b]
                pe.wait_ge(self.exps.sem, self.exps.at(n, b + 1))
                for r in range(2):
                    for jj in range(4):
                        h = 2 * (4 * u + jj) + r
                        at = h * (HD + 1)
                        first = b == 0 or self.units[b - 1][0] != qt
                        ins = mm(net.bank[6 - qt][:, at:at + HD + 1], net.pT[:, b % 2, r, jj * P:(jj + 1) * P],
                                 net.vaug[:, kt, h, :], start=(first and r == 0 and jj == 0),
                                 stop=(kt == qt and u == 1 and r == 1 and jj == 3), skip_group_check=True)
                ins.then_inc(self.pv.sem, 1)

            for b, (qt, kt, u) in enumerate(self.units):
                pe.wait_ge(self.qTb.sem, self.qTb.at(n, qt + 1))
                if b < 2:
                    pe.wait_ge(self.amax.sem, self.amax.at(n, nu - 1 + b))
                else:
                    pe.wait_ge(self.exps.sem, self.exps.at(n, b - 1))
                score(b % 2, net.kT, net.qTm, kt, qt, u, w["maskT"][kt == qt]).then_inc(self.b_scored.sem, 1)
                if b >= 1:
                    values(b - 1)
            values(nu - 1)
            pe.wait_ge(self.attended.sem, self.attended.at(n, 2))
            for tt in range(TPB):
                ins = nc.tensor.transpose(net.bank[7][:, tt * P:(tt + 1) * P], net.att[:, tt, :], net.ident[:, :])
            ins.then_inc(self.oT_psum.sem, 1)
            pe.wait_ge(self.oT.sem, self.oT.at(n, 1))
            for tt in range(TPB):
                y = net.bank[7][:, S + tt * D:S + (tt + 1) * D]
                mm(y, net.oT[:, tt * P:(tt + 1) * P], w["out"], start=True, stop=False)
                ins = mm(y, net.ones[:, :], w["bias"], start=False, stop=True)
            ins.then_inc(self.y.sem, 1)


def attention_buffers(net):
    sb = net.sb
    net.xnTb = sb("normed_T_batch", [P, 1 + S])
    net.qk = sb("q_k", [P, TPB, 2 * D])
    net.vaug = sb("v_and_one", [P, TPB, H, HD + 1])
    net.kv2 = sb("kv_self_and_previous", [P, TPB, 2, 2 * D])
    net.part = sb("bf16_parts", [P, 3, TPB, 2 * D], BF16)
    net.rest = sb("split_rest", [P, TPB, 2 * D])
    net.prod = sb("special_products", [P, TPB, 2, D])
    net.sp = sb("special_scores", [P, TPB, 2, H])
    net.mx = sb("score_max", [P, 2, TPB, H])
    net.mneg = sb("minus_max", [P, TPB, H])
    net.mrest = sb("minus_max_rest", [P, TPB, H])
    net.qs = sb("q_stack", [P, TPB, H, ST], BF16)
    net.ks = sb("k_stack", [P, TPB, H, ST], BF16)
    net.qT = sb("q_stack_T", [P, TPB, H // 2, P], BF16)
    net.qTm = sb("q_stack_max_T", [P, TPB, H // 2, P], BF16)
    net.kT = sb("k_stack_T", [P, TPB, H // 2, P], BF16)
    net.pT = sb("exp_scores_T", [P, 2, 2, 512])
    net.den = sb("softmax_sum", [P, TPB, H])
    net.att = sb("attended_tokens", [P, TPB, D])
    net.oT = sb("attended_T", [P, S])
    net.ones = sb("ones_row", [1, P])
    net.add_far = sb("add_far", [P, 3 * D])
    net.add_self = sb("add_self", [P, 2 * D])
    net.add_prev = sb("add_prev", [P, 2 * D])
    net.first_row = sb("first_row_mask", [P, 1])
    net.short_row = sb("short_patch_rows", [P, 1])
    net.causal = sb("causal_masks", [P, 4, P], BF16)
    net.patch = sb("patch_mask", [P, P], BF16)
    net.member = sb("patch_members", [7, P])
    net.bias = sb("biases_everywhere", [P, 3 * D])
    net.table = sb("rel_tables_everywhere", [P, 2, 3, HD])
    net.patchsum = net.sem("patch_members_multiplied")
    net.made = net.sem("attention_constants_steps")
    net.att_const = net.sem("attention_constants_ready")
    net.biases = net.sem("biases_loaded")


def attention_constants(net, block_gpsimd):
    g, pool = net.nc.gpsimd, block_gpsimd
    chain = Chain(pool, net.made)
    for t, value in ((net.xnTb[:, 0:1], 0.0), (net.vaug[:, :, :, HD], 1.0), (net.qs[:, :, :, :], 0.0),
                     (net.ks[:, :, :, :], 0.0), (net.ones[:, :], 1.0), (net.first_row[:, :], 0.0),
                     (net.short_row[:, :], 0.0), (net.causal[:, :, :], 0.0), (net.member[:, :], 1.0)):
        ins = g.memset(t, value)
    chain.then_wait(ins)
    g.memset(net.ks[:, :, :, 48:51], 1.0)
    for i, (base, sign) in enumerate(((S // 2 - 2, 1), (-2, 1), (S // 2 - 2, -1), (-2, -1))):
        g.affine_select(out=net.causal[:, i, :], in_=net.causal[:, i, :], compare_op=ALU.is_ge, fill=NEG,
                        base=base, pattern=[[-sign, P]], channel_multiplier=sign)
    g.affine_select(out=net.first_row[:, :], in_=net.first_row[:, :], compare_op=ALU.is_ge, fill=NEG, base=-1,
                    pattern=[[0, 1]], channel_multiplier=1)
    g.affine_select(out=net.short_row[:, :], in_=net.short_row[:, :], compare_op=ALU.is_ge, fill=NEG, base=-120,
                    pattern=[[0, 1]], channel_multiplier=1)
    whole = net.member[:, 0:120].rearrange("p (b i r) -> p b i r", b=3, r=2)
    g.affine_select(out=whole, in_=whole, compare_op=ALU.is_equal, fill=0.0, base=0,
                    pattern=[[-2, 3], [0, 20], [-1, 2]], channel_multiplier=1)
    chain.then_wait(g.affine_select(out=net.member[:, 120:128], in_=net.member[:, 120:128], compare_op=ALU.is_equal,
                                    fill=0.0, base=-6, pattern=[[0, 8]], channel_multiplier=1))
    pool.wait_ge(net.biases, 9 * 16)
    far = net.add_far
    chain.then_wait(g.tensor_scalar(far[:, 0:D], net.bias[:, 0:D], SCALE, None, ALU.mult))
    for kv in range(2):
        b = net.bias[:, (1 + kv) * D:(2 + kv) * D].rearrange("p (h d) -> p h d", d=HD)
        for row, dst in ((0, far[:, (1 + kv) * D:(2 + kv) * D]), (1, net.add_prev[:, kv * D:(kv + 1) * D]),
                         (2, net.add_self[:, kv * D:(kv + 1) * D])):
            ins = g.tensor_tensor(dst.rearrange("p (h d) -> p h d", d=HD), b,
                                  net.table[:, kv, row, :].unsqueeze(1).to_broadcast([P, H, HD]), ALU.add)
    for q in (net.wqkv0[:, 0:D], net.wqkv1[:, 0:D]):
        ins = g.tensor_scalar(q, q, SCALE, None, ALU.mult)
    chain.then_wait(ins)


def attention_mask(net, dve):
    dve.wait_ge(net.patchsum, 1)
    dve.wait_ge(net.made, 4)
    net.nc.vector.tensor_scalar(net.patch[:, :], net.bank[0][:, 0:P], -1.0, -NEG, ALU.add,
                                ALU.mult).then_inc(net.att_const, 1)


def attention_mask_members(net, pe):
    pe.wait_ge(net.made, 2)
    net.nc.tensor.matmul(net.bank[0][:, 0:P], net.member[:, :], net.member[:, :], start=True,
                         stop=True).then_inc(net.patchsum, 1)


def build(nc, x, l0_qkv, l0_out, l0_bout, l1_q, l1_k, l1_v, l1_bq, l1_bk, l1_bv, l1_out, l1_bout, rel_k, rel_v, l0_gate, l0_w1, l0_w2, l1_gate, l1_w1, l1_w3, l1_w2, l1_s1, l1_s3, l1_s2, out, stages=range(6)):
    with ExitStack() as ctx:
        net = Net(nc, ctx, None)
        l0_gate_sb = net.sb("l0_gate_w", [P, E])
        l0_w1_sb = net.sb("l0_w1", [P, E, F])
        l0_w2_sb = net.sb("l0_w2", [P, E, FT, D])
        l1_gate_sb = net.sb("l1_gate_w", [P, E])
        l1_w1_sb = net.sb("l1_w1", [P, E + 1, F])
        l1_w3_sb = net.sb("l1_w3", [P, E + 1, F])
        l1_w2_sb = net.sb("l1_w2", [P, E + 1, FT, D])
        l0_loaded = net.sem("l0_weights_loaded")
        l1_loaded = net.sem("l1_weights_loaded")
        stored = net.sem("stored")

        net.wqkv0 = net.sb("l0_wqkv", [P, 3 * D])
        net.wqkv1 = net.sb("l1_wqkv", [P, 3 * D])
        l0_wout = net.sb("l0_wout", [P, D])
        l1_wout = net.sb("l1_wout", [P, D])
        l0_bias = net.sb("l0_bout", [1, D])
        l1_bias = net.sb("l1_bout", [1, D])
        att_loaded = net.sem("attention_weights_loaded")
        attention_buffers(net)
        patched = dict(qkv=net.wqkv0[:, :], out=l0_wout[:, :], bias=l0_bias[:, :], loaded=(att_loaded, 4 * 16),
                       mask=(None, net.patch[:, :]), maskT=(None, net.patch[:, :]))
        causal = dict(qkv=net.wqkv1[:, :], out=l1_wout[:, :], bias=l1_bias[:, :], loaded=(att_loaded, 4 * 16),
                      mask=(net.causal[:, 0, :], net.causal[:, 1, :]), maskT=(net.causal[:, 2, :], net.causal[:, 3, :]))
        made = []

        def l0_ffn(name):
            made.append(Moe(net, name, True, l0_gate_sb[:, :], l0_w1_sb, None, l0_w2_sb, l0_loaded, 3 * 16))

        def l1_ffn(name):
            made.append(Moe(net, name, False, l1_gate_sb[:, :], l1_w1_sb, l1_w3_sb, l1_w2_sb, l1_loaded, 7 * 16))

        for stage in stages:
            if stage in (0, 2):
                l0_ffn(f"l0_ffn_{stage}")
            if stage in (1, 4):
                made.append(Attention(net, f"attn_{stage}", stage == 4, causal if stage == 4 else patched))
            if stage in (3, 5):
                l1_ffn(f"l1_ffn_{stage}")

        block = ctx.enter_context(nc.Block())

        @block.sync
        def _(sp):
            sp.dma_start(net.x[:, :, :], x.rearrange("b (a p) d -> p (b a) d", p=P)).then_inc(net.xload, 16)
            row = lambda b: b.rearrange("(a n) -> a n", a=1)
            sp.dma_start(net.wqkv0[:, :], l0_qkv).then_inc(net.biases, 16)
            for i, w in enumerate((l1_q, l1_k, l1_v)):
                sp.dma_start(net.wqkv1[:, i * D:(i + 1) * D], w).then_inc(net.biases, 16)
            for i, b in enumerate((l1_bq, l1_bk, l1_bv)):
                sp.dma_start(net.bias[:, i * D:(i + 1) * D], row(b).to_broadcast([P, D])).then_inc(net.biases, 16)
            for i, t in enumerate((rel_k, rel_v)):
                sp.dma_start(net.table[:, i, :, :].rearrange("p r d -> p (r d)"),
                             row(t.rearrange("r d -> (r d)")[0:3 * HD]).to_broadcast([P, 3 * HD])).then_inc(net.biases, 16)
            sp.dma_start(l0_wout[:, :], l0_out).then_inc(att_loaded, 16)
            sp.dma_start(l1_wout[:, :], l1_out).then_inc(att_loaded, 16)
            sp.dma_start(l0_bias[:, :], row(l0_bout)).then_inc(att_loaded, 16)
            sp.dma_start(l1_bias[:, :], row(l1_bout)).then_inc(att_loaded, 16)
            sp.dma_start(l0_gate_sb[:, :], l0_gate).then_inc(l0_loaded, 16)
            sp.dma_start(l0_w1_sb[:, :, :], l0_w1.rearrange("e d f -> d e f")).then_inc(l0_loaded, 16)
            sp.dma_start(l0_w2_sb[:, :, :, :], l0_w2.rearrange("e (f p) d -> p (e f) d", p=P).rearrange("p (e f) d -> p e f d", e=E)).then_inc(l0_loaded, 16)
            sp.dma_start(l1_gate_sb[:, :], l1_gate).then_inc(l1_loaded, 16)
            sp.dma_start(l1_w1_sb[:, 0:E, :], l1_w1.rearrange("e d f -> d e f")).then_inc(l1_loaded, 16)
            sp.dma_start(l1_w3_sb[:, 0:E, :], l1_w3.rearrange("e d f -> d e f")).then_inc(l1_loaded, 16)
            sp.dma_start(l1_w2_sb[:, 0:E, :, :], l1_w2.rearrange("e (f p) d -> p (e f) d", p=P).rearrange("p (e f) d -> p e f d", e=E)).then_inc(l1_loaded, 16)
            sp.dma_start(l1_w1_sb[:, E, :], l1_s1.rearrange("n d f -> d n f")).then_inc(l1_loaded, 16)
            sp.dma_start(l1_w3_sb[:, E, :], l1_s3.rearrange("n d f -> d n f")).then_inc(l1_loaded, 16)
            sp.dma_start(l1_w2_sb[:, E, :, :], l1_s2.rearrange("(f a) q d -> (a q) f d", a=2)).then_inc(l1_loaded, 16)
            sp.wait_ge(*net.ready)
            sp.dma_start(out.rearrange("b (a p) d -> p (b a) d", p=P), net.x[:, :, :]).then_inc(stored, 16)
            sp.wait_ge(stored, 16)

        @block.gpsimd
        def _(pool):
            nc.gpsimd.memset(net.ident[:, :], 1.0).then_inc(net.const, 1)
            nc.gpsimd.memset(net.minus_half[:, :], -0.5).then_inc(net.const, 1)
            pool.wait_ge(net.const, 2)
            nc.gpsimd.affine_select(out=net.ident[:, :], in_=net.ident[:, :], compare_op=ALU.is_equal, fill=0.0,
                                    base=0, pattern=[[-1, P]], channel_multiplier=1).then_inc(net.const, 1)
            pool.wait_ge(net.const, 3)
            nc.gpsimd.tensor_copy(net.identb[:, :], net.ident[:, :]).then_inc(net.const, 1)
            attention_constants(net, pool)
            for stage in made:
                stage.gpsimd(pool)

        @block.vector
        def _(dve):
            attention_mask(net, dve)
            for stage in made:
                stage.vector(dve)

        @block.scalar
        def _(act):
            for stage in made:
                stage.scalar(act)

        @block.tensor
        def _(pe):
            attention_mask_members(net, pe)
            pe.wait_ge(net.att_const, 1)
            for stage in made:
                stage.tensor(pe)


_INS = ["L0_attn_x", "L0_attn_Wqkv", "L0_attn_Wout", "L0_attn_bout", "L1_attn_W_q", "L1_attn_W_k", "L1_attn_W_v",
        "L1_attn_b_q", "L1_attn_b_k", "L1_attn_b_v", "L1_attn_W_o", "L1_attn_b_o", "L1_attn_rel_k_table",
        "L1_attn_rel_v_table", "L0_ffn_gate_w", "L0_ffn_w1", "L0_ffn_w2", "L1_ffn_gate_W", "L1_ffn_w1_e", "L1_ffn_w3_e",
        "L1_ffn_w2_e", "L1_ffn_w1_s", "L1_ffn_w3_s", "L1_ffn_w2_s"]
_TURNED = {"L1_ffn_gate_W", "L0_attn_Wqkv", "L0_attn_Wout"}


def kernel(**inputs):
    import concourse.bacc as bacc
    from concourse.bass_utils import run_bass_kernel_spmd

    nc = bacc.Bacc("TRN2", target_bir_lowering=False, num_devices=1)
    arrays, args = {}, []
    for name in _INS:
        a = np.asarray(inputs[name])
        a = np.ascontiguousarray(a.T if name in _TURNED else a)
        arrays[f"in_{name}"] = a
        args.append(nc.dram_tensor(f"in_{name}", a.shape, mybir.dt.from_np(a.dtype), kind="ExternalInput").ap())
    out = nc.dram_tensor("out_x", (B, S, D), FP32, kind="ExternalOutput").ap()
    build(nc, *args, out)
    r = run_bass_kernel_spmd(nc, [arrays], core_ids=[0])
    return r.results[0]["out_x"]
```

```python
from contextlib import ExitStack

import numpy as np

import concourse.bass as bass
from concourse import mybir

FP32 = mybir.dt.float32
BF16 = mybir.dt.bfloat16
FP32R = mybir.dt.float32r
ALU = mybir.AluOpType
ACT = mybir.ActivationFunctionType
AX = mybir.AxisListType

P = 128
B, S, D = 8, 256, 128
TPB = S // P
T = B * TPB
E = 8
F = 512
FT = F // P
NE = E + 1
SHARED = 0.5 * 0.5 / 8
STEPS = 2 * NE
CHOICE_WORDS = 4096
CAP = 2 * S // E
H, HD = 16, 8
EPS = 1e-5
NEG = -1e30
TAKEN = -1.0


class Net:

    def __init__(self, nc, ctx, dram):
        self.nc, self.ctx, self.dram = nc, ctx, dram
        self.x = self.sb("x_tokens", [P, T, D])
        self.xnT = self.sb("normed_T", [P, T * P])
        self.xn = self.sb("normed_pair", [P, TPB, D])
        self.stats = self.sb("ln_stats", [P, T, 6])
        self.mv = self.sb("ln_mean_var", [P, T, 2])
        self.vareps = self.sb("ln_var_eps", [P, T])
        self.rstd = self.sb("ln_rstd", [P, T])
        self.minus_half = self.sb("minus_half", [P, T])
        self.ident = self.sb("ident", [P, P])
        self.identb = self.sb("ident_bf16", [P, P], BF16)
        self.scores = ctx.enter_context(nc.psum_tensor("banks0to3", [P, 2, 2, 512], FP32))
        later = [ctx.enter_context(nc.psum_tensor(f"bank{n}", [P, 512], FP32)) for n in range(4, 8)]
        self.bank = [self.scores[:, n // 2, n % 2, :] for n in range(4)] + [b[:, :] for b in later]
        self.bankb = [b.bitcast(BF16) for b in self.bank]
        self.logit = self.sb("router_logit", [P, T, E])
        self.prob = self.sb("router_prob", [P, T, E])
        self.rmax = self.sb("router_max", [P, T])
        self.rsum = self.sb("router_sum", [P, T])
        self.gate = self.sb("gate", [P, T, E])
        self.top8 = self.sb("top8", [P, T, 8])
        self.left = self.sb("probs_left", [P, T, E])
        self.best = self.sb("best8", [B * E, 8])
        self.hid = self.sb("hidden", [P, 2, 2 * FT, P])
        self.sil = self.sb("silu_gate", [P, 2, 4 * P])
        self.acc = self.sb("expert_sum", [P, 4, D])
        self.accb = self.sb("expert_sum_bf16", [P, 4, D], BF16)
        self.xload = self.sem("x_loaded")
        self.const = self.sem("constants_made")
        self.sems, self.counts = {}, {}
        self.weights_split = None
        self.ready = None

    def share(self, block, layout):
        views, at = {}, 0
        for name, (rows, columns, dt) in layout.items():
            words = columns // (2 if dt is BF16 else 1)
            view = block[0:rows, at:at + words]
            views[name] = view.bitcast(BF16) if dt is BF16 else view
            at += words
        return views

    def shared(self, name):
        if name not in self.sems:
            self.sems[name] = self.sem(name)
        return self.sems[name], self.counts.get(name, 0)

    def sb(self, name, shape, dt=FP32):
        return self.ctx.enter_context(self.nc.sbuf_tensor(name, shape, dt))

    def sb_twice(self, name, shape):
        with self.nc.sbuf_tensor(f"{name}_float32r", shape, FP32R) as rounded:
            pass
        return self.sb(name, shape), rounded

    def sem(self, name):
        return self.ctx.enter_context(self.nc.semaphore(name))


class Chain:

    def __init__(self, eng, sem, base=0):
        self.eng, self.sem, self.base, self.n = eng, sem, base, 0

    def __call__(self, ins):
        ins.then_inc(self.sem, 1)
        self.n += 1
        return self.base + self.n

    def then_wait(self, ins):
        self.eng.wait_ge(self.sem, self(ins))


class Tally:

    def __init__(self, net, name, per, turns=B):
        self.sem, self.base = net.shared(name)
        self.new = self.base == 0
        self.per = per
        net.counts[name] = self.base + turns * per

    def prime(self, eng):
        if self.new:
            eng.sem_inc(self.sem, 1)

    def at(self, n, k):
        return n * self.per + (self.base + k + 1)


def layernorm_stats(net, name):
    nc = net.nc
    own = net.sem(f"{name}_stats_chain")
    var_ready = net.sem(f"{name}_var_ready")
    rstd_ready = (net.sem(f"{name}_rstd_ready"), 1)

    def vector(dve):
        chain = Chain(dve, own)
        for t in range(T):
            ins = nc.vector.bn_stats(net.stats[:, t, :], net.x[:, t, :])
        chain.then_wait(ins)
        for t in range(T):
            ins = nc.vector.bn_aggr(net.mv[:, t, :], net.stats[:, t, :])
        chain.then_wait(ins)
        nc.vector.tensor_scalar_add(net.vareps[:, :], net.mv[:, :, 1], EPS).then_inc(var_ready, 1)

    def gpsimd(pool):
        pool.wait_ge(var_ready, 1)
        nc.gpsimd.tensor_tensor(net.rstd[:, :], net.vareps[:, :], net.minus_half[:, :],
                                ALU.pow).then_inc(rstd_ready[0], 1)

    return vector, gpsimd, rstd_ready


class Front:

    GROUP = 4

    def __init__(self, net, name, gate_w, loaded, split=False):
        self.net, self.gate_w, self.loaded, self.split = net, gate_w, loaded, split
        groups = T // self.GROUP
        self.stats_dve, self.stats_pool, self.rstd_ready = layernorm_stats(net, name)
        self.xn = Tally(net, "front_xn", groups, 1)
        self.xnT_psum = Tally(net, "front_xnT_psum", groups, 1)
        self.xnT = Tally(net, "front_xnT", groups, 1)
        self.logits = Tally(net, "front_logits", 1, 1)
        self.logit = Tally(net, "front_logit", 1, 1)
        self.exps = Tally(net, "front_exps", 1, 1)
        if split:
            self.lower = Tally(net, "front_lower", 1, 1)
        self.normed = net.hid[:, :, :, :].rearrange("p a f k -> p (a f) k")

    def vector(self, dve, chain, between=None):
        net, v = self.net, self.net.nc.vector
        self.stats_dve(dve)
        dve.wait_ge(*self.rstd_ready)
        for t in range(T):
            ins = normalise(net, self.normed[:, t, :], t)
            if t % self.GROUP == self.GROUP - 1:
                ins.then_inc(self.xn.sem, 1)
        if self.split:
            dve.wait_ge(self.xnT.sem, self.xnT.at(0, T // self.GROUP))
            v.tensor_tensor(net.xnT_lower, net.xnT[:, :], net.xnT_upper,
                            ALU.subtract).then_inc(self.lower.sem, 1)
            between(dve)
        dve.wait_ge(self.logits.sem, self.logits.at(0, 1))
        lg = net.bank[7][:, 0:T * E].rearrange("p (t e) -> p t e", e=E)
        chain.then_wait(v.reduce_max(net.rmax[:, :], lg, AX.X))
        v.tensor_tensor(net.logit[:, :, :], lg, net.rmax[:, :].unsqueeze(2).to_broadcast([P, T, E]),
                        ALU.subtract).then_inc(self.logit.sem, 1)
        dve.wait_ge(self.exps.sem, self.exps.at(0, 1))
        chain.then_wait(v.reduce_sum(net.rsum[:, :], net.prob[:, :, :], AX.X))
        chain.then_wait(v.reciprocal(net.rsum[:, :], net.rsum[:, :]))
        chain.then_wait(v.tensor_tensor(net.prob[:, :, :], net.prob[:, :, :],
                                        net.rsum[:, :].unsqueeze(2).to_broadcast([P, T, E]), ALU.mult))

    def scalar(self, act):
        net, nc = self.net, self.net.nc
        width = self.GROUP * P
        for g in range(T // self.GROUP):
            act.wait_ge(self.xnT_psum.sem, self.xnT_psum.at(0, g + 1))
            at = slice(g * width, (g + 1) * width)
            ins = nc.scalar.copy(net.xnT[:, at], net.bank[g])
            if self.split:
                ins = nc.scalar.copy(net.xnT_upper[:, at], net.bank[g])
            ins.then_inc(self.xnT.sem, 1)
        act.wait_ge(self.logit.sem, self.logit.at(0, 1))
        nc.scalar.activation(net.prob[:, :, :], net.logit[:, :, :], ACT.Exp).then_inc(self.exps.sem, 1)

    def tensor(self, pe):
        net, nc = self.net, self.net.nc
        groups = T // self.GROUP
        for g in range(groups + 1):
            if g < groups:
                pe.wait_ge(self.xn.sem, self.xn.at(0, g + 1))
                for q in range(self.GROUP):
                    ins = nc.tensor.transpose(net.bank[g][:, q * P:(q + 1) * P],
                                              self.normed[:, g * self.GROUP + q, :], net.ident[:, :])
                ins.then_inc(self.xnT_psum.sem, 1)
            if g == 0:
                pe.wait_ge(*self.loaded)
                continue
            pe.wait_ge(self.xnT.sem, self.xnT.at(0, g))
            for t in range((g - 1) * self.GROUP, g * self.GROUP):
                ins = nc.tensor.matmul(net.bank[7][:, t * E:(t + 1) * E], net.xnT[:, t * P:(t + 1) * P], self.gate_w,
                                       start=True, stop=True)
        ins.then_inc(self.logits.sem, 1)


def normalise(net, dst, t):
    at = slice(t, t + 1) if isinstance(t, int) else bass.ds(t, 1)
    return net.nc.vector.tensor_scalar(dst, net.x[:, at, :].rearrange("p a d -> p (a d)"), net.mv[:, at, 0],
                                       net.rstd[:, at], ALU.subtract, ALU.mult)


class ExpertChoice:

    def __init__(self, net, name, gate_w, w1, w2, loaded):
        self.net, self.w1, self.w2 = net, w1, w2
        self.before = net.ready
        self.front = Front(net, name, gate_w, loaded)
        once = 1
        self.router_steps = Tally(net, "choice_router_steps", 5 + 1 + 2 * (CAP // 8) + 4, once)
        self.probT_psum = Tally(net, "choice_probT_psum", 1, once)
        self.picked = Tally(net, "choice_picked", 1, once)
        self.turned = Tally(net, "choice_turned", 1, once)
        self.routed = Tally(net, "choice_routed", 1, once)
        pairs = B // 2
        self.prepared = Tally(net, "choice_prepared", 1, pairs)
        self.selector = Tally(net, "choice_selector", 1, pairs)
        self.gathered = Tally(net, "choice_gathered", 2, pairs)
        self.xgT = Tally(net, "choice_xgT", 2, pairs)
        self.bcast = Tally(net, "choice_bcast", E, pairs)
        self.spread = Tally(net, "choice_spread", E, pairs)
        self.up = Tally(net, "choice_up", E, pairs)
        self.hidden = Tally(net, "choice_hidden", E, pairs)
        self.down = Tally(net, "choice_down", E, pairs)
        self.ycopied = Tally(net, "choice_ycopied", E, pairs)
        self.combined = Tally(net, "choice_combined", E, pairs)
        self.summed = Tally(net, "choice_summed", E, pairs)
        self.added = Tally(net, "choice_added", 2, pairs)
        net.ready = (self.added.sem, self.added.at(pairs, 0))

    def turns(self, eng, prepare, experts):
        prepare(0)
        with eng.Fori(0, B // 2 - 1) as i:
            experts(i, True)
        experts(B // 2 - 1, False)


    def vector(self, dve):
        net, v = self.net, self.net.nc.vector
        if self.before:
            dve.wait_ge(*self.before)
        else:
            dve.wait_ge(net.xload, 16)
            dve.wait_ge(net.const, 4)
            dve.wait_ge(net.choice_const, 1)
        for t in (self.front.xn, self.front.logit, self.router_steps, self.picked, self.routed, self.prepared, self.selector,
                  self.spread, self.summed, self.added):
            t.prime(dve)
        chain = Chain(dve, self.router_steps.sem, self.router_steps.at(0, 0))
        self.front.vector(dve, chain)
        by_half = net.gate[:, :, :].rearrange("p t e -> p (t e)").rearrange("p (a n e) -> p n a e", a=TPB, n=B)
        chain.then_wait(v.tensor_copy(by_half, net.prob[:, :, :].rearrange("p (n a) e -> p n a e", a=TPB)))
        dve.wait_ge(self.probT_psum.sem, self.probT_psum.at(0, 1))
        chain.then_wait(v.tensor_copy(net.probT[:, :], net.bank[7][0:B * E, 256:512]))
        src = net.probT
        for r in range(CAP // 8):
            chain.then_wait(v.max(net.best[:, :], src[:, :]))
            chain.then_wait(v.match_replace(net.leftT[:, :], net.best[:, :], src[:, :], TAKEN))
            src = net.leftT
        chain(v.scalar_tensor_tensor(net.gateT[:, :], net.leftT[:, :], 0.0, net.probT[:, :], ALU.is_lt, ALU.mult))
        chain.then_wait(v.tensor_scalar(net.leftT[:, :], net.leftT[:, :], 0.0, None, ALU.is_lt))
        chain.then_wait(v.tensor_tensor_scan(net.probT[:, :], net.leftT[:, :], net.leftT[:, :], 0.0,
                                             ALU.add, ALU.max))
        chain.then_wait(v.tensor_tensor(net.posT[:, :], net.probT[:, :], net.leftT[:, :], ALU.mult))
        v.tensor_copy(net.posTb[:, :], net.posT[:, :]).then_inc(self.picked.sem, 1)
        dve.wait_ge(self.turned.sem, self.turned.at(0, 1))
        for k, dst in enumerate((net.gate, net.pos)):
            src = net.bank[7][:, k * T * E:(k + 1) * T * E].rearrange("p (a n e) -> p n a e", a=TPB, n=B)
            ins = v.tensor_copy(dst[:, :, :].rearrange("p (n a) e -> p n a e", a=TPB), src)
        ins.then_inc(self.routed.sem, 1)
        dve.wait_ge(self.routed.sem, self.routed.at(0, 1))
        assert chain.n == self.router_steps.per, chain.n

        def prepare_tile(i, q):
            t = i * 4 + q
            at = slice(t, t + 1) if isinstance(t, int) else bass.ds(t, 1)
            if q == 0:
                dve.wait_ge(self.gathered.sem, self.gathered.at(i, 0))
            normalise(net, net.xnq[:, q, :], t)
            ins = v.tensor_tensor(net.pick[:, q, :, :],
                                  net.pos[:, at, :].rearrange("p a e -> p (a e)").unsqueeze(2).to_broadcast([P, E, CAP]),
                                  net.numbers[:, :].unsqueeze(1).to_broadcast([P, E, CAP]), ALU.is_equal)
            if q == 3:
                ins.then_inc(self.prepared.sem, 1)

        def select(i):
            dve.wait_ge(self.bcast.sem, self.bcast.at(i, 0))
            at = slice(i, i + 1) if isinstance(i, int) else bass.ds(i, 1)
            v.tensor_copy(net.rowsel[:, :], net.rowsels[:, at, :].rearrange("p a m -> p (a m)")
                          ).then_inc(self.selector.sem, 1)

        def prepare(i):
            select(i)
            for q in range(4):
                prepare_tile(i, q)

        def spread(i, e):
            dve.wait_ge(self.bcast.sem, self.bcast.at(i, e + 1))
            dve.wait_ge(self.combined.sem, self.combined.at(i, max(e - 3, 0)))
            v.tensor_scalar(net.back[:, e % 4, :], net.bank[6 + e % 2][:, 0:S], net.number_col[:, :], None,
                            ALU.is_equal).then_inc(self.spread.sem, 1)

        def add(i, e):
            dve.wait_ge(self.combined.sem, self.combined.at(i, e + 1))
            if e:
                dve.wait_ge(self.summed.sem, self.summed.at(i, e))
            for q in range(4):
                t = i * 4 + q
                at = slice(t, t + 1) if isinstance(t, int) else bass.ds(t, 1)
                z = net.bank[4 + q // 2][:, (q % 2) * D:(q % 2 + 1) * D]
                if e == 0:
                    ins = v.tensor_scalar(net.acc[:, q, :], z, net.gate[:, at, e], None, ALU.mult)
                else:
                    ins = v.scalar_tensor_tensor(net.acc[:, q, :], z, net.gate[:, at, e], net.acc[:, q, :],
                                                 ALU.mult, ALU.add)
            ins.then_inc(self.summed.sem, 1)

        def experts(i, more):
            for e in range(E + 2):
                if e == E and more:
                    select(i + 1)
                if e < E:
                    spread(i, e)
                if e >= 2:
                    add(i, e - 2)
                if more and 2 <= e < 6:
                    prepare_tile(i + 1, e - 2)
            dve.wait_ge(self.summed.sem, self.summed.at(i, E))
            v.tensor_copy(net.accb[:, :, :], net.acc[:, :, :]).then_inc(self.added.sem, 1)
            dve.wait_ge(self.added.sem, self.added.at(i, 1))
            at = slice(i * 4, i * 4 + 4) if isinstance(i, int) else bass.ds(i * 4, 4)
            v.scalar_tensor_tensor(net.x[:, at, :], net.accb[:, :, :], 0.5, net.x[:, at, :], ALU.mult,
                                   ALU.add).then_inc(self.added.sem, 1)

        self.turns(dve, prepare, experts)

    def gpsimd(self, pool):
        self.front.stats_pool(pool)


    def scalar(self, act):
        net, nc = self.net, self.net.nc
        for t in (self.front.xnT, self.front.exps, self.xgT, self.hidden, self.ycopied):
            t.prime(act)
        self.front.scalar(act)

        def gathered(i):
            for b in range(2):
                act.wait_ge(self.gathered.sem, self.gathered.at(i, b + 1))
                nc.scalar.copy(net.xgT[:, :, b, :], net.bank[6 + b].rearrange("p (e k) -> p e k", e=E)
                               ).then_inc(self.xgT.sem, 1)

        def gelu(i, e):
            act.wait_ge(self.up.sem, self.up.at(i, e + 1))
            act.wait_ge(self.down.sem, self.down.at(i, max(e - 1, 0)))
            nc.scalar.activation(net.hid[:, e % 2, 0:4, :].rearrange("p f k -> p (f k)"), net.bank[e % 2],
                                 ACT.Gelu_apprx_tanh).then_inc(self.hidden.sem, 1)

        def results(i, e):
            act.wait_ge(self.down.sem, self.down.at(i, e + 1))
            act.wait_ge(self.combined.sem, self.combined.at(i, max(e - 1, 0)))
            nc.scalar.copy(net.y[:, e % 2, :], net.bank[2 + e % 2][:, 0:D]).then_inc(self.ycopied.sem, 1)

        def experts(i, more):
            for e in range(E + 1):
                if e < E:
                    gelu(i, e)
                elif more:
                    gathered(i + 1)
                if e >= 1:
                    results(i, e - 1)

        self.turns(act, gathered, experts)


    def tensor(self, pe):
        net, nc, mm = self.net, self.net.nc, self.net.nc.tensor.matmul
        if not self.before:
            pe.wait_ge(net.const, 4)
            pe.wait_ge(net.choice_const, 1)
        for t in (self.front.xnT_psum, self.front.logits, self.probT_psum, self.turned, self.gathered, self.bcast, self.up,
                  self.down, self.combined):
            t.prime(pe)
        self.front.tensor(pe)
        pe.wait_ge(self.router_steps.sem, self.router_steps.at(0, 5))
        pr = net.gate[:, :, :].rearrange("p t e -> p (t e)")
        for tt in range(TPB):
            ins = nc.tensor.transpose(net.bank[7][0:B * E, 256 + tt * P:256 + (tt + 1) * P],
                                      pr[:, tt * B * E:(tt + 1) * B * E], net.ident[:, :])
        ins.then_inc(self.probT_psum.sem, 1)
        pe.wait_ge(self.picked.sem, self.picked.at(0, 1))
        for k, src in enumerate((net.gateT, net.posT)):
            for tt in range(TPB):
                ins = nc.tensor.transpose(net.bank[7][:, (k * TPB + tt) * B * E:(k * TPB + tt + 1) * B * E],
                                          src[:, tt * P:(tt + 1) * P], net.ident[0:B * E, 0:B * E])
        ins.then_inc(self.turned.sem, 1)
        pe.wait_ge(self.routed.sem, self.routed.at(0, 1))

        def gather(i):
            pe.wait_ge(self.prepared.sem, self.prepared.at(i, 1))
            pe.wait_ge(self.spread.sem, self.spread.at(i, 0))
            for b in range(2):
                for tt in range(TPB):
                    ins = mm(net.bank[6 + b], net.xnq[:, 2 * b + tt, :],
                             net.pick[:, 2 * b + tt, :, :].rearrange("p e k -> p (e k)"),
                             start=(tt == 0), stop=(tt == TPB - 1))
                ins.then_inc(self.gathered.sem, 1)

        def broadcast(i, e):
            if e == 0:
                pe.wait_ge(self.selector.sem, self.selector.at(i, 1))
                pe.wait_ge(self.xgT.sem, self.xgT.at(i, 2))
            pe.wait_ge(self.spread.sem, self.spread.at(i, max(e - 1, 0)))
            mm(net.bank[6 + e % 2][:, 0:S], net.rowsel[:, e * P:(e + 1) * P], net.posTb[:, :], start=True,
               stop=True).then_inc(self.bcast.sem, 1)

        def up(i, e):
            pe.wait_ge(self.hidden.sem, self.hidden.at(i, max(e - 1, 0)))
            for f in range(FT):
                ins = mm(net.bank[e % 2][:, f * P:(f + 1) * P], self.w1[:, e, f * P:(f + 1) * P],
                         net.xgT[:, e, :, :].rearrange("p b k -> p (b k)"), start=True, stop=True)
            ins.then_inc(self.up.sem, 1)

        def down(i, e):
            pe.wait_ge(self.hidden.sem, self.hidden.at(i, e + 1))
            pe.wait_ge(self.ycopied.sem, self.ycopied.at(i, max(e - 1, 0)))
            for f in range(FT):
                ins = mm(net.bank[2 + e % 2][:, 0:D], net.hid[:, e % 2, f, :], self.w2[:, e, f, :],
                         start=(f == 0), stop=(f == FT - 1))
            ins.then_inc(self.down.sem, 1)

        def combine(i, e):
            pe.wait_ge(self.ycopied.sem, self.ycopied.at(i, e + 1))
            pe.wait_ge(self.spread.sem, self.spread.at(i, e + 1))
            pe.wait_ge(self.summed.sem, self.summed.at(i, e))
            for tt in range(TPB):
                for b in range(2):
                    rows = slice(CAP * b, CAP * (b + 1))
                    ins = mm(net.bank[4 + b][:, tt * D:(tt + 1) * D], net.back[rows, e % 4, tt * P:(tt + 1) * P],
                             net.y[rows, e % 2, :], start=True, stop=True)
            ins.then_inc(self.combined.sem, 1)

        def experts(i, more):
            for e in range(E + 2):
                if e < E:
                    broadcast(i, e)
                    up(i, e)
                elif e == E and more:
                    gather(i + 1)
                if 1 <= e <= E:
                    down(i, e - 1)
                if e >= 2:
                    combine(i, e - 2)

        self.turns(pe, gather, experts)


def choice_buffers(net):
    block, upper = net.sb_twice("choice_only", [P, CHOICE_WORDS])
    rows, pairs = B * E, B // 2
    v = net.share(block, dict(row_selectors=(rows, pairs * E * P, BF16), row_selector=(rows, E * P, BF16),
                              pick_number_T_bf16=(rows, S, BF16), pick_number_T=(rows, S, FP32), prob_T=(rows, S, FP32),
                              left_T=(rows, S, FP32), gate_T=(rows, S, FP32), pick_number=(P, T * E, FP32),
                              pick_results=(P, 2 * D, FP32)))
    net.shared_upper = upper[:, 0:2 * F]
    net.rowsels = v["row_selectors"].rearrange("r (i m) -> r i m", i=pairs)
    net.rowsel, net.posTb, net.posT = v["row_selector"], v["pick_number_T_bf16"], v["pick_number_T"]
    net.probT, net.leftT, net.gateT = v["prob_T"], v["left_T"], v["gate_T"]
    net.pos = v["pick_number"].rearrange("p (t e) -> p t e", e=E)
    net.y = v["pick_results"].rearrange("p (a d) -> p a d", a=2)
    net.xnq = net.prod2[:, :, :, :].rearrange("p a b d -> p (a b) d")
    net.pick = net.kv2[:, :, :, :, :].rearrange("p a b c d -> p (a b c d)").rearrange("p (q e k) -> p q e k", q=4, e=E)
    kT = net.kT[:, :, :, :, :].rearrange("p a t u k -> p a (t u k)").bitcast(FP32)
    net.back = kT[:, 0].rearrange("p (a k) -> p a k", a=4)
    net.xgT = kT[:, 1].rearrange("p (e b k) -> p e b k", e=E, b=2)
    net.numbers = net.sb("numbers_row", [P, CAP])
    net.number_col = net.sb("numbers_column", [P, 1])
    net.choice_steps = net.sem("choice_constants_steps")
    net.choice_const = net.sem("choice_constants_ready")


def choice_constants(net, pool):
    g = net.nc.gpsimd
    g.iota(net.numbers[:, :], [[1, CAP]], base=1, channel_multiplier=0, allow_small_or_imprecise_dtypes=True)
    g.memset(net.rowsels[:, :, :], 1.0).then_inc(net.choice_steps, 1)
    g.iota(net.number_col[:, :], [[0, 1]], base=1, channel_multiplier=1,
           allow_small_or_imprecise_dtypes=True).then_inc(net.choice_steps, 1)
    pool.wait_ge(net.choice_steps, 2)
    g.tensor_scalar(net.number_col[CAP:P, :], net.number_col[CAP:P, :], float(-CAP), None,
                    ALU.add).then_inc(net.choice_steps, 1)
    pool.wait_ge(net.choice_steps, 3)
    view = net.rowsels[:, :, :].rearrange("r i (e b k) -> r (i e) b k", e=E, b=2)
    for i in range(B // 2):
        part = view[:, i * E:(i + 1) * E, :, :]
        ins = g.affine_select(out=part, in_=part, compare_op=ALU.is_equal, fill=0.0, base=-2 * E * i,
                              pattern=[[-1, E], [-E, 2], [0, CAP]], channel_multiplier=1)
    ins.then_inc(net.choice_const, 1)


class TokenChoice:

    def __init__(self, net, name, gate_w, whole, lower, upper, loaded):
        self.net, self.loaded = net, loaded
        (self.w1, self.w3, self.w2), self.lower = whole, lower
        self.uppers = upper
        self.before = net.ready
        self.front = Front(net, name, gate_w, loaded, split=True)
        self.splits = net.weights_split is None
        if self.splits:
            net.weights_split = net.sem("weights_lower_parts")
        self.weights_split = net.weights_split
        self.weights_upper = Tally(net, "weights_upper", 2 * NE, 1) if self.splits else None
        self.router_steps = Tally(net, "tokens_router_steps", 8, 1)
        self.gates = Tally(net, "tokens_gates", 1, 1)
        turns = B // 2
        self.up = Tally(net, "tokens_up", 2 * STEPS, turns)
        self.act = Tally(net, "tokens_silu", 2 * STEPS, turns)
        self.hidden = Tally(net, "tokens_hidden", 2 * STEPS, turns)
        self.down = Tally(net, "tokens_down", STEPS, turns)
        self.added = Tally(net, "tokens_added", STEPS, turns)
        net.ready = (self.added.sem, self.added.at(turns, 0))

    def upper(self, i, e):
        routed, shared = self.uppers
        return routed[i][:, e, :] if e < E else shared[:, i * F:(i + 1) * F]

    def vector(self, dve):
        net = self.net
        if self.before:
            dve.wait_ge(*self.before)
        else:
            dve.wait_ge(net.xload, 16)
            dve.wait_ge(net.const, 4)
        for t in (self.front.xn, self.front.lower, self.front.logit, self.router_steps, self.gates, self.hidden,
                  self.added):
            t.prime(dve)
        chain = Chain(dve, self.router_steps.sem, self.router_steps.at(0, 0))

        def lower_weights(dve):
            if self.splits:
                for k in range(2 * NE):
                    whole = (self.w1, self.w3)[k % 2][:, k // 2, :]
                    dve.wait_ge(self.weights_upper.sem, self.weights_upper.at(0, k + 1))
                    ins = net.nc.vector.tensor_tensor(self.lower[k % 2][:, k // 2, :], whole, self.upper(k % 2, k // 2),
                                                      ALU.subtract)
                ins.then_inc(self.weights_split, 1)

        self.front.vector(dve, chain, lower_weights)
        self.token_choice(dve, chain)
        assert chain.n == self.router_steps.per, chain.n
        self.main_vector(dve)

    def token_choice(self, dve, chain):
        net, nc = self.net, self.net.nc
        for t in range(T):
            ins = nc.vector.max(net.top8[:, t, :], net.prob[:, t, :])
        chain.then_wait(ins)
        chain.then_wait(nc.vector.memset(net.top8[:, :, 2:8], -3.0))
        for t in range(T):
            ins = nc.vector.match_replace(net.left[:, t, :], net.top8[:, t, :], net.prob[:, t, :], TAKEN)
        chain.then_wait(ins)
        chain.then_wait(nc.vector.tensor_scalar(net.left[:, :, :], net.left[:, :, :], 0.0, 0.25, ALU.is_lt, ALU.mult))
        nc.vector.tensor_tensor(net.gate[:, :, :], net.left[:, :, :], net.prob[:, :, :],
                                ALU.mult).then_inc(self.gates.sem, 1)

    def main_vector(self, dve):
        net, nc = self.net, self.net.nc
        dve.wait_ge(self.gates.sem, self.gates.at(0, 1))

        def add(i, step):
            dve.wait_ge(self.down.sem, self.down.at(i, step + 1))
            dve.wait_ge(self.added.sem, self.added.at(i, step))
            e = step % NE
            for tt in range(TPB):
                t = (i * 2 + step // NE) * TPB + tt
                at = slice(t, t + 1) if isinstance(t, int) else bass.ds(t, 1)
                acc = net.x[:, at, :].rearrange("p a d -> p (a d)")
                factor = SHARED if e == E else net.gate[:, at, e]
                ins = nc.vector.scalar_tensor_tensor(acc, net.bank[4 + step % 2][:, tt * D:(tt + 1) * D], factor, acc,
                                                     ALU.mult, ALU.add)
            ins.then_inc(self.added.sem, 1)

        def gated(i, step, half):
            dve.wait_ge(self.act.sem, self.act.at(i, 2 * step + half + 1))
            if step >= 2:
                dve.wait_ge(self.down.sem, self.down.at(i, step - 1))
            nc.vector.tensor_tensor(
                net.hid[:, step % 2, 4 * half:4 * half + 4, :].rearrange("p a b -> p (a b)"),
                net.sil[:, half, :], net.bank[2 + half][:, :], ALU.mult).then_inc(self.hidden.sem, 1)

        for step in range(2):
            for half in range(2):
                gated(0, step, half)

        def turn(i, last):
            for step in range(2, STEPS if last else STEPS + 2):
                gated(i, step, 0)
                add(i, step - 2)
                gated(i, step, 1)

        with dve.Fori(0, B // 2 - 1) as i:
            turn(i, False)
        turn(B // 2 - 1, True)
        add(B // 2 - 1, STEPS - 2)
        add(B // 2 - 1, STEPS - 1)

    def gpsimd(self, pool):
        self.front.stats_pool(pool)

    def scalar(self, act):
        net, nc = self.net, self.net.nc
        for t in (self.front.xnT, self.front.exps, self.act):
            t.prime(act)
        if self.splits:
            self.weights_upper.prime(act)
            act.wait_ge(*self.loaded)
            act.wait_ge(*(self.before or (net.choice_const, 1)))
            for k in range(2 * NE):
                nc.scalar.copy(self.upper(k % 2, k // 2), (self.w1, self.w3)[k % 2][:, k // 2, :]
                               ).then_inc(self.weights_upper.sem, 1)
        self.front.scalar(act)
        with act.Fori(0, B // 2) as i:
            for k in range(2 * STEPS):
                act.wait_ge(self.up.sem, self.up.at(i, k + 1))
                act.wait_ge(self.hidden.sem, self.hidden.at(i, max(k - 1, 0)))
                nc.scalar.activation(net.sil[:, k % 2, :], net.bank[k % 2][:, :], ACT.Silu).then_inc(self.act.sem, 1)

    def tensor(self, pe):
        net, nc = self.net, self.net.nc
        if not self.before:
            pe.wait_ge(net.const, 4)
        for t in (self.front.xnT_psum, self.front.logits, self.up, self.down):
            t.prime(pe)
        self.front.tensor(pe)
        pe.wait_ge(self.front.lower.sem, self.front.lower.at(0, 1))
        pe.wait_ge(self.weights_split, 1)

        def product(out, left, right):
            nc.tensor.matmul(out, left[0], right[0], start=True, stop=False)
            nc.tensor.matmul(out, left[0], right[1], start=False, stop=False)
            return nc.tensor.matmul(out, left[1], right[0], start=False, stop=True)

        def up(i, step):
            n, e = i * 2 + step // NE, step % NE
            at = slice(n * S, (n + 1) * S) if isinstance(n, int) else bass.ds(n * S, S)
            x = [part[:, at] for part in (net.xnT_upper, net.xnT_lower)]
            for half in range(2):
                if step >= 1:
                    pe.wait_ge(self.hidden.sem, self.hidden.at(i, 2 * step + half - 1))
                for w in range(2):
                    for f in range(2):
                        c = slice((2 * half + f) * P, (2 * half + f + 1) * P)
                        ins = product(net.bank[2 * w + half][:, f * S:(f + 1) * S],
                                      (self.upper(w, e)[:, c], self.lower[w][:, e, c]), x)
                ins.then_inc(self.up.sem, 1)

        def down(i, step):
            pe.wait_ge(self.added.sem, self.added.at(i, max(step - 1, 0)))
            hid = net.hid[:, step % 2, :, :].rearrange("p (f a) t -> p f a t", a=TPB)
            for half in range(2):
                pe.wait_ge(self.hidden.sem, self.hidden.at(i, 2 * step + half + 1))
                for tt in range(TPB):
                    for f in (2 * half, 2 * half + 1):
                        ins = nc.tensor.matmul(net.bank[4 + step % 2][:, tt * D:(tt + 1) * D], hid[:, f, tt, :],
                                               self.w2[:, step % NE, f, :], start=(tt == 0 and f == 0),
                                               stop=(tt == TPB - 1 and f == FT - 1), skip_group_check=True)
            ins.then_inc(self.down.sem, 1)

        def turn(i, last):
            for step in range(STEPS):
                if not (last and step == STEPS - 1):
                    up(i, step + 1)
                down(i, step)

        up(0, 0)
        with pe.Fori(0, B // 2 - 1) as i:
            turn(i, False)
        turn(B // 2 - 1, True)


VS = 32
ST = 64
SPLIT_Q = ((0, 3), (3, 2), (5, 1))
SPLIT_K = ((0, 0, 2, 3), (0, 5, 1, 1), (1, 1, 2, 3), (2, 2, 1, 1))
SCALE = float(HD) ** -0.5


class Attention:

    def __init__(self, net, name, rel, w):
        self.net, self.name, self.rel, self.w = net, name, rel, w
        self.before = net.ready
        self.pairs = ((0, 0), (1, 0), (1, 1)) if rel else ((0, 0), (1, 1))
        self.units = [(qt, kt, u) for qt, kt in self.pairs for u in range(2)]
        nu = len(self.units)
        self.units_first = sum(1 for qt, _, _ in self.units if qt == 0)
        self.stats_dve, self.stats_pool, self.rstd_ready = layernorm_stats(net, name)
        self.xn = Tally(net, "attn_xn", 1)
        self.xnT_psum = Tally(net, "attn_xnT_psum", 1)
        self.xnT = Tally(net, "attn_xnT", 1)
        self.proj = Tally(net, "attn_proj", 2)
        self.proj_read = Tally(net, "attn_proj_read", 2)
        self.parts = Tally(net, "attn_parts", 1)
        self.stacks = Tally(net, "attn_stacks", 1)
        self.stackT = Tally(net, "attn_stackT", 4)
        self.stackTm = Tally(net, "attn_stackTm", 2)
        self.qkT = Tally(net, "attn_qkT", 4)
        self.a_scored = Tally(net, "attn_a_scored", nu)
        self.amax = Tally(net, "attn_amax", nu)
        self.mparts = Tally(net, "attn_mparts", 1)
        self.qTb = Tally(net, "attn_qTb", 2)
        self.b_scored = Tally(net, "attn_b_scored", nu)
        self.exps = Tally(net, "attn_exps", nu)
        self.pv = Tally(net, "attn_pv", nu)
        self.special = Tally(net, "attn_special", 1)
        self.pspecial = Tally(net, "attn_pspecial", 1)
        self.attended = Tally(net, "attn_attended", 2)
        self.oT_psum = Tally(net, "attn_oT_psum", 1)
        self.oT = Tally(net, "attn_oT", 1)
        self.y = Tally(net, "attn_y", 1)
        self.added = Tally(net, "attn_added", 1)
        self.front_steps = Tally(net, "attn_front_steps", 13 if rel else 6)
        self.max_steps = Tally(net, "attn_max_steps", 8 if rel else 6)
        self.back_steps = Tally(net, "attn_back_steps", 9 if rel else 5)
        self.vready = Tally(net, "attn_vready", 1)
        self.pvT = Tally(net, "attn_pvT", 2)
        self.pv_tokens = Tally(net, "attn_pv_tokens", 2)
        net.ready = (self.added.sem, self.added.at(B, 0))

    def permute(self, copy, dst, src, back=False):
        if self.rel:
            return copy(dst[:, 0:S], src[:, 0:S])
        for tt in range(TPB):
            runs = ((slice(tt * P, tt * P + 120), slice(tt * 120, tt * 120 + 120)),
                    (slice(tt * P + 120, tt * P + 128), slice(240 + tt, 255 + tt, 2)))
            for patched, natural in runs:
                to, fro = (natural, patched) if back else (patched, natural)
                ins = copy(dst[:, to], src[:, fro])
        return ins

    def turns(self, eng, first, step):
        first()
        with eng.Fori(0, B // 2 - 1) as i:
            step(i * 2, 0, True, True)
            step(i * 2 + 1, 1, True, True)
        step(B - 2, 0, True, False)
        step(B - 1, 1, False, False)


    def vector(self, dve):
        net, v = self.net, self.net.nc.vector
        dve.wait_ge(*self.before) if self.before else dve.wait_ge(net.xload, 16)
        for t in (self.xn, self.proj_read, self.parts, self.stacks, self.amax, self.mparts, self.special, self.attended,
                  self.added, self.vready, self.front_steps, self.max_steps, self.back_steps):
            t.prime(dve)
        self.stats_dve(dve)
        dve.wait_ge(*self.rstd_ready)
        dve.wait_ge(net.att_const, 1)

        def normalise(n):
            dve.wait_ge(self.xnT_psum.sem, self.xnT_psum.at(n, 0))
            for tt in range(TPB):
                t = n * TPB + tt
                at = slice(t, t + 1) if isinstance(t, int) else bass.ds(t, 1)
                ins = v.tensor_scalar(net.xn[:, tt, :], net.x[:, at, :].rearrange("p a d -> p (a d)"),
                                      net.mv[:, at, 0], net.rstd[:, at], ALU.subtract, ALU.mult)
            ins.then_inc(self.xn.sem, 1)

        def project(n, b, tt, chain):
            dve.wait_ge(self.proj.sem, self.proj.at(n, tt + 1))
            main, shifted = net.bank[4], net.bank[5]
            if self.rel:
                chain(v.tensor_tensor(net.qk[:, tt, :], main[:, 0:2 * D], net.add_far[:, 0:2 * D], ALU.add))
                chain(v.tensor_tensor(net.v[:, b, tt, :], main[:, 2 * D:3 * D], net.add_far[:, 2 * D:3 * D], ALU.add))
                chain(v.tensor_tensor(net.kv2[:, b, tt, 0, :], main[:, D:3 * D], net.add_self[:, :], ALU.add))
                v.tensor_tensor(net.kv2[:, b, tt, 1, :], shifted[:, 0:2 * D], net.add_prev[:, :],
                                ALU.add).then_inc(self.proj_read.sem, 1)
            else:
                chain(v.tensor_copy(net.qk[:, tt, :], main[:, 0:2 * D]))
                v.tensor_copy(net.v[:, b, tt, :], main[:, 2 * D:3 * D]).then_inc(self.proj_read.sem, 1)

        def split(n, b, chain, between=lambda: None, then=lambda: None):
            dve.wait_ge(self.proj_read.sem, self.proj_read.at(n, 2))
            chain.then_wait(v.tensor_copy(net.part[:, 0], net.qk[:, :, :]))
            chain.then_wait(v.tensor_tensor(net.rest[:, :, :], net.qk[:, :, :], net.part[:, 0], ALU.subtract))
            between()
            chain.then_wait(v.tensor_copy(net.part[:, 1], net.rest[:, :, :]))
            chain.then_wait(v.tensor_tensor(net.rest[:, :, :], net.rest[:, :, :], net.part[:, 1], ALU.subtract))
            v.tensor_copy(net.part[:, 2], net.rest[:, :, :]).then_inc(self.parts.sem, 1)
            then()
            dve.wait_ge(self.parts.sem, self.parts.at(n, 1))
            v.memset(net.qs[:, b, :, :, 48:51], 0.0)
            for tt in range(TPB):
                slots = net.qs[:, b, tt, :, 0:48].rearrange("p h (s d) -> p h s d", d=HD)
                for i, (first, many) in enumerate(SPLIT_Q):
                    q = net.part[:, i, tt, 0:D].rearrange("p (h d) -> p h d", d=HD).unsqueeze(2)
                    v.tensor_copy(slots[:, :, first:first + many, :], q.to_broadcast([P, H, many, HD]))
                slots = net.ks[:, tt, :, 0:48].rearrange("p h (s d) -> p h s d", d=HD)
                for i, first, many, step in SPLIT_K:
                    k = net.part[:, i, tt, D:2 * D].rearrange("p (h d) -> p h d", d=HD).unsqueeze(2)
                    ins = v.tensor_copy(slots[:, :, first:first + (many - 1) * step + 1:step, :],
                                        k.to_broadcast([P, H, many, HD]))
            ins.then_inc(self.stacks.sem, 1)

        def special_scores(n, b, chain):
            if not self.rel:
                return
            sp = net.sp[:, b]
            for tt in range(TPB):
                ins = v.tensor_tensor(net.prod[:, tt, :, :], net.kv2[:, b, tt, :, 0:D],
                                      net.qk[:, tt, 0:D].unsqueeze(1).to_broadcast([P, 2, D]), ALU.mult)
            chain.then_wait(ins)
            chain.then_wait(v.reduce_sum(
                sp.rearrange("p a b h -> p (a b h)"),
                net.prod[:, :, :, :].rearrange("p a b (h d) -> p (a b h) d", d=HD), AX.X))
            chain.then_wait(v.tensor_scalar(sp[:, 0, 1, :], sp[:, 0, 1, :], net.first_row[:, :], None, ALU.add))

        def special_values(n, b, chain):
            sp = net.sp[:, b]
            dve.wait_ge(self.pspecial.sem, self.pspecial.at(n, 1))
            if self.rel:
                for tt in range(TPB):
                    v2 = net.kv2[:, b, tt, :, D:2 * D].rearrange("p b (h d) -> p b h d", d=HD)
                    ins = v.tensor_tensor(net.prod2[:, tt, :, :].rearrange("p b (h d) -> p b h d", d=HD), v2,
                                          sp[:, tt, :, :].unsqueeze(3).to_broadcast([P, 2, H, HD]), ALU.mult)
                chain.then_wait(ins)
                chain.then_wait(v.tensor_tensor(net.prod2[:, :, 0, :], net.prod2[:, :, 0, :], net.prod2[:, :, 1, :],
                                                ALU.add))
                chain.then_wait(v.tensor_tensor(net.spsum[:, :, :], sp[:, :, 0, :], sp[:, :, 1, :], ALU.add))
            else:
                chain.then_wait(v.tensor_scalar(net.spsum[:, :, :], sp[:, :, 0, :], 12.0, None, ALU.mult))

        def largest(n, a):
            qt, kt, u = self.units[a]
            dve.wait_ge(self.a_scored.sem, self.a_scored.at(n, a + 1))
            out = net.mx[:, int(kt != qt), qt, :].rearrange("p (j r) -> p r j", r=2)[:, :, 4 * u:4 * u + 4]
            v.reduce_max(out, net.scores[:, 0].rearrange("p r (j k) -> p r j k", j=4), AX.X).then_inc(self.amax.sem, 1)

        def maximum(n, b, chain):
            dve.wait_ge(self.amax.sem, self.amax.at(n, len(self.units)))
            m = net.mx[:, 0, :, :]
            sp = net.sp[:, b]
            if self.rel:
                chain.then_wait(v.tensor_tensor(m, m, sp[:, :, 0, :], ALU.max))
                chain.then_wait(v.tensor_tensor(m, m, sp[:, :, 1, :], ALU.max))
                chain.then_wait(v.tensor_tensor(net.mx[:, 0, 1, :], net.mx[:, 0, 1, :], net.mx[:, 1, 1, :], ALU.max))
            else:
                chain.then_wait(v.tensor_scalar(m, m, net.short_row[:, :], None, ALU.max))
            chain.then_wait(v.tensor_scalar(net.mneg[:, :, :], m, -1.0, None, ALU.mult))
            mrow = [net.qs[:, b, :, :, 48 + i] for i in range(3)]
            chain.then_wait(v.tensor_copy(mrow[0], net.mneg[:, :, :]))
            chain.then_wait(v.tensor_tensor(net.mrest[:, :, :], net.mneg[:, :, :], mrow[0], ALU.subtract))
            chain.then_wait(v.tensor_copy(mrow[1], net.mrest[:, :, :]))
            chain.then_wait(v.tensor_tensor(net.mrest[:, :, :], net.mrest[:, :, :], mrow[1], ALU.subtract))
            v.tensor_copy(mrow[2], net.mrest[:, :, :]).then_inc(self.mparts.sem, 1)
            if self.rel:
                ins = v.tensor_tensor(sp, sp, net.mneg[:, :, :].unsqueeze(2).to_broadcast([P, TPB, 2, H]), ALU.add)
            else:
                ins = v.tensor_scalar(sp[:, :, 0, :], net.mneg[:, :, :], net.short_row[:, :], None, ALU.add)
            ins.then_inc(self.special.sem, 1)

        def finish(n, qt, chain):
            dve.wait_ge(self.pv_tokens.sem, self.pv_tokens.at(n, qt + 1))
            pv = net.bank[6 + qt].rearrange("p (h s) -> p h s", s=VS)
            den = net.den[:, qt, :]
            chain.then_wait(v.tensor_tensor(den, pv[:, :, HD], net.spsum[:, qt, :], ALU.add))
            chain.then_wait(v.reciprocal(den, den))
            o = net.att[:, qt, :].rearrange("p (h d) -> p h d", d=HD)
            src = pv[:, :, 0:HD]
            if self.rel:
                chain.then_wait(v.tensor_tensor(o, src, net.prod2[:, qt, 0, :].rearrange("p (h d) -> p h d", d=HD),
                                                ALU.add))
                src = o
            v.tensor_tensor(o, src, den.unsqueeze(2).to_broadcast([P, H, HD]),
                            ALU.mult).then_inc(self.attended.sem, 1)

        def add(n):
            dve.wait_ge(self.y.sem, self.y.at(n, 1))
            at = slice(n * TPB, (n + 1) * TPB) if isinstance(n, int) else bass.ds(n * TPB, TPB)
            xt = net.x[:, at, :]
            v.tensor_tensor(xt, net.bank[7][:, 0:S].rearrange("p (a d) -> p a d", a=TPB), xt,
                            ALU.add).then_inc(self.added.sem, 1)

        def values(n, b):
            if isinstance(n, int) and n == 0:
                ins = v.tensor_copy(net.vaug[:, :, :, 0:HD],
                                    net.v[:, b].rearrange("p t (h d) -> p t h d", d=HD))
            else:
                dve.wait_ge(self.pv.sem, self.pv.at(n, 0))
                ins = v.tensor_copy(net.vaug[:, :, :, 0:HD],
                                    net.v[:, b].rearrange("p t (h d) -> p t h d", d=HD))
            ins.then_inc(self.vready.sem, 1)

        def chain_of(tally, n):
            return Chain(dve, tally.sem, tally.at(n, 0))

        def first():
            normalise(0)
            front = chain_of(self.front_steps, 0)
            for tt in range(TPB):
                project(0, 0, tt, front)
            split(0, 0, front)
            special_scores(0, 0, front)
            assert front.n == self.front_steps.per, front.n
            normalise(1)
            project_and_maximise(0, 0)
            values(0, 0)

        def project_and_maximise(n, b, with_max=True, with_front=True):
            most = len(self.units)
            if with_front:
                front = chain_of(self.front_steps, n + 1)
            maxima = iter(range(most))

            def some(many):
                for _ in range(many if with_max else 0):
                    largest(n, next(maxima))

            some(1)
            if with_front:
                project(n + 1, 1 - b, 0, front)
            some(1)
            if with_front:
                project(n + 1, 1 - b, 1, front)
                split(n + 1, 1 - b, front, lambda: some(1), lambda: some(int(most > 4)))
                some(1)
                special_scores(n + 1, 1 - b, front)
                assert front.n == self.front_steps.per, front.n
            for a in maxima if with_max else ():
                largest(n, a)
            if with_max:
                longest = chain_of(self.max_steps, n)
                maximum(n, b, longest)
                assert longest.n == self.max_steps.per, longest.n

        def step(n, b, with_max, with_front):
            back = chain_of(self.back_steps, n)
            if with_front:
                normalise(n + 2)
            special_values(n, b, back)
            project_and_maximise(n + 1, 1 - b, with_max, with_front)
            finish(n, 0, back)
            finish(n, 1, back)
            assert back.n == self.back_steps.per, back.n
            if with_max:
                values(n + 1, 1 - b)
            add(n)

        self.turns(dve, first, step)


    def gpsimd(self, pool):
        self.stats_pool(pool)


    def scalar(self, act):
        net, nc = self.net, self.net.nc
        for t in (self.xnT, self.qkT, self.qTb, self.exps, self.pspecial, self.pvT, self.oT):
            t.prime(act)

        def normed(n):
            act.wait_ge(self.xnT_psum.sem, self.xnT_psum.at(n, 1))
            self.permute(nc.scalar.copy, net.xnTb[:, 1:1 + S], net.bank[4][:, 0:S]).then_inc(self.xnT.sem, 1)

        def stacked(n, b, groups):
            for g in groups:
                dst = (net.qT[:, 0], net.kT[:, b, 0], net.qT[:, 1], net.kT[:, b, 1])[g]
                act.wait_ge(self.stackT.sem, self.stackT.at(n, g + 1))
                nc.scalar.copy(dst.rearrange("p j t -> p (j t)"), net.bankb[4 + g % 2]).then_inc(self.qkT.sem, 1)

        def shifted_queries(n):
            for tt in range(TPB):
                act.wait_ge(self.stackTm.sem, self.stackTm.at(n, tt + 1))
                nc.scalar.copy(net.qTm[:, tt].rearrange("p j t -> p (j t)"), net.bankb[6 + tt]).then_inc(self.qTb.sem, 1)

        def special(n, b):
            act.wait_ge(self.special.sem, self.special.at(n, 1))
            sp = net.sp[:, b] if self.rel else net.sp[:, b, :, 0, :]
            nc.scalar.activation(sp, sp, ACT.Exp).then_inc(self.pspecial.sem, 1)

        def exponentials(n):
            for i in range(len(self.units)):
                act.wait_ge(self.b_scored.sem, self.b_scored.at(n, i + 1))
                act.wait_ge(self.pv.sem, self.pv.at(n, max(i - 1, 0)))
                nc.scalar.activation(net.pT[:, i % 2, :, :], net.scores[:, 1], ACT.Exp).then_inc(self.exps.sem, 1)
                if i == self.units_first:
                    by_head(n, 0)
            by_head(n, 1)

        def by_head(n, qt):
            act.wait_ge(self.pv.sem, self.pv.at(n, (self.units_first, len(self.units))[qt]))
            nc.scalar.copy(net.pvT[:, qt, :], net.bank[6 + qt]).then_inc(self.pvT.sem, 1)

        def turned(n):
            act.wait_ge(self.oT_psum.sem, self.oT_psum.at(n, 1))
            self.permute(nc.scalar.copy, net.oT[:, :], net.bank[6][:, 0:S], back=True).then_inc(self.oT.sem, 1)

        def first():
            for n in range(2):
                normed(n)
                stacked(n, n, range(4))

        def step(n, b, with_max, with_front):
            special(n, b)
            shifted_queries(n)
            if with_front:
                normed(n + 2)
            exponentials(n)
            if with_front:
                stacked(n + 2, b, range(4))
            turned(n)

        self.turns(act, first, step)


    def tensor(self, pe):
        net, nc, mm = self.net, self.net.nc, self.net.nc.tensor.matmul
        w = self.w
        nu = len(self.units)
        pe.wait_ge(net.att_const, 1)
        pe.wait_ge(*w["loaded"])
        for t in (self.xnT_psum, self.proj, self.stackT, self.stackTm, self.a_scored, self.b_scored, self.pv, self.pv_tokens,
                  self.oT_psum, self.y):
            t.prime(pe)

        def score(slot, left, right, u, mask):
            for r in range(2):
                bank = net.scores[:, slot, r, :]
                cols, m = mask
                out = bank.rearrange("p (j k) -> p j k", j=4)[:, :, cols]
                mm(out, net.identb[:, :], m.unsqueeze(1).to_broadcast([P, 4, m.shape[1]]), start=True, stop=False,
                   skip_group_check=True)
            for jj in range(4):
                for r in range(2):
                    rows = slice(64 * r, 64 * r + 64)
                    ins = mm(net.scores[:, slot, r, jj * P:(jj + 1) * P], left[rows, 4 * u + jj, :],
                             right[rows, 4 * u + jj, :], start=False, stop=(jj == 3), skip_group_check=True)
            return ins

        def turn_normed(n):
            pe.wait_ge(self.xn.sem, self.xn.at(n, 1))
            pe.wait_ge(self.qkT.sem, self.qkT.at(n, 0))
            for tt in range(TPB):
                ins = nc.tensor.transpose(net.bank[4][:, tt * P:(tt + 1) * P], net.xn[:, tt, :], net.ident[:, :])
            ins.then_inc(self.xnT_psum.sem, 1)

        def project(n, tt):
            pe.wait_ge(self.xnT.sem, self.xnT.at(n, 1))
            pe.wait_ge(self.proj_read.sem, self.proj_read.at(n, tt))
            ins = mm(net.bank[4][:, 0:3 * D], net.xnTb[:, 1 + tt * P:1 + (tt + 1) * P], w["qkv"],
                     start=True, stop=True)
            if self.rel:
                ins = mm(net.bank[5][:, 0:2 * D], net.xnTb[:, tt * P:(tt + 1) * P], w["qkv"][:, D:3 * D],
                         start=True, stop=True)
            ins.then_inc(self.proj.sem, 1)

        def turn_stack(src, bank):
            for j in range(H // 2):
                ins = nc.tensor.transpose(bank[:, j * P:(j + 1) * P],
                                          src[:, 2 * j:2 * j + 2, :].rearrange("p h s -> p (h s)"), net.identb[:, :])
            return ins

        def stacks(n, b, groups):
            for g in groups:
                if g == 0:
                    pe.wait_ge(self.stacks.sem, self.stacks.at(n, 1))
                    pe.wait_ge(self.proj_read.sem, self.proj_read.at(n, 2))
                if g >= 2:
                    pe.wait_ge(self.qkT.sem, self.qkT.at(n, g - 1))
                src = (net.qs[:, b, 0], net.ks[:, 0], net.qs[:, b, 1], net.ks[:, 1])[g]
                turn_stack(src, net.bankb[4 + g % 2]).then_inc(self.stackT.sem, 1)

        def query_scores(n, b, a):
            qt, kt, u = self.units[a]
            if a == 0:
                pe.wait_ge(self.qkT.sem, self.qkT.at(n, 4))
            pe.wait_ge(self.amax.sem, self.amax.at(n, a))
            score(0, net.qT[:, qt], net.kT[:, b, kt], u, w["mask"][kt == qt]).then_inc(self.a_scored.sem, 1)

        def key_scores(n, b, i):
            qt, kt, u = self.units[i]
            if i == 0:
                pe.wait_ge(self.qTb.sem, self.qTb.at(n, 2))
            pe.wait_ge(self.exps.sem, self.exps.at(n, i))
            score(1, net.kT[:, b, kt], net.qTm[:, qt], u, w["maskT"][kt == qt]).then_inc(self.b_scored.sem, 1)

        def shifted_queries(n, b):
            pe.wait_ge(self.mparts.sem, self.mparts.at(n, 1))
            pe.wait_ge(self.added.sem, self.added.at(n, 0))
            for tt in range(TPB):
                turn_stack(net.qs[:, b, tt], net.bankb[6 + tt]).then_inc(self.stackTm.sem, 1)

        def values(n, b, i):
            qt, kt, u = self.units[i]
            if i == 0:
                pe.wait_ge(self.vready.sem, self.vready.at(n, 1))
            pe.wait_ge(self.exps.sem, self.exps.at(n, i + 1))
            first = i == 0 or self.units[i - 1][0] != qt
            for jj in range(4):
                for r in range(2):
                    h = 2 * (4 * u + jj) + r
                    rows, cols = slice(32 * (h % 4), 32 * (h % 4) + VS), slice(h // 4 * P, (h // 4 + 1) * P)
                    ins = mm(net.bank[6 + qt][rows, cols], net.vaug[:, kt, h, :],
                             net.pT[:, i % 2, r, jj * P:(jj + 1) * P], start=(first and jj < 2),
                             stop=(kt == qt and u == 1 and jj >= 2), skip_group_check=True)
            ins.then_inc(self.pv.sem, 1)

        def by_token(n, qt):
            pe.wait_ge(self.pvT.sem, self.pvT.at(n, qt + 1))
            for c in range(H // 4):
                ins = nc.tensor.transpose(net.bank[6 + qt][:, c * P:(c + 1) * P], net.pvT[:, qt, c * P:(c + 1) * P],
                                          net.ident[:, :])
            ins.then_inc(self.pv_tokens.sem, 1)

        def turn_attended(n):
            pe.wait_ge(self.attended.sem, self.attended.at(n, 2))
            for tt in range(TPB):
                ins = nc.tensor.transpose(net.bank[6][:, tt * P:(tt + 1) * P], net.att[:, tt, :], net.ident[:, :])
            ins.then_inc(self.oT_psum.sem, 1)

        def output(n):
            pe.wait_ge(self.oT.sem, self.oT.at(n, 1))
            for tt in range(TPB):
                y = net.bank[7][:, tt * D:(tt + 1) * D]
                mm(y, net.oT[:, tt * P:(tt + 1) * P], w["out"], start=True, stop=False)
                ins = mm(y, net.ones[:, :], w["bias"], start=False, stop=True)
            ins.then_inc(self.y.sem, 1)

        def first():
            turn_normed(0)
            project(0, 0)
            project(0, 1)
            stacks(0, 0, range(4))
            turn_normed(1)
            for a in range(nu):
                query_scores(0, 0, a)
                if a < TPB:
                    project(1, a)
            stacks(1, 1, range(4))

        def step(n, b, with_max, with_front):
            shifted_queries(n, b)
            if with_front:
                turn_normed(n + 2)
            if with_max:
                query_scores(n + 1, 1 - b, 0)
            if with_front:
                project(n + 2, 0)
            key_scores(n, b, 0)
            if with_max:
                query_scores(n + 1, 1 - b, 1)
            if with_front:
                project(n + 2, 1)
            for i in range(nu):
                if i + 1 < nu:
                    key_scores(n, b, i + 1)
                values(n, b, i)
                if with_max and i + 2 < nu:
                    query_scores(n + 1, 1 - b, i + 2)
                if i == self.units_first:
                    by_token(n, 0)
            if with_front:
                stacks(n + 2, b, (0, 1))
            by_token(n, 1)
            if with_front:
                stacks(n + 2, b, (2, 3))
            turn_attended(n)
            output(n)

        self.turns(pe, first, step)


def attention_buffers(net):
    sb = net.sb
    net.xnTb = sb("normed_T_batch", [P, 1 + S])
    block, lower = net.sb_twice("attention_front", [P, 9 * S])
    v = net.share(block, dict(q_k=(P, TPB * 2 * D, FP32), bf16_parts=(P, 3 * TPB * 2 * D, BF16),
                              split_rest=(P, TPB * 2 * D, FP32), special_products=(P, TPB * 2 * D, FP32)))
    net.qk = v["q_k"].rearrange("p (t c) -> p t c", t=TPB)
    net.part = v["bf16_parts"].rearrange("p (i t c) -> p i t c", i=3, t=TPB)
    net.rest = v["split_rest"].rearrange("p (t c) -> p t c", t=TPB)
    net.prod = v["special_products"].rearrange("p (t a d) -> p t a d", t=TPB, a=2)
    net.xnT_lower = lower[:, 0:T * P]
    net.vaug = sb("v_and_one", [P, TPB, H, VS])
    net.pvT = net.hid[:, 1].rearrange("p a b -> p (a b)").rearrange("p (a b) -> p a b", a=2)
    net.v = sb("v_tokens", [P, 2, TPB, D])
    net.prod2 = sb("special_values", [P, TPB, 2, D])
    net.spsum = sb("special_sum", [P, TPB, H])
    net.kv2, upper = net.sb_twice("kv_self_and_previous", [P, 2, TPB, 2, 2 * D])
    net.xnT_upper = upper[:, :, :, :, :].rearrange("p a b c d -> p (a b c d)")
    net.sp = sb("special_scores", [P, 2, TPB, 2, H])
    net.mx = sb("score_max", [P, 2, TPB, H])
    net.mneg = sb("minus_max", [P, TPB, H])
    net.mrest = sb("minus_max_rest", [P, TPB, H])
    net.qs = sb("q_stack", [P, 2, TPB, H, ST], BF16)
    net.ks = sb("k_stack", [P, TPB, H, ST], BF16)
    net.qT = net.hid[:, 0].rearrange("p a b -> p (a b)").bitcast(BF16).rearrange("p (t u k) -> p t u k", t=TPB, k=P)
    net.qTm = sb("q_stack_max_T", [P, TPB, H // 2, P], BF16)
    net.kT = sb("k_stack_T", [P, 2, TPB, H // 2, P], BF16)
    net.pT = net.xnT[:, :].rearrange("p (a b k) -> p a b k", a=2, b=2)
    net.den = sb("softmax_sum", [P, TPB, H])
    net.att = sb("attended_tokens", [P, TPB, D])
    net.oT = sb("attended_T", [P, S])
    net.ones = sb("ones_row", [1, P])
    net.add_far = sb("add_far", [P, 3 * D])
    net.add_self = sb("add_self", [P, 2 * D])
    net.add_prev = sb("add_prev", [P, 2 * D])
    net.first_row = sb("first_row_mask", [P, 1])
    net.short_row = sb("short_patch_rows", [P, 1])
    net.causal = sb("causal_masks", [P, 4, P], BF16)
    net.patch = sb("patch_mask", [P, P], BF16)
    net.member = sb("patch_members", [7, P])
    net.bias = sb("biases_everywhere", [P, 3 * D])
    net.table = sb("rel_tables_everywhere", [P, 2, 3, HD])
    net.patchsum = net.sem("patch_members_multiplied")
    net.made = net.sem("attention_constants_steps")
    net.att_const = net.sem("attention_constants_ready")
    net.biases = net.sem("biases_loaded")


def attention_constants(net, block_gpsimd):
    g, pool = net.nc.gpsimd, block_gpsimd
    chain = Chain(pool, net.made)
    for t, value in ((net.xnTb[:, 0:1], 0.0), (net.vaug[:, :, :, :], 0.0), (net.qs[:, :, :, :, :].rearrange("p b t h s -> p (b t h s)"), 0.0),
                     (net.ks[:, :, :, :], 0.0), (net.ones[:, :], 1.0), (net.first_row[:, :], 0.0),
                     (net.short_row[:, :], 0.0), (net.causal[:, :, :], 0.0), (net.member[:, :], 1.0)):
        ins = g.memset(t, value)
    chain.then_wait(ins)
    g.memset(net.ks[:, :, :, 48:51], 1.0)
    g.memset(net.vaug[:, :, :, HD], 1.0)
    for i, (base, sign) in enumerate(((S // 2 - 2, 1), (-2, 1), (S // 2 - 2, -1), (-2, -1))):
        g.affine_select(out=net.causal[:, i, :], in_=net.causal[:, i, :], compare_op=ALU.is_ge, fill=NEG,
                        base=base, pattern=[[-sign, P]], channel_multiplier=sign)
    g.affine_select(out=net.first_row[:, :], in_=net.first_row[:, :], compare_op=ALU.is_ge, fill=NEG, base=-1,
                    pattern=[[0, 1]], channel_multiplier=1)
    g.affine_select(out=net.short_row[:, :], in_=net.short_row[:, :], compare_op=ALU.is_ge, fill=NEG, base=-120,
                    pattern=[[0, 1]], channel_multiplier=1)
    whole = net.member[:, 0:120].rearrange("p (b i r) -> p b i r", b=3, r=2)
    g.affine_select(out=whole, in_=whole, compare_op=ALU.is_equal, fill=0.0, base=0,
                    pattern=[[-2, 3], [0, 20], [-1, 2]], channel_multiplier=1)
    chain.then_wait(g.affine_select(out=net.member[:, 120:128], in_=net.member[:, 120:128], compare_op=ALU.is_equal,
                                    fill=0.0, base=-6, pattern=[[0, 8]], channel_multiplier=1))
    pool.wait_ge(net.biases, 9 * 16)
    far = net.add_far
    chain.then_wait(g.tensor_scalar(far[:, 0:D], net.bias[:, 0:D], SCALE, None, ALU.mult))
    for kv in range(2):
        b = net.bias[:, (1 + kv) * D:(2 + kv) * D].rearrange("p (h d) -> p h d", d=HD)
        for row, dst in ((0, far[:, (1 + kv) * D:(2 + kv) * D]), (1, net.add_prev[:, kv * D:(kv + 1) * D]),
                         (2, net.add_self[:, kv * D:(kv + 1) * D])):
            ins = g.tensor_tensor(dst.rearrange("p (h d) -> p h d", d=HD), b,
                                  net.table[:, kv, row, :].unsqueeze(1).to_broadcast([P, H, HD]), ALU.add)
    for q in (net.wqkv0[:, 0:D], net.wqkv1[:, 0:D]):
        ins = g.tensor_scalar(q, q, SCALE, None, ALU.mult)
    chain.then_wait(ins)


def attention_mask(net, dve):
    dve.wait_ge(net.patchsum, 1)
    dve.wait_ge(net.made, 4)
    net.nc.vector.tensor_scalar(net.patch[:, :], net.bank[0][:, 0:P], -1.0, -NEG, ALU.add,
                                ALU.mult).then_inc(net.att_const, 1)


def attention_mask_members(net, pe):
    pe.wait_ge(net.made, 2)
    net.nc.tensor.matmul(net.bank[0][:, 0:P], net.member[:, :], net.member[:, :], start=True,
                         stop=True).then_inc(net.patchsum, 1)


def build(nc, x, l0_qkv, l0_out, l0_bout, l1_q, l1_k, l1_v, l1_bq, l1_bk, l1_bv, l1_out, l1_bout, rel_k, rel_v, l0_gate, l0_w1, l0_w2, l1_gate, l1_w1, l1_w3, l1_w2, l1_s1, l1_s3, l1_s2, out, stages=range(6)):
    with ExitStack() as ctx:
        net = Net(nc, ctx, None)
        l0_gate_sb = net.sb("l0_gate_w", [P, E])
        l0_w1_sb, w1_upper = net.sb_twice("l0_w1", [P, E, F])
        l0_w2_sb, w3_upper = net.sb_twice("l0_w2", [P, E, FT, D])
        l1_gate_sb = net.sb("l1_gate_w", [P, E])
        l1_w1_sb, w1_lower = net.sb_twice("l1_w1", [P, NE, F])
        l1_w3_sb, w3_lower = net.sb_twice("l1_w3", [P, NE, F])
        l1_w2_sb = net.sb("l1_w2", [P, NE, FT, D])
        l0_loaded = net.sem("l0_weights_loaded")
        l1_loaded = net.sem("l1_weights_loaded")
        stored = net.sem("stored")

        net.wqkv0 = net.sb("l0_wqkv", [P, 3 * D])
        net.wqkv1 = net.sb("l1_wqkv", [P, 3 * D])
        l0_wout = net.sb("l0_wout", [P, D])
        l1_wout = net.sb("l1_wout", [P, D])
        l0_bias = net.sb("l0_bout", [1, D])
        l1_bias = net.sb("l1_bout", [1, D])
        att_loaded = net.sem("attention_weights_loaded")
        attention_buffers(net)
        choice_buffers(net)
        l1_upper = ((w1_upper, w3_upper[:, :, :, :].rearrange("p e f d -> p e (f d)")), net.shared_upper)
        patched = dict(qkv=net.wqkv0[:, :], out=l0_wout[:, :], bias=l0_bias[:, :], loaded=(att_loaded, 4 * 16),
                       mask=(None, (slice(0, P), net.patch[:, :])), maskT=(None, (slice(0, P), net.patch[:, :])))
        causal = dict(qkv=net.wqkv1[:, :], out=l1_wout[:, :], bias=l1_bias[:, :], loaded=(att_loaded, 4 * 16),
                      mask=((slice(P - 1, P), net.causal[:, 0, P - 1:P]), (slice(0, P), net.causal[:, 1, :])),
                      maskT=((slice(0, 1), net.causal[:, 2, 0:1]), (slice(0, P), net.causal[:, 3, :])))
        made = []

        def l0_ffn(name):
            made.append(ExpertChoice(net, name, l0_gate_sb[:, :], l0_w1_sb, l0_w2_sb, (l0_loaded, 3 * 16)))

        def l1_ffn(name):
            made.append(TokenChoice(net, name, l1_gate_sb[:, :], (l1_w1_sb, l1_w3_sb, l1_w2_sb),
                                    (w1_lower, w3_lower), l1_upper, (l1_loaded, 7 * 16)))

        for stage in stages:
            if stage in (0, 2):
                l0_ffn(f"l0_ffn_{stage}")
            if stage in (1, 4):
                made.append(Attention(net, f"attn_{stage}", stage == 4, causal if stage == 4 else patched))
            if stage in (3, 5):
                l1_ffn(f"l1_ffn_{stage}")

        first_attention = next((stage for stage in made if isinstance(stage, Attention)), None)
        block = ctx.enter_context(nc.Block())

        @block.sync
        def _(sp):
            sp.dma_start(net.x[:, :, :], x.rearrange("b (a p) d -> p (b a) d", p=P)).then_inc(net.xload, 16)
            row = lambda b: b.rearrange("(a n) -> a n", a=1)
            sp.dma_start(net.wqkv0[:, :], l0_qkv).then_inc(net.biases, 16)
            for i, w in enumerate((l1_q, l1_k, l1_v)):
                sp.dma_start(net.wqkv1[:, i * D:(i + 1) * D], w).then_inc(net.biases, 16)
            for i, b in enumerate((l1_bq, l1_bk, l1_bv)):
                sp.dma_start(net.bias[:, i * D:(i + 1) * D], row(b).to_broadcast([P, D])).then_inc(net.biases, 16)
            for i, t in enumerate((rel_k, rel_v)):
                sp.dma_start(net.table[:, i, :, :].rearrange("p r d -> p (r d)"),
                             row(t.rearrange("r d -> (r d)")[0:3 * HD]).to_broadcast([P, 3 * HD])).then_inc(net.biases, 16)
            sp.dma_start(l0_wout[:, :], l0_out).then_inc(att_loaded, 16)
            sp.dma_start(l1_wout[:, :], l1_out).then_inc(att_loaded, 16)
            sp.dma_start(l0_bias[:, :], row(l0_bout)).then_inc(att_loaded, 16)
            sp.dma_start(l1_bias[:, :], row(l1_bout)).then_inc(att_loaded, 16)
            sp.dma_start(l0_gate_sb[:, :], l0_gate).then_inc(l0_loaded, 16)
            sp.dma_start(l0_w1_sb[:, :, :], l0_w1.rearrange("e d f -> d e f")).then_inc(l0_loaded, 16)
            sp.dma_start(l0_w2_sb[:, :, :, :], l0_w2.rearrange("e (f p) d -> p (e f) d", p=P).rearrange("p (e f) d -> p e f d", e=E)).then_inc(l0_loaded, 16)
            sp.dma_start(l1_gate_sb[:, :], l1_gate).then_inc(l1_loaded, 16)
            sp.dma_start(l1_w1_sb[:, 0:E, :], l1_w1.rearrange("e d f -> d e f")).then_inc(l1_loaded, 16)
            sp.dma_start(l1_w3_sb[:, 0:E, :], l1_w3.rearrange("e d f -> d e f")).then_inc(l1_loaded, 16)
            sp.dma_start(l1_w2_sb[:, 0:E, :, :], l1_w2.rearrange("e (f p) d -> p (e f) d", p=P).rearrange("p (e f) d -> p e f d", e=E)).then_inc(l1_loaded, 16)
            sp.dma_start(l1_w1_sb[:, E, :], l1_s1.rearrange("n d f -> d n f")).then_inc(l1_loaded, 16)
            sp.dma_start(l1_w3_sb[:, E, :], l1_s3.rearrange("n d f -> d n f")).then_inc(l1_loaded, 16)
            sp.dma_start(l1_w2_sb[:, E, :, :], l1_s2.rearrange("(f a) q d -> (a q) f d", a=2)).then_inc(l1_loaded, 16)
            sp.wait_ge(*net.ready)
            sp.dma_start(out.rearrange("b (a p) d -> p (b a) d", p=P), net.x[:, :, :]).then_inc(stored, 16)
            sp.wait_ge(stored, 16)

        @block.gpsimd
        def _(pool):
            nc.gpsimd.memset(net.ident[:, :], 1.0).then_inc(net.const, 1)
            nc.gpsimd.memset(net.minus_half[:, :], -0.5).then_inc(net.const, 1)
            pool.wait_ge(net.const, 2)
            nc.gpsimd.affine_select(out=net.ident[:, :], in_=net.ident[:, :], compare_op=ALU.is_equal, fill=0.0,
                                    base=0, pattern=[[-1, P]], channel_multiplier=1).then_inc(net.const, 1)
            pool.wait_ge(net.const, 3)
            nc.gpsimd.tensor_copy(net.identb[:, :], net.ident[:, :]).then_inc(net.const, 1)
            choice_constants(net, pool)
            made[0].gpsimd(pool)
            attention_constants(net, pool)
            for stage in made[1:]:
                stage.gpsimd(pool)

        @block.vector
        def _(dve):
            for stage in made:
                if stage is first_attention:
                    attention_mask(net, dve)
                stage.vector(dve)

        @block.scalar
        def _(act):
            for stage in made:
                stage.scalar(act)

        @block.tensor
        def _(pe):
            for stage in made:
                if stage is first_attention:
                    attention_mask_members(net, pe)
                    pe.wait_ge(net.att_const, 1)
                stage.tensor(pe)


_INS = ["L0_attn_x", "L0_attn_Wqkv", "L0_attn_Wout", "L0_attn_bout", "L1_attn_W_q", "L1_attn_W_k", "L1_attn_W_v",
        "L1_attn_b_q", "L1_attn_b_k", "L1_attn_b_v", "L1_attn_W_o", "L1_attn_b_o", "L1_attn_rel_k_table",
        "L1_attn_rel_v_table", "L0_ffn_gate_w", "L0_ffn_w1", "L0_ffn_w2", "L1_ffn_gate_W", "L1_ffn_w1_e", "L1_ffn_w3_e",
        "L1_ffn_w2_e", "L1_ffn_w1_s", "L1_ffn_w3_s", "L1_ffn_w2_s"]
_TURNED = {"L1_ffn_gate_W", "L0_attn_Wqkv", "L0_attn_Wout"}


def kernel(**inputs):
    import concourse.bacc as bacc
    from concourse.bass_utils import run_bass_kernel_spmd

    nc = bacc.Bacc("TRN2", target_bir_lowering=False, num_devices=1)
    arrays, args = {}, []
    for name in _INS:
        a = np.asarray(inputs[name])
        a = np.ascontiguousarray(a.T if name in _TURNED else a)
        arrays[f"in_{name}"] = a
        args.append(nc.dram_tensor(f"in_{name}", a.shape, mybir.dt.from_np(a.dtype), kind="ExternalInput").ap())
    out = nc.dram_tensor("out_x", (B, S, D), FP32, kind="ExternalOutput").ap()
    build(nc, *args, out)
    r = run_bass_kernel_spmd(nc, [arrays], core_ids=[0])
    return r.results[0]["out_x"]
```

```python
from contextlib import ExitStack

import numpy as np

import concourse.bass as bass
from concourse import mybir

FP32 = mybir.dt.float32
BF16 = mybir.dt.bfloat16
FP32R = mybir.dt.float32r
ALU = mybir.AluOpType
ACT = mybir.ActivationFunctionType
AX = mybir.AxisListType

P = 128
B, S, D = 8, 256, 128
TPB = S // P
T = B * TPB
E = 8
F = 512
FT = F // P
NE = E + 1
SHARED = 0.5 * 0.5 / 8
STEPS = 2 * NE
GROUP = 4
BY_POOL = 4
CHOICE_WORDS = 4096
CAP = 2 * S // E
H, HD = 16, 8
EPS = 1e-5
NEG = -1e30
TAKEN = -1.0


class Net:

    def __init__(self, nc, ctx):
        self.nc, self.ctx = nc, ctx
        self.x = self.sb("x_tokens", [P, T, D])
        self.xnT = self.sb("normed_T", [P, T * P])
        self.xn = self.sb("normed_pair", [P, TPB, D])
        self.stats = self.sb("ln_stats", [P, T, 6])
        self.mv = self.sb("ln_mean_var", [P, T, 2])
        self.vareps = self.sb("ln_var_eps", [P, T])
        self.rstd = self.sb("ln_rstd", [P, T])
        self.minus_half = self.sb("minus_half", [P, T])
        self.ident = self.sb("ident", [P, P])
        self.identb = self.sb("ident_bf16", [P, P], BF16)
        self.scores = ctx.enter_context(nc.psum_tensor("banks0to3", [P, 2, 2, 512], FP32))
        later = [ctx.enter_context(nc.psum_tensor(f"bank{n}", [P, 512], FP32)) for n in range(4, 8)]
        self.bank = [self.scores[:, n // 2, n % 2, :] for n in range(4)] + [b[:, :] for b in later]
        self.bankb = [b.bitcast(BF16) for b in self.bank]
        self.logit = self.sb("router_logit", [P, T, E])
        self.prob = self.sb("router_prob", [P, T, E])
        self.rmax = self.sb("router_max", [P, T])
        self.rsum = self.sb("router_sum", [P, T])
        self.gate = self.sb("gate", [P, T, E])
        self.top8 = self.sb("top8", [P, T, 8])
        self.left = self.sb("probs_left", [P, T, E])
        self.best = self.sb("best8", [B * E, 8])
        self.hid = self.sb("hidden", [P, 2, 2 * FT, P])
        self.sil = self.sb("silu_gate", [P, 2, 4 * P])
        self.acc = self.sb("expert_sum", [P, 4, D])
        self.accb = self.sb("expert_sum_bf16", [P, 4, D], BF16)
        self.xload = [self.sem(f"x_loaded_{g}") for g in range(T // GROUP)]
        self.const = self.sem("constants_made")
        self.sems, self.counts = {}, {}
        self.weights_split = None
        self.ready = None

    def carve(self, block, layout):
        views, at = {}, 0
        for name, (rows, columns, dt) in layout.items():
            words = columns // (2 if dt is BF16 else 1)
            view = block[0:rows, at:at + words]
            views[name] = view.bitcast(BF16) if dt is BF16 else view
            at += words
        return views

    def shared(self, name):
        if name not in self.sems:
            self.sems[name] = self.sem(name)
        return self.sems[name], self.counts.get(name, 0)

    def sb(self, name, shape, dt=FP32):
        return self.ctx.enter_context(self.nc.sbuf_tensor(name, shape, dt))

    def sb_twice(self, name, shape):
        with self.nc.sbuf_tensor(f"{name}_float32r", shape, FP32R) as rounded:
            pass
        return self.sb(name, shape), rounded

    def sem(self, name):
        return self.ctx.enter_context(self.nc.semaphore(name))


class Chain:

    def __init__(self, eng, sem, base=0):
        self.eng, self.sem, self.base, self.n = eng, sem, base, 0

    def __call__(self, ins):
        ins.then_inc(self.sem, 1)
        self.n += 1
        return self.base + self.n

    def then_wait(self, ins):
        self.eng.wait_ge(self.sem, self(ins))


class Tally:

    def __init__(self, net, name, per, turns=B):
        self.sem, self.base = net.shared(name)
        self.new = self.base == 0
        self.per = per
        net.counts[name] = self.base + turns * per

    def prime(self, eng):
        if self.new:
            eng.sem_inc(self.sem, 1)

    def at(self, n, k):
        return n * self.per + (self.base + k + 1)


class Spread:

    def __init__(self, net, name):
        self.net = net
        self.first = net.ready is None
        self.own = net.sem(f"{name}_stats_steps")
        self.var_ready = net.sem(f"{name}_var_ready")
        self.rstd_ready = net.sem(f"{name}_rstd_ready")

    def vector(self, dve, g):
        net, v = self.net, self.net.nc.vector
        tiles = range(g * GROUP, (g + 1) * GROUP)
        if self.first:
            dve.wait_ge(net.xload[g], 16)
        for t in tiles:
            ins = v.bn_stats(net.stats[:, t, :], net.x[:, t, :])
        ins.then_inc(self.own, 1)
        dve.wait_ge(self.own, 2 * g + 1)
        for t in tiles:
            ins = v.bn_aggr(net.mv[:, t, :], net.stats[:, t, :])
        ins.then_inc(self.own, 1)
        dve.wait_ge(self.own, 2 * g + 2)
        at = slice(g * GROUP, (g + 1) * GROUP)
        v.tensor_scalar_add(net.vareps[:, at], net.mv[:, at, 1], EPS).then_inc(self.var_ready, 1)

    def gpsimd(self, pool):
        net = self.net
        for g in range(T // GROUP):
            pool.wait_ge(self.var_ready, g + 1)
            at = slice(g * GROUP, (g + 1) * GROUP)
            net.nc.gpsimd.tensor_tensor(net.rstd[:, at], net.vareps[:, at], net.minus_half[:, at],
                                        ALU.pow).then_inc(self.rstd_ready, 1)

    def wait(self, dve, g):
        dve.wait_ge(self.rstd_ready, g + 1)


class Front:

    def __init__(self, net, name, gate_w, loaded, split=False):
        self.net, self.gate_w, self.loaded, self.split = net, gate_w, loaded, split
        groups = T // GROUP
        self.spread = Spread(net, name)
        self.xn = Tally(net, "front_xn", groups, 1)
        self.xnT_psum = Tally(net, "front_xnT_psum", groups, 1)
        self.xnT = Tally(net, "front_xnT", groups, 1)
        self.logits = Tally(net, "front_logits", 1, 1)
        self.logit = Tally(net, "front_logit", 1, 1)
        self.exps = Tally(net, "front_exps", 1, 1)
        if split:
            self.lower = Tally(net, "front_lower", T // GROUP, 1)
        self.normed = net.hid[:, :, :, :].rearrange("p a f k -> p (a f) k")

    def vector(self, dve, chain, between=lambda g: None):
        net, v = self.net, self.net.nc.vector

        def lower(g):
            at = slice(g * GROUP * P, (g + 1) * GROUP * P)
            dve.wait_ge(self.xnT.sem, self.xnT.at(0, g + 1))
            v.tensor_tensor(net.xnT_lower[:, at], net.xnT[:, at], net.xnT_upper[:, at],
                            ALU.subtract).then_inc(self.lower.sem, 1)

        self.spread.vector(dve, 0)
        for g in range(T // GROUP):
            if (g + 1) * GROUP < T:
                self.spread.vector(dve, g + 1)
            self.spread.wait(dve, g)
            for t in range(g * GROUP, (g + 1) * GROUP):
                ins = normalise(net, self.normed[:, t, :], t)
            ins.then_inc(self.xn.sem, 1)
            between(g)
            if self.split and g:
                lower(g - 1)
        if self.split:
            lower(T // GROUP - 1)
        dve.wait_ge(self.logits.sem, self.logits.at(0, 1))
        lg = net.bank[7][:, 0:T * E].rearrange("p (t e) -> p t e", e=E)
        chain.then_wait(v.reduce_max(net.rmax[:, :], lg, AX.X))
        v.tensor_tensor(net.logit[:, :, :], lg, net.rmax[:, :].unsqueeze(2).to_broadcast([P, T, E]),
                        ALU.subtract).then_inc(self.logit.sem, 1)
        dve.wait_ge(self.exps.sem, self.exps.at(0, 1))
        chain.then_wait(v.reduce_sum(net.rsum[:, :], net.prob[:, :, :], AX.X))
        chain.then_wait(v.reciprocal(net.rsum[:, :], net.rsum[:, :]))
        chain.then_wait(v.tensor_tensor(net.prob[:, :, :], net.prob[:, :, :],
                                        net.rsum[:, :].unsqueeze(2).to_broadcast([P, T, E]), ALU.mult))

    def scalar(self, act, between=lambda g: None):
        net, nc = self.net, self.net.nc
        width = GROUP * P
        for g in range(T // GROUP):
            between(g)
            act.wait_ge(self.xnT_psum.sem, self.xnT_psum.at(0, g + 1))
            at = slice(g * width, (g + 1) * width)
            ins = nc.scalar.copy(net.xnT[:, at], net.bank[g])
            if self.split:
                ins = nc.scalar.copy(net.xnT_upper[:, at], net.bank[g])
            ins.then_inc(self.xnT.sem, 1)
        act.wait_ge(self.logit.sem, self.logit.at(0, 1))
        nc.scalar.activation(net.prob[:, :, :], net.logit[:, :, :], ACT.Exp).then_inc(self.exps.sem, 1)

    def tensor(self, pe):
        net, nc = self.net, self.net.nc
        groups = T // GROUP
        for g in range(groups + 1):
            if g < groups:
                pe.wait_ge(self.xn.sem, self.xn.at(0, g + 1))
                for q in range(GROUP):
                    ins = nc.tensor.transpose(net.bank[g][:, q * P:(q + 1) * P],
                                              self.normed[:, g * GROUP + q, :], net.ident[:, :])
                ins.then_inc(self.xnT_psum.sem, 1)
            if g == 0:
                pe.wait_ge(*self.loaded)
                continue
            pe.wait_ge(self.xnT.sem, self.xnT.at(0, g))
            for t in range((g - 1) * GROUP, g * GROUP):
                ins = nc.tensor.matmul(net.bank[7][:, t * E:(t + 1) * E], net.xnT[:, t * P:(t + 1) * P], self.gate_w,
                                       start=True, stop=True)
        ins.then_inc(self.logits.sem, 1)


def normalise(net, dst, t):
    at = slice(t, t + 1) if isinstance(t, int) else bass.ds(t, 1)
    return net.nc.vector.tensor_scalar(dst, net.x[:, at, :].rearrange("p a d -> p (a d)"), net.mv[:, at, 0],
                                       net.rstd[:, at], ALU.subtract, ALU.mult)


class ExpertChoice:

    def __init__(self, net, name, gate_w, w1, w2, loaded):
        self.net, self.w1, self.w2 = net, w1, w2
        self.before = net.ready
        self.front = Front(net, name, gate_w, net.gates_loaded)
        self.loaded = loaded
        once = 1
        self.router_steps = Tally(net, "choice_router_steps", 5 + 1 + 2 * (CAP // 8) + 4, once)
        self.probT_psum = Tally(net, "choice_probT_psum", 1, once)
        self.picked = Tally(net, "choice_picked", 1, once)
        self.turned = Tally(net, "choice_turned", 1, once)
        self.routed = Tally(net, "choice_routed", 1, once)
        pairs = B // 2
        self.prepared = Tally(net, "choice_prepared", 4, pairs)
        self.split_steps = Tally(net, "choice_split_steps", 8, pairs)
        self.selector = Tally(net, "choice_selector", 1, pairs)
        self.gathered = Tally(net, "choice_gathered", 2, pairs)
        self.xgT = Tally(net, "choice_xgT", 2, pairs)
        self.bcast = Tally(net, "choice_bcast", E, pairs)
        self.spread = Tally(net, "choice_spread", E, pairs)
        self.up = Tally(net, "choice_up", E, pairs)
        self.hidden = Tally(net, "choice_hidden", E, pairs)
        self.down = Tally(net, "choice_down", E, pairs)
        self.ycopied = Tally(net, "choice_ycopied", E, pairs)
        self.combined = Tally(net, "choice_combined", E, pairs)
        self.summed = Tally(net, "choice_summed", E, pairs)
        self.added = Tally(net, "choice_added", 2, pairs)
        net.ready = (self.added.sem, self.added.at(pairs, 0))

    def turns(self, eng, prepare, experts):
        prepare(0)
        with eng.Fori(0, B // 2 - 1) as i:
            experts(i, True)
        experts(B // 2 - 1, False)


    def vector(self, dve):
        net, v = self.net, self.net.nc.vector
        if self.before:
            dve.wait_ge(*self.before)
        else:
            dve.wait_ge(net.const, 4)
        for t in (self.front.xn, self.front.logit, self.router_steps, self.picked, self.routed, self.prepared,
                  self.split_steps, self.selector,
                  self.spread, self.summed, self.added):
            t.prime(dve)
        chain = Chain(dve, self.router_steps.sem, self.router_steps.at(0, 0))
        self.front.vector(dve, chain)
        by_half = net.gate[:, :, :].rearrange("p t e -> p (t e)").rearrange("p (a n e) -> p n a e", a=TPB, n=B)
        chain.then_wait(v.tensor_copy(by_half, net.prob[:, :, :].rearrange("p (n a) e -> p n a e", a=TPB)))
        dve.wait_ge(self.probT_psum.sem, self.probT_psum.at(0, 1))
        chain.then_wait(v.tensor_copy(net.probT[:, :], net.bank[7][0:B * E, 256:512]))
        src = net.probT
        for r in range(CAP // 8):
            chain.then_wait(v.max(net.best[:, :], src[:, :]))
            chain.then_wait(v.match_replace(net.leftT[:, :], net.best[:, :], src[:, :], TAKEN))
            src = net.leftT
        chain(v.scalar_tensor_tensor(net.gateT[:, :], net.leftT[:, :], 0.0, net.probT[:, :], ALU.is_lt, ALU.mult))
        chain.then_wait(v.tensor_scalar(net.leftT[:, :], net.leftT[:, :], 0.0, None, ALU.is_lt))
        chain.then_wait(v.tensor_tensor_scan(net.probT[:, :], net.leftT[:, :], net.leftT[:, :], 0.0,
                                             ALU.add, ALU.max))
        chain.then_wait(v.tensor_tensor(net.posT[:, :], net.probT[:, :], net.leftT[:, :], ALU.mult))
        v.tensor_copy(net.posTb[:, :], net.posT[:, :]).then_inc(self.picked.sem, 1)
        dve.wait_ge(self.turned.sem, self.turned.at(0, 1))
        for k, dst in enumerate((net.gate, net.pos)):
            src = net.bank[7][:, k * T * E:(k + 1) * T * E].rearrange("p (a n e) -> p n a e", a=TPB, n=B)
            ins = v.tensor_copy(dst[:, :, :].rearrange("p (n a) e -> p n a e", a=TPB), src)
        ins.then_inc(self.routed.sem, 1)
        dve.wait_ge(self.routed.sem, self.routed.at(0, 1))
        assert chain.n == self.router_steps.per, chain.n

        def prepare_tile(i, q):
            t = i * 4 + q
            at = slice(t, t + 1) if isinstance(t, int) else bass.ds(t, 1)
            if q == 0:
                dve.wait_ge(self.gathered.sem, self.gathered.at(i, 0))
            step = 2 * q
            normalise(net, net.xnq[:, q, :], t).then_inc(self.split_steps.sem, 1)
            dve.wait_ge(self.split_steps.sem, self.split_steps.at(i, step + 1))
            v.tensor_copy(net.xnq_upper[:, q, :], net.xnq[:, q, :]).then_inc(self.split_steps.sem, 1)
            pos = net.pos[:, at, :].rearrange("p a e -> p (a e)")
            v.tensor_tensor(net.pick[:, q, :, :], pos.unsqueeze(2).to_broadcast([P, E, CAP]),
                            net.numbers[:, :].unsqueeze(1).to_broadcast([P, E, CAP]), ALU.is_equal)
            dve.wait_ge(self.split_steps.sem, self.split_steps.at(i, step + 2))
            v.tensor_tensor(net.xnq_lower[:, q, :], net.xnq[:, q, :], net.xnq_upper[:, q, :],
                            ALU.subtract).then_inc(self.prepared.sem, 1)

        def select(i):
            dve.wait_ge(self.bcast.sem, self.bcast.at(i, 0))
            at = slice(i, i + 1) if isinstance(i, int) else bass.ds(i, 1)
            v.tensor_copy(net.rowsel[:, :], net.rowsels[:, at, :].rearrange("p a m -> p (a m)")
                          ).then_inc(self.selector.sem, 1)

        def prepare(i):
            dve.wait_ge(net.choice_const, 1)
            select(i)
            for q in range(4):
                prepare_tile(i, q)

        def spread(i, e):
            dve.wait_ge(self.bcast.sem, self.bcast.at(i, e + 1))
            dve.wait_ge(self.combined.sem, self.combined.at(i, max(e - 3, 0)))
            v.tensor_scalar(net.back[:, e % 4, :], net.bank[6 + e % 2][:, 0:S], net.number_col[:, :], None,
                            ALU.is_equal).then_inc(self.spread.sem, 1)

        def add(i, e):
            dve.wait_ge(self.combined.sem, self.combined.at(i, e + 1))
            if e:
                dve.wait_ge(self.summed.sem, self.summed.at(i, e))
            for q in range(4):
                t = i * 4 + q
                at = slice(t, t + 1) if isinstance(t, int) else bass.ds(t, 1)
                z = net.bank[4 + q // 2][:, (q % 2) * D:(q % 2 + 1) * D]
                if e == 0:
                    ins = v.tensor_scalar(net.acc[:, q, :], z, net.gate[:, at, e], None, ALU.mult)
                else:
                    ins = v.scalar_tensor_tensor(net.acc[:, q, :], z, net.gate[:, at, e], net.acc[:, q, :],
                                                 ALU.mult, ALU.add)
            ins.then_inc(self.summed.sem, 1)

        def experts(i, more):
            for e in range(E + 2):
                if e == E and more:
                    select(i + 1)
                if e < E:
                    spread(i, e)
                if e >= 2:
                    add(i, e - 2)
                if more and 2 <= e < 6:
                    prepare_tile(i + 1, e - 2)
            dve.wait_ge(self.summed.sem, self.summed.at(i, E))
            v.tensor_copy(net.accb[:, :, :], net.acc[:, :, :]).then_inc(self.added.sem, 1)
            dve.wait_ge(self.added.sem, self.added.at(i, 1))
            at = slice(i * 4, i * 4 + 4) if isinstance(i, int) else bass.ds(i * 4, 4)
            v.scalar_tensor_tensor(net.x[:, at, :], net.accb[:, :, :], 0.5, net.x[:, at, :], ALU.mult,
                                   ALU.add).then_inc(self.added.sem, 1)

        self.turns(dve, prepare, experts)

    def gpsimd(self, pool):
        self.front.spread.gpsimd(pool)


    def scalar(self, act):
        net, nc = self.net, self.net.nc
        for t in (self.front.xnT, self.front.exps, self.xgT, self.hidden, self.ycopied):
            t.prime(act)
        self.front.scalar(act)

        def gathered(i):
            for b in range(2):
                act.wait_ge(self.gathered.sem, self.gathered.at(i, b + 1))
                nc.scalar.copy(net.xgT[:, :, b, :], net.bank[6 + b].rearrange("p (e k) -> p e k", e=E)
                               ).then_inc(self.xgT.sem, 1)

        def gelu(i, e):
            act.wait_ge(self.up.sem, self.up.at(i, e + 1))
            act.wait_ge(self.down.sem, self.down.at(i, max(e - 1, 0)))
            nc.scalar.activation(net.hid[:, e % 2, 0:4, :].rearrange("p f k -> p (f k)"), net.bank[e % 2],
                                 ACT.Gelu_apprx_tanh).then_inc(self.hidden.sem, 1)

        def results(i, e):
            act.wait_ge(self.down.sem, self.down.at(i, e + 1))
            act.wait_ge(self.combined.sem, self.combined.at(i, max(e - 1, 0)))
            nc.scalar.copy(net.y[:, e % 2, :], net.bank[2 + e % 2][:, 0:D]).then_inc(self.ycopied.sem, 1)

        def experts(i, more):
            for e in range(E + 1):
                if e < E:
                    gelu(i, e)
                if e >= 1:
                    results(i, e - 1)
            if more:
                gathered(i + 1)

        self.turns(act, gathered, experts)


    def tensor(self, pe):
        net, nc, mm = self.net, self.net.nc, self.net.nc.tensor.matmul
        if not self.before:
            pe.wait_ge(net.const, 4)
        for t in (self.front.xnT_psum, self.front.logits, self.probT_psum, self.turned, self.gathered, self.bcast,
                  self.up, self.down, self.combined):
            t.prime(pe)
        self.front.tensor(pe)
        pe.wait_ge(self.router_steps.sem, self.router_steps.at(0, 5))
        pr = net.gate[:, :, :].rearrange("p t e -> p (t e)")
        for tt in range(TPB):
            ins = nc.tensor.transpose(net.bank[7][0:B * E, 256 + tt * P:256 + (tt + 1) * P],
                                      pr[:, tt * B * E:(tt + 1) * B * E], net.ident[:, :])
        ins.then_inc(self.probT_psum.sem, 1)
        pe.wait_ge(self.picked.sem, self.picked.at(0, 1))
        for k, src in enumerate((net.gateT, net.posT)):
            for tt in range(TPB):
                ins = nc.tensor.transpose(net.bank[7][:, (k * TPB + tt) * B * E:(k * TPB + tt + 1) * B * E],
                                          src[:, tt * P:(tt + 1) * P], net.ident[0:B * E, 0:B * E])
        ins.then_inc(self.turned.sem, 1)
        pe.wait_ge(self.routed.sem, self.routed.at(0, 1))

        pe.wait_ge(*self.loaded)

        def gather(i):
            pe.wait_ge(self.spread.sem, self.spread.at(i, 0))
            for b in range(2):
                for tt in range(TPB):
                    q = 2 * b + tt
                    pe.wait_ge(self.prepared.sem, self.prepared.at(i, q + 1))
                    pick = net.pick[:, q, :, :].rearrange("p e k -> p (e k)")
                    mm(net.bank[6 + b], net.xnq_upper[:, q, :], pick, start=(tt == 0), stop=False)
                    ins = mm(net.bank[6 + b], net.xnq_lower[:, q, :], pick, start=False, stop=(tt == TPB - 1))
                ins.then_inc(self.gathered.sem, 1)

        def broadcast(i, e):
            if e == 0:
                pe.wait_ge(self.selector.sem, self.selector.at(i, 1))
                pe.wait_ge(self.xgT.sem, self.xgT.at(i, 2))
            pe.wait_ge(self.spread.sem, self.spread.at(i, max(e - 1, 0)))
            mm(net.bank[6 + e % 2][:, 0:S], net.rowsel[:, e * P:(e + 1) * P], net.posTb[:, :], start=True,
               stop=True).then_inc(self.bcast.sem, 1)

        def up(i, e):
            pe.wait_ge(self.hidden.sem, self.hidden.at(i, max(e - 1, 0)))
            for f in range(FT):
                ins = mm(net.bank[e % 2][:, f * P:(f + 1) * P], self.w1[:, e, f * P:(f + 1) * P],
                         net.xgT[:, e, :, :].rearrange("p b k -> p (b k)"), start=True, stop=True)
            ins.then_inc(self.up.sem, 1)

        def down(i, e):
            pe.wait_ge(self.hidden.sem, self.hidden.at(i, e + 1))
            pe.wait_ge(self.ycopied.sem, self.ycopied.at(i, max(e - 1, 0)))
            for f in range(FT):
                ins = mm(net.bank[2 + e % 2][:, 0:D], net.hid[:, e % 2, f, :], self.w2[:, e, f, :],
                         start=(f == 0), stop=(f == FT - 1))
            ins.then_inc(self.down.sem, 1)

        def combine(i, e):
            pe.wait_ge(self.ycopied.sem, self.ycopied.at(i, e + 1))
            pe.wait_ge(self.spread.sem, self.spread.at(i, e + 1))
            pe.wait_ge(self.summed.sem, self.summed.at(i, e))
            for tt in range(TPB):
                for b in range(2):
                    rows = slice(CAP * b, CAP * (b + 1))
                    ins = mm(net.bank[4 + b][:, tt * D:(tt + 1) * D], net.back[rows, e % 4, tt * P:(tt + 1) * P],
                             net.y[rows, e % 2, :], start=True, stop=True)
            ins.then_inc(self.combined.sem, 1)

        def experts(i, more):
            for e in range(E + 2):
                if e < E:
                    broadcast(i, e)
                    up(i, e)
                if 1 <= e <= E:
                    down(i, e - 1)
                if e >= 2:
                    combine(i, e - 2)
                if e == E and more:
                    gather(i + 1)

        self.turns(pe, gather, experts)


def choice_buffers(net):
    block, upper = net.sb_twice("choice_only", [P, CHOICE_WORDS])
    rows, pairs = B * E, B // 2
    v = net.carve(block, dict(row_selectors=(rows, pairs * E * P, BF16), row_selector=(rows, E * P, BF16),
                              pick_number_T_bf16=(rows, S, BF16), pick_number_T=(rows, S, FP32), prob_T=(rows, S, FP32),
                              left_T=(rows, S, FP32), gate_T=(rows, S, FP32), pick_number=(P, T * E, FP32),
                              pick_results=(P, 2 * D, FP32)))
    net.shared_upper = upper[:, 0:2 * F]
    net.rowsels = v["row_selectors"].rearrange("r (i m) -> r i m", i=pairs)
    net.rowsel, net.posTb, net.posT = v["row_selector"], v["pick_number_T_bf16"], v["pick_number_T"]
    net.probT, net.leftT, net.gateT = v["prob_T"], v["left_T"], v["gate_T"]
    net.pos = v["pick_number"].rearrange("p (t e) -> p t e", e=E)
    net.y = v["pick_results"].rearrange("p (a d) -> p a d", a=2)
    net.xnq = net.prod2[:, :, :, :].rearrange("p a b d -> p (a b) d")
    net.pick = net.xnT_upper.rearrange("p (q e k) -> p q e k", q=4, e=E)
    parts = net.xnT_lower[:, 0:2 * 4 * D].rearrange("p (i q d) -> p i q d", i=2, q=4)
    net.xnq_upper, net.xnq_lower = parts[:, 0], parts[:, 1]
    kT = net.kT[:, :, :, :, :].rearrange("p a t u k -> p a (t u k)").bitcast(FP32)
    net.back = kT[:, 0].rearrange("p (a k) -> p a k", a=4)
    net.xgT = kT[:, 1].rearrange("p (e b k) -> p e b k", e=E, b=2)
    net.numbers = net.sb("numbers_row", [P, CAP])
    net.number_col = net.sb("numbers_column", [P, 1])
    net.choice_steps = net.sem("choice_constants_steps")
    net.choice_const = net.sem("choice_constants_ready")


def choice_constants(net, pool):
    g = net.nc.gpsimd
    g.iota(net.numbers[:, :], [[1, CAP]], base=1, channel_multiplier=0, allow_small_or_imprecise_dtypes=True)
    g.memset(net.rowsels[:, :, :], 1.0).then_inc(net.choice_steps, 1)
    g.iota(net.number_col[:, :], [[0, 1]], base=1, channel_multiplier=1,
           allow_small_or_imprecise_dtypes=True).then_inc(net.choice_steps, 1)
    pool.wait_ge(net.choice_steps, 2)
    g.tensor_scalar(net.number_col[CAP:P, :], net.number_col[CAP:P, :], float(-CAP), None,
                    ALU.add).then_inc(net.choice_steps, 1)
    pool.wait_ge(net.choice_steps, 3)
    view = net.rowsels[:, :, :].rearrange("r i (e b k) -> r (i e) b k", e=E, b=2)
    for i in range(B // 2):
        part = view[:, i * E:(i + 1) * E, :, :]
        ins = g.affine_select(out=part, in_=part, compare_op=ALU.is_equal, fill=0.0, base=-2 * E * i,
                              pattern=[[-1, E], [-E, 2], [0, CAP]], channel_multiplier=1)
    ins.then_inc(net.choice_const, 1)


class TokenChoice:

    def __init__(self, net, name, gate_w, whole, lower, upper, loaded):
        self.net, self.loaded = net, loaded
        (self.w1, self.w3, self.w2), self.lower = whole, lower
        self.uppers = upper
        self.before = net.ready
        self.front = Front(net, name, gate_w, net.gates_loaded, split=True)
        self.splits = net.weights_split is None
        if self.splits:
            net.weights_split = net.sem("weights_lower_parts")
        self.weights_split = net.weights_split
        self.weights_upper = Tally(net, "weights_upper", 2 * NE, 1) if self.splits else None
        self.router_steps = Tally(net, "tokens_router_steps", 8, 1)
        self.gates = Tally(net, "tokens_gates", 1, 1)
        turns = B // 2
        self.up = Tally(net, "tokens_up", 2 * STEPS, turns)
        self.act = Tally(net, "tokens_silu", 2 * STEPS, turns)
        self.hidden = Tally(net, "tokens_hidden", 2 * STEPS, turns)
        self.down = Tally(net, "tokens_down", STEPS, turns)
        self.added = Tally(net, "tokens_added", STEPS, turns)
        net.ready = (self.added.sem, self.added.at(turns, 0))

    def share(self, who, g):
        groups = T // GROUP
        if who == "scalar":
            return range(g * 2 * NE // groups, (g + 1) * 2 * NE // groups)
        last = 2 * NE - BY_POOL
        return range(g * last // groups, (g + 1) * last // groups)

    def lower_weight(self, eng, ops, k):
        i, e = k % 2, k // 2
        eng.wait_ge(self.weights_upper.sem, self.weights_upper.at(0, k + 1))
        ops.tensor_tensor(self.lower[i][:, e, :], (self.w1, self.w3)[i][:, e, :], self.upper(i, e),
                          ALU.subtract).then_inc(self.weights_split, 1)

    def upper(self, i, e):
        routed, shared = self.uppers
        return routed[i][:, e, :] if e < E else shared[:, i * F:(i + 1) * F]

    def vector(self, dve):
        net = self.net
        if self.before:
            dve.wait_ge(*self.before)
        else:
            dve.wait_ge(net.const, 4)
        for t in (self.front.xn, self.front.lower, self.front.logit, self.router_steps, self.gates, self.hidden,
                  self.added):
            t.prime(dve)
        chain = Chain(dve, self.router_steps.sem, self.router_steps.at(0, 0))

        def lower_weights(g):
            if self.splits:
                for k in self.share("vector", g):
                    self.lower_weight(dve, net.nc.vector, k)

        self.front.vector(dve, chain, lower_weights)
        self.token_choice(dve, chain)
        assert chain.n == self.router_steps.per, chain.n
        self.main_vector(dve)

    def token_choice(self, dve, chain):
        net, nc = self.net, self.net.nc
        for t in range(T):
            ins = nc.vector.max(net.top8[:, t, :], net.prob[:, t, :])
        chain.then_wait(ins)
        chain.then_wait(nc.vector.memset(net.top8[:, :, 2:8], -3.0))
        for t in range(T):
            ins = nc.vector.match_replace(net.left[:, t, :], net.top8[:, t, :], net.prob[:, t, :], TAKEN)
        chain.then_wait(ins)
        chain.then_wait(nc.vector.tensor_scalar(net.left[:, :, :], net.left[:, :, :], 0.0, 0.25, ALU.is_lt, ALU.mult))
        nc.vector.tensor_tensor(net.gate[:, :, :], net.left[:, :, :], net.prob[:, :, :],
                                ALU.mult).then_inc(self.gates.sem, 1)

    def main_vector(self, dve):
        net, nc = self.net, self.net.nc
        dve.wait_ge(self.gates.sem, self.gates.at(0, 1))

        def add(i, step):
            dve.wait_ge(self.down.sem, self.down.at(i, step + 1))
            dve.wait_ge(self.added.sem, self.added.at(i, step))
            e = step % NE
            for tt in range(TPB):
                t = (i * 2 + step // NE) * TPB + tt
                at = slice(t, t + 1) if isinstance(t, int) else bass.ds(t, 1)
                acc = net.x[:, at, :].rearrange("p a d -> p (a d)")
                factor = SHARED if e == E else net.gate[:, at, e]
                ins = nc.vector.scalar_tensor_tensor(acc, net.bank[4 + step % 2][:, tt * D:(tt + 1) * D], factor, acc,
                                                     ALU.mult, ALU.add)
            ins.then_inc(self.added.sem, 1)

        def gated(i, step, half):
            dve.wait_ge(self.act.sem, self.act.at(i, 2 * step + half + 1))
            if step >= 2:
                dve.wait_ge(self.down.sem, self.down.at(i, step - 1))
            nc.vector.tensor_tensor(
                net.hid[:, step % 2, 4 * half:4 * half + 4, :].rearrange("p a b -> p (a b)"),
                net.sil[:, half, :], net.bank[2 + half][:, :], ALU.mult).then_inc(self.hidden.sem, 1)

        for step in range(2):
            for half in range(2):
                gated(0, step, half)

        def turn(i, last):
            for step in range(2, STEPS if last else STEPS + 2):
                gated(i, step, 0)
                add(i, step - 2)
                gated(i, step, 1)

        with dve.Fori(0, B // 2 - 1) as i:
            turn(i, False)
        turn(B // 2 - 1, True)
        add(B // 2 - 1, STEPS - 2)
        add(B // 2 - 1, STEPS - 1)

    def gpsimd(self, pool):
        self.front.spread.gpsimd(pool)
        if self.splits:
            for k in range(2 * NE - BY_POOL, 2 * NE):
                self.lower_weight(pool, self.net.nc.gpsimd, k)

    def scalar(self, act):
        net, nc = self.net, self.net.nc
        for t in (self.front.xnT, self.front.exps, self.act):
            t.prime(act)
        if self.splits:
            self.weights_upper.prime(act)
            act.wait_ge(*self.loaded)
            act.wait_ge(*(self.before or (net.choice_const, 1)))

        def upper_weights(g):
            if self.splits:
                for k in self.share("scalar", g):
                    nc.scalar.copy(self.upper(k % 2, k // 2), (self.w1, self.w3)[k % 2][:, k // 2, :]
                                   ).then_inc(self.weights_upper.sem, 1)

        self.front.scalar(act, upper_weights)
        with act.Fori(0, B // 2) as i:
            for k in range(2 * STEPS):
                act.wait_ge(self.up.sem, self.up.at(i, k + 1))
                act.wait_ge(self.hidden.sem, self.hidden.at(i, max(k - 1, 0)))
                nc.scalar.activation(net.sil[:, k % 2, :], net.bank[k % 2][:, :], ACT.Silu).then_inc(self.act.sem, 1)

    def tensor(self, pe):
        net, nc = self.net, self.net.nc
        if not self.before:
            pe.wait_ge(net.const, 4)
        for t in (self.front.xnT_psum, self.front.logits, self.up, self.down):
            t.prime(pe)
        self.front.tensor(pe)
        pe.wait_ge(self.front.lower.sem, self.front.lower.at(0, T // GROUP))
        pe.wait_ge(*self.loaded)
        pe.wait_ge(self.weights_split, 2 * NE)

        def product(out, left, right):
            nc.tensor.matmul(out, left[0], right[0], start=True, stop=False)
            nc.tensor.matmul(out, left[0], right[1], start=False, stop=False)
            return nc.tensor.matmul(out, left[1], right[0], start=False, stop=True)

        def up(i, step):
            n, e = i * 2 + step // NE, step % NE
            at = slice(n * S, (n + 1) * S) if isinstance(n, int) else bass.ds(n * S, S)
            x = [part[:, at] for part in (net.xnT_upper, net.xnT_lower)]
            for half in range(2):
                if step >= 1:
                    pe.wait_ge(self.hidden.sem, self.hidden.at(i, 2 * step + half - 1))
                for w in range(2):
                    for f in range(2):
                        c = slice((2 * half + f) * P, (2 * half + f + 1) * P)
                        ins = product(net.bank[2 * w + half][:, f * S:(f + 1) * S],
                                      (self.upper(w, e)[:, c], self.lower[w][:, e, c]), x)
                ins.then_inc(self.up.sem, 1)

        def down(i, step):
            pe.wait_ge(self.added.sem, self.added.at(i, max(step - 1, 0)))
            hid = net.hid[:, step % 2, :, :].rearrange("p (f a) t -> p f a t", a=TPB)
            for half in range(2):
                pe.wait_ge(self.hidden.sem, self.hidden.at(i, 2 * step + half + 1))
                for tt in range(TPB):
                    for f in (2 * half, 2 * half + 1):
                        ins = nc.tensor.matmul(net.bank[4 + step % 2][:, tt * D:(tt + 1) * D], hid[:, f, tt, :],
                                               self.w2[:, step % NE, f, :], start=(tt == 0 and f == 0),
                                               stop=(tt == TPB - 1 and f == FT - 1), skip_group_check=True)
            ins.then_inc(self.down.sem, 1)

        def turn(i, last):
            for step in range(STEPS):
                if not (last and step == STEPS - 1):
                    up(i, step + 1)
                down(i, step)

        up(0, 0)
        with pe.Fori(0, B // 2 - 1) as i:
            turn(i, False)
        turn(B // 2 - 1, True)


VS = 32
ST = 64
SPLIT_Q = ((0, 3), (3, 2), (5, 1))
SPLIT_K = ((0, 0, 2, 3), (0, 5, 1, 1), (1, 1, 2, 3), (2, 2, 1, 1))
SCALE = float(HD) ** -0.5


class Attention:

    def __init__(self, net, name, rel, w):
        self.net, self.name, self.rel, self.w = net, name, rel, w
        self.before = net.ready
        self.pairs = ((0, 0), (1, 0), (1, 1)) if rel else ((0, 0), (1, 1))
        self.units = [(qt, kt, u) for qt, kt in self.pairs for u in range(2)]
        nu = len(self.units)
        self.units_first = sum(1 for qt, _, _ in self.units if qt == 0)
        self.spread = Spread(net, name)
        self.xn = Tally(net, "attn_xn", 1)
        self.xnT_psum = Tally(net, "attn_xnT_psum", 1)
        self.xnT = Tally(net, "attn_xnT", 1)
        self.proj = Tally(net, "attn_proj", 2)
        self.proj_read = Tally(net, "attn_proj_read", 2)
        self.parts = Tally(net, "attn_parts", 1)
        self.stacks = Tally(net, "attn_stacks", 1)
        self.stackT = Tally(net, "attn_stackT", 4)
        self.stackTm = Tally(net, "attn_stackTm", 2)
        self.qkT = Tally(net, "attn_qkT", 4)
        self.a_scored = Tally(net, "attn_a_scored", nu)
        self.amax = Tally(net, "attn_amax", nu)
        self.mparts = Tally(net, "attn_mparts", 1)
        self.qTb = Tally(net, "attn_qTb", 2)
        self.b_scored = Tally(net, "attn_b_scored", nu)
        self.exps = Tally(net, "attn_exps", nu)
        self.pv = Tally(net, "attn_pv", nu)
        self.special = Tally(net, "attn_special", 1)
        self.pspecial = Tally(net, "attn_pspecial", 1)
        self.attended = Tally(net, "attn_attended", 2)
        self.oT_psum = Tally(net, "attn_oT_psum", 1)
        self.oT = Tally(net, "attn_oT", 1)
        self.y = Tally(net, "attn_y", 1)
        self.added = Tally(net, "attn_added", 1)
        self.front_steps = Tally(net, "attn_front_steps", 13 if rel else 6)
        self.max_steps = Tally(net, "attn_max_steps", 8 if rel else 6)
        self.back_steps = Tally(net, "attn_back_steps", 9 if rel else 5)
        self.vready = Tally(net, "attn_vready", 1)
        self.pvT = Tally(net, "attn_pvT", 2)
        self.pv_tokens = Tally(net, "attn_pv_tokens", 2)
        net.ready = (self.added.sem, self.added.at(B, 0))

    def permute(self, copy, dst, src, back=False):
        if self.rel:
            return copy(dst[:, 0:S], src[:, 0:S])
        for tt in range(TPB):
            runs = ((slice(tt * P, tt * P + 120), slice(tt * 120, tt * 120 + 120)),
                    (slice(tt * P + 120, tt * P + 128), slice(240 + tt, 255 + tt, 2)))
            for patched, natural in runs:
                to, fro = (natural, patched) if back else (patched, natural)
                ins = copy(dst[:, to], src[:, fro])
        return ins

    def turns(self, eng, first, step):
        first()
        with eng.Fori(0, B // 2 - 1) as i:
            step(i * 2, 0, True, True)
            step(i * 2 + 1, 1, True, True)
        step(B - 2, 0, True, False)
        step(B - 1, 1, False, False)


    def vector(self, dve):
        net, v = self.net, self.net.nc.vector
        if self.before:
            dve.wait_ge(*self.before)
        for t in (self.xn, self.proj_read, self.parts, self.stacks, self.amax, self.mparts, self.special, self.attended,
                  self.added, self.vready, self.front_steps, self.max_steps, self.back_steps):
            t.prime(dve)
        self.spread.vector(dve, 0)
        self.spread.wait(dve, 0)

        def normalise(n):
            dve.wait_ge(self.xnT_psum.sem, self.xnT_psum.at(n, 0))
            for tt in range(TPB):
                t = n * TPB + tt
                at = slice(t, t + 1) if isinstance(t, int) else bass.ds(t, 1)
                ins = v.tensor_scalar(net.xn[:, tt, :], net.x[:, at, :].rearrange("p a d -> p (a d)"),
                                      net.mv[:, at, 0], net.rstd[:, at], ALU.subtract, ALU.mult)
            ins.then_inc(self.xn.sem, 1)

        def project(n, b, tt, chain):
            dve.wait_ge(self.proj.sem, self.proj.at(n, tt + 1))
            main, shifted = net.bank[4], net.bank[5]
            if self.rel:
                chain(v.tensor_tensor(net.qk[:, tt, :], main[:, 0:2 * D], net.add_far[:, 0:2 * D], ALU.add))
                chain(v.tensor_tensor(net.v[:, b, tt, :], main[:, 2 * D:3 * D], net.add_far[:, 2 * D:3 * D], ALU.add))
                chain(v.tensor_tensor(net.kv2[:, b, tt, 0, :], main[:, D:3 * D], net.add_self[:, :], ALU.add))
                v.tensor_tensor(net.kv2[:, b, tt, 1, :], shifted[:, 0:2 * D], net.add_prev[:, :],
                                ALU.add).then_inc(self.proj_read.sem, 1)
            else:
                chain(v.tensor_copy(net.qk[:, tt, :], main[:, 0:2 * D]))
                v.tensor_copy(net.v[:, b, tt, :], main[:, 2 * D:3 * D]).then_inc(self.proj_read.sem, 1)

        def split(n, b, chain, between=lambda: None, then=lambda: None):
            dve.wait_ge(self.proj_read.sem, self.proj_read.at(n, 2))
            chain.then_wait(v.tensor_copy(net.part[:, 0], net.qk[:, :, :]))
            chain.then_wait(v.tensor_tensor(net.rest[:, :, :], net.qk[:, :, :], net.part[:, 0], ALU.subtract))
            between()
            chain.then_wait(v.tensor_copy(net.part[:, 1], net.rest[:, :, :]))
            chain.then_wait(v.tensor_tensor(net.rest[:, :, :], net.rest[:, :, :], net.part[:, 1], ALU.subtract))
            v.tensor_copy(net.part[:, 2], net.rest[:, :, :]).then_inc(self.parts.sem, 1)
            then()
            dve.wait_ge(self.parts.sem, self.parts.at(n, 1))
            v.memset(net.qs[:, b, :, :, 48:51], 0.0)
            for tt in range(TPB):
                slots = net.qs[:, b, tt, :, 0:48].rearrange("p h (s d) -> p h s d", d=HD)
                for i, (first, many) in enumerate(SPLIT_Q):
                    q = net.part[:, i, tt, 0:D].rearrange("p (h d) -> p h d", d=HD).unsqueeze(2)
                    v.tensor_copy(slots[:, :, first:first + many, :], q.to_broadcast([P, H, many, HD]))
                slots = net.ks[:, tt, :, 0:48].rearrange("p h (s d) -> p h s d", d=HD)
                for i, first, many, step in SPLIT_K:
                    k = net.part[:, i, tt, D:2 * D].rearrange("p (h d) -> p h d", d=HD).unsqueeze(2)
                    ins = v.tensor_copy(slots[:, :, first:first + (many - 1) * step + 1:step, :],
                                        k.to_broadcast([P, H, many, HD]))
            ins.then_inc(self.stacks.sem, 1)

        def special_scores(n, b, chain):
            if not self.rel:
                return
            sp = net.sp[:, b]
            for tt in range(TPB):
                ins = v.tensor_tensor(net.prod[:, tt, :, :], net.kv2[:, b, tt, :, 0:D],
                                      net.qk[:, tt, 0:D].unsqueeze(1).to_broadcast([P, 2, D]), ALU.mult)
            chain.then_wait(ins)
            chain.then_wait(v.reduce_sum(
                sp.rearrange("p a b h -> p (a b h)"),
                net.prod[:, :, :, :].rearrange("p a b (h d) -> p (a b h) d", d=HD), AX.X))
            chain.then_wait(v.tensor_scalar(sp[:, 0, 1, :], sp[:, 0, 1, :], net.first_row[:, :], None, ALU.add))

        def special_values(n, b, chain):
            sp = net.sp[:, b]
            dve.wait_ge(self.pspecial.sem, self.pspecial.at(n, 1))
            if self.rel:
                for tt in range(TPB):
                    v2 = net.kv2[:, b, tt, :, D:2 * D].rearrange("p b (h d) -> p b h d", d=HD)
                    ins = v.tensor_tensor(net.prod2[:, tt, :, :].rearrange("p b (h d) -> p b h d", d=HD), v2,
                                          sp[:, tt, :, :].unsqueeze(3).to_broadcast([P, 2, H, HD]), ALU.mult)
                chain.then_wait(ins)
                chain.then_wait(v.tensor_tensor(net.prod2[:, :, 0, :], net.prod2[:, :, 0, :], net.prod2[:, :, 1, :],
                                                ALU.add))
                chain.then_wait(v.tensor_tensor(net.spsum[:, :, :], sp[:, :, 0, :], sp[:, :, 1, :], ALU.add))
            else:
                chain.then_wait(v.tensor_scalar(net.spsum[:, :, :], sp[:, :, 0, :], 12.0, None, ALU.mult))

        def largest(n, a):
            qt, kt, u = self.units[a]
            dve.wait_ge(self.a_scored.sem, self.a_scored.at(n, a + 1))
            out = net.mx[:, int(kt != qt), qt, :].rearrange("p (j r) -> p r j", r=2)[:, :, 4 * u:4 * u + 4]
            v.reduce_max(out, net.scores[:, 0].rearrange("p r (j k) -> p r j k", j=4), AX.X).then_inc(self.amax.sem, 1)

        def maximum(n, b, chain):
            dve.wait_ge(self.amax.sem, self.amax.at(n, len(self.units)))
            m = net.mx[:, 0, :, :]
            sp = net.sp[:, b]
            if self.rel:
                chain.then_wait(v.tensor_tensor(m, m, sp[:, :, 0, :], ALU.max))
                chain.then_wait(v.tensor_tensor(m, m, sp[:, :, 1, :], ALU.max))
                chain.then_wait(v.tensor_tensor(net.mx[:, 0, 1, :], net.mx[:, 0, 1, :], net.mx[:, 1, 1, :], ALU.max))
            else:
                chain.then_wait(v.tensor_scalar(m, m, net.short_row[:, :], None, ALU.max))
            chain.then_wait(v.tensor_scalar(net.mneg[:, :, :], m, -1.0, None, ALU.mult))
            mrow = [net.qs[:, b, :, :, 48 + i] for i in range(3)]
            chain.then_wait(v.tensor_copy(mrow[0], net.mneg[:, :, :]))
            chain.then_wait(v.tensor_tensor(net.mrest[:, :, :], net.mneg[:, :, :], mrow[0], ALU.subtract))
            chain.then_wait(v.tensor_copy(mrow[1], net.mrest[:, :, :]))
            chain.then_wait(v.tensor_tensor(net.mrest[:, :, :], net.mrest[:, :, :], mrow[1], ALU.subtract))
            v.tensor_copy(mrow[2], net.mrest[:, :, :]).then_inc(self.mparts.sem, 1)
            if self.rel:
                ins = v.tensor_tensor(sp, sp, net.mneg[:, :, :].unsqueeze(2).to_broadcast([P, TPB, 2, H]), ALU.add)
            else:
                ins = v.tensor_scalar(sp[:, :, 0, :], net.mneg[:, :, :], net.short_row[:, :], None, ALU.add)
            ins.then_inc(self.special.sem, 1)

        def finish(n, qt, chain):
            dve.wait_ge(self.pv_tokens.sem, self.pv_tokens.at(n, qt + 1))
            pv = net.bank[6 + qt].rearrange("p (h s) -> p h s", s=VS)
            den = net.den[:, qt, :]
            chain.then_wait(v.tensor_tensor(den, pv[:, :, HD], net.spsum[:, qt, :], ALU.add))
            chain.then_wait(v.reciprocal(den, den))
            o = net.att[:, qt, :].rearrange("p (h d) -> p h d", d=HD)
            src = pv[:, :, 0:HD]
            if self.rel:
                chain.then_wait(v.tensor_tensor(o, src, net.prod2[:, qt, 0, :].rearrange("p (h d) -> p h d", d=HD),
                                                ALU.add))
                src = o
            v.tensor_tensor(o, src, den.unsqueeze(2).to_broadcast([P, H, HD]),
                            ALU.mult).then_inc(self.attended.sem, 1)

        def add(n):
            dve.wait_ge(self.y.sem, self.y.at(n, 1))
            at = slice(n * TPB, (n + 1) * TPB) if isinstance(n, int) else bass.ds(n * TPB, TPB)
            xt = net.x[:, at, :]
            v.tensor_tensor(xt, net.bank[1][:, 0:S].rearrange("p (a d) -> p a d", a=TPB), xt,
                            ALU.add).then_inc(self.added.sem, 1)

        def values(n, b):
            if isinstance(n, int) and n == 0:
                ins = v.tensor_copy(net.vaug[:, :, :, 0:HD],
                                    net.v[:, b].rearrange("p t (h d) -> p t h d", d=HD))
            else:
                dve.wait_ge(self.pv.sem, self.pv.at(n, 0))
                ins = v.tensor_copy(net.vaug[:, :, :, 0:HD],
                                    net.v[:, b].rearrange("p t (h d) -> p t h d", d=HD))
            ins.then_inc(self.vready.sem, 1)

        def chain_of(tally, n):
            return Chain(dve, tally.sem, tally.at(n, 0))

        def first():
            normalise(0)
            front = chain_of(self.front_steps, 0)
            for g in range(1, T // GROUP):
                self.spread.vector(dve, g)
            dve.wait_ge(net.att_const, 1)
            for tt in range(TPB):
                project(0, 0, tt, front)
            split(0, 0, front)
            special_scores(0, 0, front)
            assert front.n == self.front_steps.per, front.n
            normalise(1)
            self.spread.wait(dve, T // GROUP - 1)
            project_and_maximise(0, 0)
            values(0, 0)

        def project_and_maximise(n, b, with_max=True, with_front=True, then=lambda: None):
            most = len(self.units)
            if with_front:
                front = chain_of(self.front_steps, n + 1)
            maxima = iter(range(most))

            def some(many):
                for _ in range(many if with_max else 0):
                    largest(n, next(maxima))

            some(1)
            if with_front:
                project(n + 1, 1 - b, 0, front)
            some(1)
            if with_front:
                project(n + 1, 1 - b, 1, front)
                split(n + 1, 1 - b, front, lambda: some(1), lambda: some(int(most > 4)))
                some(1)
                special_scores(n + 1, 1 - b, front)
                assert front.n == self.front_steps.per, front.n
            for a in maxima if with_max else ():
                largest(n, a)
            then()
            if with_max:
                longest = chain_of(self.max_steps, n)
                maximum(n, b, longest)
                assert longest.n == self.max_steps.per, longest.n

        def step(n, b, with_max, with_front):
            back = chain_of(self.back_steps, n)
            if with_front:
                normalise(n + 2)
            special_values(n, b, back)
            project_and_maximise(n + 1, 1 - b, with_max, with_front, lambda: finish(n, 0, back))
            if with_max:
                values(n + 1, 1 - b)
            finish(n, 1, back)
            assert back.n == self.back_steps.per, back.n
            add(n)

        self.turns(dve, first, step)


    def gpsimd(self, pool):
        self.spread.gpsimd(pool)


    def scalar(self, act):
        net, nc = self.net, self.net.nc
        for t in (self.xnT, self.qkT, self.qTb, self.exps, self.pspecial, self.pvT, self.oT):
            t.prime(act)

        def normed(n):
            act.wait_ge(self.xnT_psum.sem, self.xnT_psum.at(n, 1))
            self.permute(nc.scalar.copy, net.xnTb[:, 1:1 + S], net.bank[4][:, 0:S]).then_inc(self.xnT.sem, 1)

        def stacked(n, b, groups):
            for g in groups:
                dst = (net.qT[:, 0], net.kT[:, b, 0], net.qT[:, 1], net.kT[:, b, 1])[g]
                act.wait_ge(self.stackT.sem, self.stackT.at(n, g + 1))
                nc.scalar.copy(dst.rearrange("p j t -> p (j t)"), net.bankb[4 + g % 2]).then_inc(self.qkT.sem, 1)

        def shifted_queries(n):
            for tt in range(TPB):
                act.wait_ge(self.stackTm.sem, self.stackTm.at(n, tt + 1))
                nc.scalar.copy(net.qTm[:, tt].rearrange("p j t -> p (j t)"), net.bankb[6 + tt]
                               ).then_inc(self.qTb.sem, 1)

        def special(n, b):
            act.wait_ge(self.special.sem, self.special.at(n, 1))
            sp = net.sp[:, b] if self.rel else net.sp[:, b, :, 0, :]
            nc.scalar.activation(sp, sp, ACT.Exp).then_inc(self.pspecial.sem, 1)

        def exponentials(n):
            for i in range(len(self.units)):
                act.wait_ge(self.b_scored.sem, self.b_scored.at(n, i + 1))
                act.wait_ge(self.pv.sem, self.pv.at(n, max(i - 1, 0)))
                nc.scalar.activation(net.pT[:, i % 2, :, :], net.scores[:, 1], ACT.Exp).then_inc(self.exps.sem, 1)
                if i == self.units_first:
                    by_head(n, 0)
            by_head(n, 1)

        def by_head(n, qt):
            act.wait_ge(self.pv.sem, self.pv.at(n, (self.units_first, len(self.units))[qt]))
            nc.scalar.copy(net.pvT[:, qt, :], net.bank[6 + qt]).then_inc(self.pvT.sem, 1)

        def turned(n):
            act.wait_ge(self.oT_psum.sem, self.oT_psum.at(n, 1))
            self.permute(nc.scalar.copy, net.oT[:, :], net.bank[0][:, 0:S], back=True).then_inc(self.oT.sem, 1)

        def first():
            for n in range(2):
                normed(n)
                stacked(n, n, range(4))

        def step(n, b, with_max, with_front):
            special(n, b)
            shifted_queries(n)
            if with_front:
                normed(n + 2)
            exponentials(n)
            if with_front:
                stacked(n + 2, b, range(4))
            turned(n)

        self.turns(act, first, step)


    def tensor(self, pe):
        net, nc, mm = self.net, self.net.nc, self.net.nc.tensor.matmul
        w = self.w
        nu = len(self.units)
        pe.wait_ge(net.att_const, 1)
        pe.wait_ge(*w["loaded"])
        for t in (self.xnT_psum, self.proj, self.stackT, self.stackTm, self.a_scored, self.b_scored, self.pv,
                  self.pv_tokens, self.oT_psum, self.y):
            t.prime(pe)

        def score(slot, left, right, u, mask):
            for r in range(2):
                bank = net.scores[:, slot, r, :]
                cols, m = mask
                out = bank.rearrange("p (j k) -> p j k", j=4)[:, :, cols]
                mm(out, net.identb[:, :], m.unsqueeze(1).to_broadcast([P, 4, m.shape[1]]), start=True, stop=False,
                   skip_group_check=True)
            for jj in range(4):
                for r in range(2):
                    rows = slice(64 * r, 64 * r + 64)
                    ins = mm(net.scores[:, slot, r, jj * P:(jj + 1) * P], left[rows, 4 * u + jj, :],
                             right[rows, 4 * u + jj, :], start=False, stop=(jj == 3), skip_group_check=True)
            return ins

        def turn_normed(n):
            pe.wait_ge(self.xn.sem, self.xn.at(n, 1))
            pe.wait_ge(self.qkT.sem, self.qkT.at(n, 0))
            for tt in range(TPB):
                ins = nc.tensor.transpose(net.bank[4][:, tt * P:(tt + 1) * P], net.xn[:, tt, :], net.ident[:, :])
            ins.then_inc(self.xnT_psum.sem, 1)

        def project(n, tt):
            pe.wait_ge(self.xnT.sem, self.xnT.at(n, 1))
            pe.wait_ge(self.proj_read.sem, self.proj_read.at(n, tt))
            ins = mm(net.bank[4][:, 0:3 * D], net.xnTb[:, 1 + tt * P:1 + (tt + 1) * P], w["qkv"],
                     start=True, stop=True)
            if self.rel:
                ins = mm(net.bank[5][:, 0:2 * D], net.xnTb[:, tt * P:(tt + 1) * P], w["qkv"][:, D:3 * D],
                         start=True, stop=True)
            ins.then_inc(self.proj.sem, 1)

        def turn_stack(src, bank):
            for j in range(H // 2):
                ins = nc.tensor.transpose(bank[:, j * P:(j + 1) * P],
                                          src[:, 2 * j:2 * j + 2, :].rearrange("p h s -> p (h s)"), net.identb[:, :])
            return ins

        def stacks(n, b, groups):
            for g in groups:
                if g == 0:
                    pe.wait_ge(self.stacks.sem, self.stacks.at(n, 1))
                    pe.wait_ge(self.proj_read.sem, self.proj_read.at(n, 2))
                if g >= 2:
                    pe.wait_ge(self.qkT.sem, self.qkT.at(n, g - 1))
                src = (net.qs[:, b, 0], net.ks[:, 0], net.qs[:, b, 1], net.ks[:, 1])[g]
                turn_stack(src, net.bankb[4 + g % 2]).then_inc(self.stackT.sem, 1)

        def query_scores(n, b, a):
            qt, kt, u = self.units[a]
            if a == 0:
                pe.wait_ge(self.qkT.sem, self.qkT.at(n, 4))
                if not (isinstance(n, int) and n == 0):
                    pe.wait_ge(self.added.sem, self.added.at(n - 1, 0))
            pe.wait_ge(self.amax.sem, self.amax.at(n, a))
            score(0, net.qT[:, qt], net.kT[:, b, kt], u, w["mask"][kt == qt]).then_inc(self.a_scored.sem, 1)

        def key_scores(n, b, i):
            qt, kt, u = self.units[i]
            if i == 0:
                pe.wait_ge(self.qTb.sem, self.qTb.at(n, 2))
            pe.wait_ge(self.exps.sem, self.exps.at(n, i))
            score(1, net.kT[:, b, kt], net.qTm[:, qt], u, w["maskT"][kt == qt]).then_inc(self.b_scored.sem, 1)

        def shifted_queries(n, b):
            pe.wait_ge(self.mparts.sem, self.mparts.at(n, 1))
            pe.wait_ge(self.attended.sem, self.attended.at(n, 0))
            for tt in range(TPB):
                turn_stack(net.qs[:, b, tt], net.bankb[6 + tt]).then_inc(self.stackTm.sem, 1)

        def values(n, b, i):
            qt, kt, u = self.units[i]
            if i == 0:
                pe.wait_ge(self.vready.sem, self.vready.at(n, 1))
            pe.wait_ge(self.exps.sem, self.exps.at(n, i + 1))
            first = i == 0 or self.units[i - 1][0] != qt
            for jj in range(4):
                for r in range(2):
                    h = 2 * (4 * u + jj) + r
                    rows, cols = slice(32 * (h % 4), 32 * (h % 4) + VS), slice(h // 4 * P, (h // 4 + 1) * P)
                    ins = mm(net.bank[6 + qt][rows, cols], net.vaug[:, kt, h, :],
                             net.pT[:, i % 2, r, jj * P:(jj + 1) * P], start=(first and jj < 2),
                             stop=(kt == qt and u == 1 and jj >= 2), skip_group_check=True)
            ins.then_inc(self.pv.sem, 1)

        def by_token(n, qt):
            pe.wait_ge(self.pvT.sem, self.pvT.at(n, qt + 1))
            for c in range(H // 4):
                ins = nc.tensor.transpose(net.bank[6 + qt][:, c * P:(c + 1) * P], net.pvT[:, qt, c * P:(c + 1) * P],
                                          net.ident[:, :])
            ins.then_inc(self.pv_tokens.sem, 1)

        def turn_attended(n):
            pe.wait_ge(self.attended.sem, self.attended.at(n, 2))
            for tt in range(TPB):
                ins = nc.tensor.transpose(net.bank[0][:, tt * P:(tt + 1) * P], net.att[:, tt, :], net.ident[:, :])
            ins.then_inc(self.oT_psum.sem, 1)

        def output(n):
            pe.wait_ge(self.oT.sem, self.oT.at(n, 1))
            for tt in range(TPB):
                y = net.bank[1][:, tt * D:(tt + 1) * D]
                mm(y, net.oT[:, tt * P:(tt + 1) * P], w["out"], start=True, stop=False)
                ins = mm(y, net.ones[:, :], w["bias"], start=False, stop=True)
            ins.then_inc(self.y.sem, 1)

        def first():
            turn_normed(0)
            project(0, 0)
            project(0, 1)
            stacks(0, 0, range(4))
            turn_normed(1)
            for a in range(nu):
                query_scores(0, 0, a)
                if a < TPB:
                    project(1, a)
            stacks(1, 1, range(4))
            shifted_queries(0, 0)

        def step(n, b, with_max, with_front):
            if with_max:
                query_scores(n + 1, 1 - b, 0)
            if with_front:
                turn_normed(n + 2)
            key_scores(n, b, 0)
            if with_front:
                project(n + 2, 0)
            if with_max:
                query_scores(n + 1, 1 - b, 1)
            if with_front:
                project(n + 2, 1)
            for i in range(nu):
                if i + 1 < nu:
                    key_scores(n, b, i + 1)
                values(n, b, i)
                if with_max and i + 2 < nu:
                    query_scores(n + 1, 1 - b, i + 2)
                if i == self.units_first:
                    by_token(n, 0)
            if with_front:
                stacks(n + 2, b, (0, 1))
            by_token(n, 1)
            if with_front:
                stacks(n + 2, b, (2, 3))
            turn_attended(n)
            if with_max:
                shifted_queries(n + 1, 1 - b)
            output(n)

        self.turns(pe, first, step)


def attention_buffers(net):
    sb = net.sb
    net.xnTb = sb("normed_T_batch", [P, 1 + S])
    block, lower = net.sb_twice("attention_front", [P, 9 * S])
    v = net.carve(block, dict(q_k=(P, TPB * 2 * D, FP32), bf16_parts=(P, 3 * TPB * 2 * D, BF16),
                              split_rest=(P, TPB * 2 * D, FP32), special_products=(P, TPB * 2 * D, FP32)))
    net.qk = v["q_k"].rearrange("p (t c) -> p t c", t=TPB)
    net.part = v["bf16_parts"].rearrange("p (i t c) -> p i t c", i=3, t=TPB)
    net.rest = v["split_rest"].rearrange("p (t c) -> p t c", t=TPB)
    net.prod = v["special_products"].rearrange("p (t a d) -> p t a d", t=TPB, a=2)
    net.xnT_lower = lower[:, 0:T * P]
    net.vaug = sb("v_and_one", [P, TPB, H, VS])
    net.pvT = net.hid[:, 1].rearrange("p a b -> p (a b)").rearrange("p (a b) -> p a b", a=2)
    net.v = sb("v_tokens", [P, 2, TPB, D])
    net.prod2 = sb("special_values", [P, TPB, 2, D])
    net.spsum = sb("special_sum", [P, TPB, H])
    net.kv2, upper = net.sb_twice("kv_self_and_previous", [P, 2, TPB, 2, 2 * D])
    net.xnT_upper = upper[:, :, :, :, :].rearrange("p a b c d -> p (a b c d)")
    net.sp = sb("special_scores", [P, 2, TPB, 2, H])
    net.mx = sb("score_max", [P, 2, TPB, H])
    net.mneg = sb("minus_max", [P, TPB, H])
    net.mrest = sb("minus_max_rest", [P, TPB, H])
    net.qs = sb("q_stack", [P, 2, TPB, H, ST], BF16)
    net.ks = sb("k_stack", [P, TPB, H, ST], BF16)
    net.qT = net.hid[:, 0].rearrange("p a b -> p (a b)").bitcast(BF16).rearrange("p (t u k) -> p t u k", t=TPB, k=P)
    net.qTm = sb("q_stack_max_T", [P, TPB, H // 2, P], BF16)
    net.kT = sb("k_stack_T", [P, 2, TPB, H // 2, P], BF16)
    net.pT = net.xnT[:, :].rearrange("p (a b k) -> p a b k", a=2, b=2)
    net.den = sb("softmax_sum", [P, TPB, H])
    net.att = sb("attended_tokens", [P, TPB, D])
    net.oT = sb("attended_T", [P, S])
    net.ones = sb("ones_row", [1, P])
    net.add_far = sb("add_far", [P, 3 * D])
    net.add_self = sb("add_self", [P, 2 * D])
    net.add_prev = sb("add_prev", [P, 2 * D])
    net.first_row = sb("first_row_mask", [P, 1])
    net.short_row = sb("short_patch_rows", [P, 1])
    net.causal = sb("causal_masks", [P, 4, P], BF16)
    net.patch = sb("patch_mask", [P, P], BF16)
    net.member = sb("patch_members", [7, P])
    net.bias = sb("biases_everywhere", [P, 3 * D])
    net.table = sb("rel_tables_everywhere", [P, 2, 3, HD])
    net.patchsum = net.sem("patch_members_multiplied")
    net.made = net.sem("attention_constants_steps")
    net.att_const = net.sem("attention_constants_ready")
    net.biases = net.sem("biases_loaded")


def attention_constants(net, block_gpsimd):
    g, pool = net.nc.gpsimd, block_gpsimd
    chain = Chain(pool, net.made)
    for t, value in ((net.xnTb[:, 0:1], 0.0), (net.vaug[:, :, :, :], 0.0),
                     (net.qs[:, :, :, :, :].rearrange("p b t h s -> p (b t h s)"), 0.0),
                     (net.ks[:, :, :, :], 0.0), (net.ones[:, :], 1.0), (net.first_row[:, :], 0.0),
                     (net.short_row[:, :], 0.0), (net.causal[:, :, :], 0.0), (net.member[:, :], 1.0)):
        ins = g.memset(t, value)
    chain.then_wait(ins)
    g.memset(net.ks[:, :, :, 48:51], 1.0)
    g.memset(net.vaug[:, :, :, HD], 1.0)
    for i, (base, sign) in enumerate(((S // 2 - 2, 1), (-2, 1), (S // 2 - 2, -1), (-2, -1))):
        g.affine_select(out=net.causal[:, i, :], in_=net.causal[:, i, :], compare_op=ALU.is_ge, fill=NEG,
                        base=base, pattern=[[-sign, P]], channel_multiplier=sign)
    g.affine_select(out=net.first_row[:, :], in_=net.first_row[:, :], compare_op=ALU.is_ge, fill=NEG, base=-1,
                    pattern=[[0, 1]], channel_multiplier=1)
    g.affine_select(out=net.short_row[:, :], in_=net.short_row[:, :], compare_op=ALU.is_ge, fill=NEG, base=-120,
                    pattern=[[0, 1]], channel_multiplier=1)
    whole = net.member[:, 0:120].rearrange("p (b i r) -> p b i r", b=3, r=2)
    g.affine_select(out=whole, in_=whole, compare_op=ALU.is_equal, fill=0.0, base=0,
                    pattern=[[-2, 3], [0, 20], [-1, 2]], channel_multiplier=1)
    chain.then_wait(g.affine_select(out=net.member[:, 120:128], in_=net.member[:, 120:128], compare_op=ALU.is_equal,
                                    fill=0.0, base=-6, pattern=[[0, 8]], channel_multiplier=1))
    pool.wait_ge(net.biases, 9 * 16)
    far = net.add_far
    chain.then_wait(g.tensor_scalar(far[:, 0:D], net.bias[:, 0:D], SCALE, None, ALU.mult))
    for kv in range(2):
        b = net.bias[:, (1 + kv) * D:(2 + kv) * D].rearrange("p (h d) -> p h d", d=HD)
        for row, dst in ((0, far[:, (1 + kv) * D:(2 + kv) * D]), (1, net.add_prev[:, kv * D:(kv + 1) * D]),
                         (2, net.add_self[:, kv * D:(kv + 1) * D])):
            ins = g.tensor_tensor(dst.rearrange("p (h d) -> p h d", d=HD), b,
                                  net.table[:, kv, row, :].unsqueeze(1).to_broadcast([P, H, HD]), ALU.add)
    for q in (net.wqkv0[:, 0:D], net.wqkv1[:, 0:D]):
        ins = g.tensor_scalar(q, q, SCALE, None, ALU.mult)
    chain.then_wait(ins)


def attention_mask(net, dve):
    dve.wait_ge(net.patchsum, 1)
    dve.wait_ge(net.made, 4)
    net.nc.vector.tensor_scalar(net.patch[:, :], net.bank[0][:, 0:P], -1.0, -NEG, ALU.add,
                                ALU.mult).then_inc(net.att_const, 1)


def attention_mask_members(net, pe):
    pe.wait_ge(net.made, 2)
    net.nc.tensor.matmul(net.bank[0][:, 0:P], net.member[:, :], net.member[:, :], start=True,
                         stop=True).then_inc(net.patchsum, 1)


def build(nc, x, l0_qkv, l0_out, l0_bout, l1_q, l1_k, l1_v, l1_bq, l1_bk, l1_bv, l1_out, l1_bout, rel_k, rel_v,
          l0_gate, l0_w1, l0_w2, l1_gate, l1_w1, l1_w3, l1_w2, l1_s1, l1_s3, l1_s2, out, stages=range(6)):
    with ExitStack() as ctx:
        net = Net(nc, ctx)
        l0_gate_sb = net.sb("l0_gate_w", [P, E])
        l0_w1_sb, w1_upper = net.sb_twice("l0_w1", [P, E, F])
        l0_w2_sb, w3_upper = net.sb_twice("l0_w2", [P, E, FT, D])
        l1_gate_sb = net.sb("l1_gate_w", [P, E])
        l1_w1_sb, w1_lower = net.sb_twice("l1_w1", [P, NE, F])
        l1_w3_sb, w3_lower = net.sb_twice("l1_w3", [P, NE, F])
        l1_w2_sb = net.sb("l1_w2", [P, NE, FT, D])
        l0_loaded = net.sem("l0_weights_loaded")
        l1_loaded = net.sem("l1_weights_loaded")
        net.gates_loaded = (net.sem("router_weights_loaded"), 2 * 16)
        stored = net.sem("stored")

        net.wqkv0 = net.sb("l0_wqkv", [P, 3 * D])
        net.wqkv1 = net.sb("l1_wqkv", [P, 3 * D])
        l0_wout = net.sb("l0_wout", [P, D])
        l1_wout = net.sb("l1_wout", [P, D])
        l0_bias = net.sb("l0_bout", [1, D])
        l1_bias = net.sb("l1_bout", [1, D])
        att_loaded = net.sem("attention_weights_loaded")
        attention_buffers(net)
        choice_buffers(net)
        l1_upper = ((w1_upper, w3_upper[:, :, :, :].rearrange("p e f d -> p e (f d)")), net.shared_upper)
        patched = dict(qkv=net.wqkv0[:, :], out=l0_wout[:, :], bias=l0_bias[:, :], loaded=(att_loaded, 4 * 16),
                       mask=(None, (slice(0, P), net.patch[:, :])), maskT=(None, (slice(0, P), net.patch[:, :])))
        causal = dict(qkv=net.wqkv1[:, :], out=l1_wout[:, :], bias=l1_bias[:, :], loaded=(att_loaded, 4 * 16),
                      mask=((slice(P - 1, P), net.causal[:, 0, P - 1:P]), (slice(0, P), net.causal[:, 1, :])),
                      maskT=((slice(0, 1), net.causal[:, 2, 0:1]), (slice(0, P), net.causal[:, 3, :])))
        made = []

        def l0_ffn(name):
            made.append(ExpertChoice(net, name, l0_gate_sb[:, :], l0_w1_sb, l0_w2_sb, (l0_loaded, 2 * 16)))

        def l1_ffn(name):
            made.append(TokenChoice(net, name, l1_gate_sb[:, :], (l1_w1_sb, l1_w3_sb, l1_w2_sb),
                                    (w1_lower, w3_lower), l1_upper, (l1_loaded, 6 * 16)))

        for stage in stages:
            if stage in (0, 2):
                l0_ffn(f"l0_ffn_{stage}")
            if stage in (1, 4):
                made.append(Attention(net, f"attn_{stage}", stage == 4, causal if stage == 4 else patched))
            if stage in (3, 5):
                l1_ffn(f"l1_ffn_{stage}")

        first_attention = next((stage for stage in made if isinstance(stage, Attention)), None)
        block = ctx.enter_context(nc.Block())

        @block.sync
        def _(sp):
            for g, loaded in enumerate(net.xload):
                at = slice(g * GROUP, (g + 1) * GROUP)
                sp.dma_start(net.x[:, at, :], x.rearrange("b (a p) d -> p (b a) d", p=P)[:, at, :]).then_inc(loaded, 16)
            second = lambda w: w.rearrange("e (f p) d -> p (e f) d", p=P).rearrange("p (e f) d -> p e f d", e=E)
            sp.dma_start(l0_gate_sb[:, :], l0_gate).then_inc(net.gates_loaded[0], 16)
            sp.dma_start(l1_gate_sb[:, :], l1_gate).then_inc(net.gates_loaded[0], 16)
            sp.dma_start(l0_w1_sb[:, :, :], l0_w1.rearrange("e d f -> d e f")).then_inc(l0_loaded, 16)
            sp.dma_start(l0_w2_sb[:, :, :, :], second(l0_w2)).then_inc(l0_loaded, 16)
            row = lambda b: b.rearrange("(a n) -> a n", a=1)
            sp.dma_start(net.wqkv0[:, :], l0_qkv).then_inc(net.biases, 16)
            for i, w in enumerate((l1_q, l1_k, l1_v)):
                sp.dma_start(net.wqkv1[:, i * D:(i + 1) * D], w).then_inc(net.biases, 16)
            for i, b in enumerate((l1_bq, l1_bk, l1_bv)):
                sp.dma_start(net.bias[:, i * D:(i + 1) * D], row(b).to_broadcast([P, D])).then_inc(net.biases, 16)
            for i, t in enumerate((rel_k, rel_v)):
                sp.dma_start(net.table[:, i, :, :].rearrange("p r d -> p (r d)"),
                             row(t.rearrange("r d -> (r d)")[0:3 * HD]).to_broadcast([P, 3 * HD])
                             ).then_inc(net.biases, 16)
            sp.dma_start(l0_wout[:, :], l0_out).then_inc(att_loaded, 16)
            sp.dma_start(l1_wout[:, :], l1_out).then_inc(att_loaded, 16)
            sp.dma_start(l0_bias[:, :], row(l0_bout)).then_inc(att_loaded, 16)
            sp.dma_start(l1_bias[:, :], row(l1_bout)).then_inc(att_loaded, 16)
            sp.dma_start(l1_w1_sb[:, 0:E, :], l1_w1.rearrange("e d f -> d e f")).then_inc(l1_loaded, 16)
            sp.dma_start(l1_w3_sb[:, 0:E, :], l1_w3.rearrange("e d f -> d e f")).then_inc(l1_loaded, 16)
            sp.dma_start(l1_w2_sb[:, 0:E, :, :], second(l1_w2)).then_inc(l1_loaded, 16)
            sp.dma_start(l1_w1_sb[:, E, :], l1_s1.rearrange("n d f -> d n f")).then_inc(l1_loaded, 16)
            sp.dma_start(l1_w3_sb[:, E, :], l1_s3.rearrange("n d f -> d n f")).then_inc(l1_loaded, 16)
            sp.dma_start(l1_w2_sb[:, E, :, :], l1_s2.rearrange("(f a) q d -> (a q) f d", a=2)).then_inc(l1_loaded, 16)
            sp.wait_ge(*net.ready)
            sp.dma_start(out.rearrange("b (a p) d -> p (b a) d", p=P), net.x[:, :, :]).then_inc(stored, 16)
            sp.wait_ge(stored, 16)

        @block.gpsimd
        def _(pool):
            nc.gpsimd.memset(net.ident[:, :], 1.0).then_inc(net.const, 1)
            nc.gpsimd.memset(net.minus_half[:, :], -0.5).then_inc(net.const, 1)
            pool.wait_ge(net.const, 2)
            nc.gpsimd.affine_select(out=net.ident[:, :], in_=net.ident[:, :], compare_op=ALU.is_equal, fill=0.0,
                                    base=0, pattern=[[-1, P]], channel_multiplier=1).then_inc(net.const, 1)
            pool.wait_ge(net.const, 3)
            nc.gpsimd.tensor_copy(net.identb[:, :], net.ident[:, :]).then_inc(net.const, 1)
            made[0].gpsimd(pool)
            choice_constants(net, pool)
            attention_constants(net, pool)
            for stage in made[1:]:
                stage.gpsimd(pool)

        @block.vector
        def _(dve):
            for stage in made:
                if stage is first_attention:
                    attention_mask(net, dve)
                stage.vector(dve)

        @block.scalar
        def _(act):
            for stage in made:
                stage.scalar(act)

        @block.tensor
        def _(pe):
            for stage in made:
                if stage is first_attention:
                    attention_mask_members(net, pe)
                    pe.wait_ge(net.att_const, 1)
                stage.tensor(pe)


_INS = ["L0_attn_x", "L0_attn_Wqkv", "L0_attn_Wout", "L0_attn_bout", "L1_attn_W_q", "L1_attn_W_k", "L1_attn_W_v",
        "L1_attn_b_q", "L1_attn_b_k", "L1_attn_b_v", "L1_attn_W_o", "L1_attn_b_o", "L1_attn_rel_k_table",
        "L1_attn_rel_v_table", "L0_ffn_gate_w", "L0_ffn_w1", "L0_ffn_w2", "L1_ffn_gate_W", "L1_ffn_w1_e", "L1_ffn_w3_e",
        "L1_ffn_w2_e", "L1_ffn_w1_s", "L1_ffn_w3_s", "L1_ffn_w2_s"]
_TURNED = {"L1_ffn_gate_W", "L0_attn_Wqkv", "L0_attn_Wout"}


def kernel(**inputs):
    import concourse.bacc as bacc
    from concourse.bass_utils import run_bass_kernel_spmd

    nc = bacc.Bacc("TRN2", target_bir_lowering=False, num_devices=1)
    arrays, args = {}, []
    for name in _INS:
        a = np.asarray(inputs[name])
        a = np.ascontiguousarray(a.T if name in _TURNED else a)
        arrays[f"in_{name}"] = a
        args.append(nc.dram_tensor(f"in_{name}", a.shape, mybir.dt.from_np(a.dtype), kind="ExternalInput").ap())
    out = nc.dram_tensor("out_x", (B, S, D), FP32, kind="ExternalOutput").ap()
    build(nc, *args, out)
    r = run_bass_kernel_spmd(nc, [arrays], core_ids=[0])
    return r.results[0]["out_x"]
```
